# Optimizing a Trainium2 kernel written in Bass

```python
import numpy as np
import jax
import jax.numpy as jnp

def _softmax(x, axis=-1):
    return jax.nn.softmax(x, axis=axis)

def _gelu(x):
    return jax.nn.gelu(x, approximate=True)

def _silu(x):
    return jax.nn.silu(x)

def _sigmoid(x):
    return jax.nn.sigmoid(x)

def _layernorm(x, axis=-1, eps=1e-05):
    m = jnp.mean(x, axis=axis, keepdims=True)
    v = jnp.var(x, axis=axis, keepdims=True)
    return (x - m) / jnp.sqrt(v + eps)

def _scatter_add(tgt, idx, src, axis=0):
    return tgt.at[idx].add(src)

def _segment_sum(src, seg, n):
    return jax.ops.segment_sum(src, seg, n)
kernel_name = 'mk_seq_preln_d2_jaxref_r8_26b24a'

def setup_inputs(seed: int=0):
    np.random.seed(seed)
    _w = jnp.asarray

    def _L0_attn_setup():
        import jax, jax.numpy as jnp
        import numpy as np
        DIM = 128
        HEADS = 16
        GROUPS = 4
        DIM_HEAD = 64
        INNER = HEADS * DIM_HEAD
        KV_DIM = 2 * DIM_HEAD * GROUPS
        B, N = (4, 256)
        EPS = 1e-06

        def _layernorm(x, scale, bias, eps=EPS):
            mu = jnp.mean(x, axis=-1, keepdims=True)
            var = jnp.mean(jnp.square(x - mu), axis=-1, keepdims=True)
            return (x - mu) * jax.lax.rsqrt(var + eps) * scale + bias
        key = jax.random.key(seed)
        ks = jax.random.split(key, 10)
        lecun = lambda k, shape: jax.random.normal(k, shape, jnp.float32) * (1.0 / np.sqrt(shape[0]))
        return {'x': jax.random.normal(ks[0], (B, N, DIM), jnp.float32), 'ln_scale': jnp.ones((DIM,), jnp.float32), 'ln_bias': jnp.zeros((DIM,), jnp.float32), 'Wq': lecun(ks[1], (DIM, INNER)), 'Wkv': lecun(ks[2], (DIM, KV_DIM)), 'qn_scale': jnp.ones((DIM_HEAD,), jnp.float32), 'qn_bias': jnp.zeros((DIM_HEAD,), jnp.float32), 'kn_scale': jnp.ones((DIM_HEAD,), jnp.float32), 'kn_bias': jnp.zeros((DIM_HEAD,), jnp.float32), 'Wout': lecun(ks[3], (INNER, DIM))}
    _L0_attn_in = _L0_attn_setup()

    def _L0_ffn_setup():
        import jax, jax.numpy as jnp
        import numpy as np
        B, S, D, F, E, TOP_K = (4, 256, 128, 512, 8, 2)
        LN_EPS = 1e-05
        key = jax.random.key(seed)
        ks = jax.random.split(key, 4)
        sc = lambda fan_in: 1.0 / np.sqrt(fan_in)
        return {'x': jax.random.normal(ks[0], (B, S, D), jnp.float32), 'W1': jax.random.normal(ks[1], (E, D, F), jnp.float32) * sc(D), 'b1': jnp.zeros((E, F), jnp.float32), 'W2': jax.random.normal(ks[2], (E, F, D), jnp.float32) * sc(F), 'b2': jnp.zeros((E, D), jnp.float32), 'Wr': jax.random.normal(ks[3], (D, E), jnp.float32) * sc(D), 'br': jnp.zeros((E,), jnp.float32), 'gamma': jnp.ones((D,), jnp.float32), 'beta': jnp.zeros((D,), jnp.float32)}
    _L0_ffn_in = _L0_ffn_setup()

    def _L1_attn_setup():
        import jax, jax.numpy as jnp
        import numpy as np
        L, B, E = (256, 4, 128)
        S = 128
        EH = 2 * E
        CHUNK = 64
        MAXPOS = 64
        EPS = 1e-05

        def rope(x, axes):
            shape = x.shape
            spatial = [shape[i] for i in axes]
            total = int(np.prod(spatial))
            pos = jnp.arange(total, dtype=x.dtype).reshape(spatial)
            for _ in range(axes[-1] + 1, len(shape) - 1):
                pos = pos[..., None]
            half = shape[-1] // 2
            inv_freq = 10000.0 ** (-jnp.arange(half, dtype=x.dtype) / half)
            sinusoid = pos[..., None] * inv_freq
            sin, cos = (jnp.sin(sinusoid), jnp.cos(sinusoid))
            x1, x2 = jnp.split(x, 2, axis=-1)
            return jnp.concatenate([x1 * cos - x2 * sin, x2 * cos + x1 * sin], axis=-1)

        def rel_pos_bias(w, seq_len):
            t = jnp.pad(w[:2 * seq_len - 1], (0, seq_len))
            t = jnp.tile(t, seq_len)[:-seq_len].reshape(seq_len, 3 * seq_len - 2)
            r = (2 * seq_len - 1) // 2
            return t[:, r:-r]
        key = jax.random.key(seed)
        ks = jax.random.split(key, 12)

        def n(k, shape, std):
            return jax.random.normal(k, shape, dtype=jnp.float32) * std
        query = jax.random.normal(ks[0], (L, B, E), dtype=jnp.float32)
        return dict(query=query, key_in=query, value_in=query, ln_g=jnp.ones((E,), jnp.float32), ln_b=jnp.zeros((E,), jnp.float32), Wu=n(ks[1], (EH, E), 1.0 / np.sqrt(E)), bu=jnp.zeros((EH,), jnp.float32), Wv=n(ks[2], (EH, E), 1.0 / np.sqrt(E)), bv=jnp.zeros((EH,), jnp.float32), Wb=n(ks[3], (S, E), 1.0 / np.sqrt(E)), bb=jnp.zeros((S,), jnp.float32), qqw=n(ks[4], (S,), 0.02), qqb=jnp.zeros((S,), jnp.float32), qkw=n(ks[5], (S,), 0.02), qkb=jnp.zeros((S,), jnp.float32), lqw=n(ks[6], (S,), 0.02), lqb=jnp.zeros((S,), jnp.float32), lkw=n(ks[7], (S,), 0.02), lkb=jnp.zeros((S,), jnp.float32), Wo=n(ks[8], (E, EH), 1.0 / np.sqrt(EH)), bo=jnp.zeros((E,), jnp.float32), w_rel=n(ks[9], (2 * MAXPOS - 1,), 0.02))
    _L1_attn_in = _L1_attn_setup()

    def _L1_ffn_setup():
        import jax, jax.numpy as jnp
        import numpy as np
        DIM = 128
        HIDDEN = 384
        SCALE = 1.0 / 127.0

        def _dequant(w_int, dtype):
            return w_int.astype(dtype) * jnp.asarray(SCALE, dtype)
        key = jax.random.key(seed)
        k_x, k_g, k_u, k_d = jax.random.split(key, 4)
        x = jax.random.normal(k_x, (4, 256, DIM), dtype=jnp.float32)
        w_gate = jax.random.randint(k_g, (HIDDEN, DIM), -127, 128, dtype=jnp.int32)
        w_up = jax.random.randint(k_u, (HIDDEN, DIM), -127, 128, dtype=jnp.int32)
        w_down = jax.random.randint(k_d, (DIM, HIDDEN), -127, 128, dtype=jnp.int32)
        return {'x': x, 'w_gate': w_gate, 'w_up': w_up, 'w_down': w_down}
    _L1_ffn_in = _L1_ffn_setup()
    _d = {'L0_attn_x': _L0_attn_in['x'], 'L0_attn_ln_scale': _L0_attn_in['ln_scale'], 'L0_attn_ln_bias': _L0_attn_in['ln_bias'], 'L0_attn_Wq': _L0_attn_in['Wq'], 'L0_attn_Wkv': _L0_attn_in['Wkv'], 'L0_attn_qn_scale': _L0_attn_in['qn_scale'], 'L0_attn_qn_bias': _L0_attn_in['qn_bias'], 'L0_attn_kn_scale': _L0_attn_in['kn_scale'], 'L0_attn_kn_bias': _L0_attn_in['kn_bias'], 'L0_attn_Wout': _L0_attn_in['Wout'], 'L0_ffn_W1': _L0_ffn_in['W1'], 'L0_ffn_b1': _L0_ffn_in['b1'], 'L0_ffn_W2': _L0_ffn_in['W2'], 'L0_ffn_b2': _L0_ffn_in['b2'], 'L0_ffn_Wr': _L0_ffn_in['Wr'], 'L0_ffn_br': _L0_ffn_in['br'], 'L0_ffn_gamma': _L0_ffn_in['gamma'], 'L0_ffn_beta': _L0_ffn_in['beta'], 'L1_attn_key_in': _L1_attn_in['key_in'], 'L1_attn_value_in': _L1_attn_in['value_in'], 'L1_attn_ln_g': _L1_attn_in['ln_g'], 'L1_attn_ln_b': _L1_attn_in['ln_b'], 'L1_attn_Wu': _L1_attn_in['Wu'], 'L1_attn_bu': _L1_attn_in['bu'], 'L1_attn_Wv': _L1_attn_in['Wv'], 'L1_attn_bv': _L1_attn_in['bv'], 'L1_attn_Wb': _L1_attn_in['Wb'], 'L1_attn_bb': _L1_attn_in['bb'], 'L1_attn_qqw': _L1_attn_in['qqw'], 'L1_attn_qqb': _L1_attn_in['qqb'], 'L1_attn_qkw': _L1_attn_in['qkw'], 'L1_attn_qkb': _L1_attn_in['qkb'], 'L1_attn_lqw': _L1_attn_in['lqw'], 'L1_attn_lqb': _L1_attn_in['lqb'], 'L1_attn_lkw': _L1_attn_in['lkw'], 'L1_attn_lkb': _L1_attn_in['lkb'], 'L1_attn_Wo': _L1_attn_in['Wo'], 'L1_attn_bo': _L1_attn_in['bo'], 'L1_attn_w_rel': _L1_attn_in['w_rel'], 'L1_ffn_w_gate': _L1_ffn_in['w_gate'], 'L1_ffn_w_up': _L1_ffn_in['w_up'], 'L1_ffn_w_down': _L1_ffn_in['w_down']}
    _x0 = _d['L0_attn_x']
    _d['L0_attn_x'] = jax.random.normal(jax.random.fold_in(jax.random.key(seed), 1), (2, 1024, 128), dtype=_x0.dtype)
    del _x0
    return _d

def reference(L0_attn_x, L0_attn_ln_scale, L0_attn_ln_bias, L0_attn_Wq, L0_attn_Wkv, L0_attn_qn_scale, L0_attn_qn_bias, L0_attn_kn_scale, L0_attn_kn_bias, L0_attn_Wout, L0_ffn_W1, L0_ffn_b1, L0_ffn_W2, L0_ffn_b2, L0_ffn_Wr, L0_ffn_br, L0_ffn_gamma, L0_ffn_beta, L1_attn_key_in, L1_attn_value_in, L1_attn_ln_g, L1_attn_ln_b, L1_attn_Wu, L1_attn_bu, L1_attn_Wv, L1_attn_bv, L1_attn_Wb, L1_attn_bb, L1_attn_qqw, L1_attn_qqb, L1_attn_qkw, L1_attn_qkb, L1_attn_lqw, L1_attn_lqb, L1_attn_lkw, L1_attn_lkb, L1_attn_Wo, L1_attn_bo, L1_attn_w_rel, L1_ffn_w_gate, L1_ffn_w_up, L1_ffn_w_down):

    def _L0_attn_ref(x, ln_scale, ln_bias, Wq, Wkv, qn_scale, qn_bias, kn_scale, kn_bias, Wout):
        import jax, jax.numpy as jnp
        import numpy as np
        DIM = 128
        HEADS = 16
        GROUPS = 4
        DIM_HEAD = 64
        INNER = HEADS * DIM_HEAD
        KV_DIM = 2 * DIM_HEAD * GROUPS
        B, N = (4, 256)
        EPS = 1e-06

        def _layernorm(x, scale, bias, eps=EPS):
            mu = jnp.mean(x, axis=-1, keepdims=True)
            var = jnp.mean(jnp.square(x - mu), axis=-1, keepdims=True)
            return (x - mu) * jax.lax.rsqrt(var + eps) * scale + bias
        b, n, _ = x.shape
        g, hg, d = (GROUPS, HEADS // GROUPS, DIM_HEAD)
        scale = d ** (-0.5)
        xn = _layernorm(x, ln_scale, ln_bias)
        q = (xn @ Wq).reshape(b, n, HEADS, d).transpose(0, 2, 1, 3)
        kv = xn @ Wkv
        k, v = jnp.split(kv, 2, axis=-1)
        k = k.reshape(b, n, g, d).transpose(0, 2, 1, 3)
        v = v.reshape(b, n, g, d).transpose(0, 2, 1, 3)
        q = _layernorm(q, qn_scale, qn_bias)
        k = _layernorm(k, kn_scale, kn_bias)
        qg = q.reshape(b, g, hg, n, d)
        dots = jnp.einsum('bghqd,bgkd->bghqk', qg, k) * scale
        attn = jax.nn.softmax(dots, axis=-1)
        out = jnp.einsum('bghqk,bgkd->bghqd', attn, v)
        out = out.transpose(0, 3, 1, 2, 4).reshape(b, n, g * hg * d)
        return out @ Wout

    def _L0_ffn_ref(x, W1, b1, W2, b2, Wr, br, gamma, beta):
        import jax, jax.numpy as jnp
        import numpy as np
        B, S, D, F, E, TOP_K = (4, 256, 128, 512, 8, 2)
        LN_EPS = 1e-05
        b, s, d = x.shape
        e = Wr.shape[1]
        rw = jax.nn.softmax(x.mean(axis=1) @ Wr + br, axis=-1)
        x_flat = x.reshape(-1, d)
        rw_tok = jnp.repeat(rw, s, axis=0)
        tk_w, tk_i = jax.lax.top_k(rw_tok, TOP_K)
        tk_w = jax.nn.softmax(tk_w, axis=-1)
        h = jax.nn.gelu(jnp.einsum('nd,edf->enf', x_flat, W1) + b1[:, None, :], approximate=False)
        expert_out = jnp.einsum('enf,efd->end', h, W2) + b2[:, None, :]
        onehot = jax.nn.one_hot(tk_i, e, dtype=x.dtype)
        cw = jnp.einsum('nk,nke->ne', tk_w, onehot)
        out = jnp.einsum('ne,end->nd', cw, expert_out).reshape(b, s, d)
        y = out + x
        mu = y.mean(axis=-1, keepdims=True)
        var = y.var(axis=-1, keepdims=True)
        return (y - mu) / jnp.sqrt(var + LN_EPS) * gamma + beta

    def _L1_attn_ref(query, key_in, value_in, ln_g, ln_b, Wu, bu, Wv, bv, Wb, bb, qqw, qqb, qkw, qkb, lqw, lqb, lkw, lkb, Wo, bo, w_rel):
        import jax, jax.numpy as jnp
        import numpy as np
        L, B, E = (256, 4, 128)
        S = 128
        EH = 2 * E
        CHUNK = 64
        MAXPOS = 64
        EPS = 1e-05

        def rope(x, axes):
            shape = x.shape
            spatial = [shape[i] for i in axes]
            total = int(np.prod(spatial))
            pos = jnp.arange(total, dtype=x.dtype).reshape(spatial)
            for _ in range(axes[-1] + 1, len(shape) - 1):
                pos = pos[..., None]
            half = shape[-1] // 2
            inv_freq = 10000.0 ** (-jnp.arange(half, dtype=x.dtype) / half)
            sinusoid = pos[..., None] * inv_freq
            sin, cos = (jnp.sin(sinusoid), jnp.cos(sinusoid))
            x1, x2 = jnp.split(x, 2, axis=-1)
            return jnp.concatenate([x1 * cos - x2 * sin, x2 * cos + x1 * sin], axis=-1)

        def rel_pos_bias(w, seq_len):
            t = jnp.pad(w[:2 * seq_len - 1], (0, seq_len))
            t = jnp.tile(t, seq_len)[:-seq_len].reshape(seq_len, 3 * seq_len - 2)
            r = (2 * seq_len - 1) // 2
            return t[:, r:-r]
        tgt_len = query.shape[0]
        len_pad = (CHUNK - tgt_len % CHUNK) % CHUNK
        q = jnp.pad(query, ((0, len_pad), (0, 0), (0, 0)))
        Lp = q.shape[0]
        nc = Lp // CHUNK
        q = q.transpose(1, 0, 2)
        shortcut = q
        mu = q.mean(-1, keepdims=True)
        var = q.var(-1, keepdims=True)
        xn = (q - mu) / jnp.sqrt(var + EPS) * ln_g + ln_b
        u = jax.nn.silu(xn @ Wu.T + bu)
        v = jax.nn.silu(xn @ Wv.T + bv)
        base = jax.nn.silu(xn @ Wb.T + bb)
        bsz = q.shape[0]

        def mk(wt, bi):
            t = (base * wt + bi).reshape(bsz, nc, CHUNK, S)
            return rope(t, [1, 2])
        quad_q, quad_k = (mk(qqw, qqb), mk(qkw, qkb))
        lin_q, lin_k = (mk(lqw, lqb), mk(lkw, lkb))
        vch = v.reshape(bsz, nc, CHUNK, EH)
        quad_qk = jnp.einsum('bgne,bgme->bgnm', quad_q, quad_k)
        bias = rel_pos_bias(w_rel, MAXPOS)[:CHUNK, :CHUNK]
        kernel = jnp.square(jax.nn.relu(quad_qk / CHUNK + bias))
        causal = jnp.tril(jnp.ones((CHUNK, CHUNK), dtype=bool))
        kernel = jnp.where(causal, kernel, 0.0)
        quadratic = jnp.einsum('bgnm,bgme->bgne', kernel, vch)
        lin_kv = jnp.einsum('bgnk,bgne->bgke', lin_k, vch) / CHUNK
        cmask = jnp.tril(jnp.ones((nc, nc), dtype=lin_kv.dtype), k=-1)
        lin_kv = jnp.einsum('bhke,gh->bgke', lin_kv, cmask)
        linear = jnp.einsum('bgnk,bgke->bgne', lin_q, lin_kv)
        x = (u.reshape(bsz, nc, CHUNK, EH) * (linear + quadratic)).reshape(bsz, Lp, EH)
        x = x @ Wo.T + bo
        out = (x + shortcut).transpose(1, 0, 2)[:tgt_len]
        return out

    def _L1_ffn_ref(x, w_gate, w_up, w_down):
        import jax, jax.numpy as jnp
        import numpy as np
        DIM = 128
        HIDDEN = 384
        SCALE = 1.0 / 127.0

        def _dequant(w_int, dtype):
            return w_int.astype(dtype) * jnp.asarray(SCALE, dtype)
        wg = _dequant(w_gate, x.dtype)
        wu = _dequant(w_up, x.dtype)
        wd = _dequant(w_down, x.dtype)
        gate = jnp.einsum('bsd,hd->bsh', x, wg)
        up = jnp.einsum('bsd,hd->bsh', x, wu)
        h = jax.nn.silu(gate) * up
        return jnp.einsum('bsh,dh->bsd', h, wd)
    x = L0_attn_x
    x = x + _L0_attn_ref(_layernorm(x, axis=-1), L0_attn_ln_scale, L0_attn_ln_bias, L0_attn_Wq, L0_attn_Wkv, L0_attn_qn_scale, L0_attn_qn_bias, L0_attn_kn_scale, L0_attn_kn_bias, L0_attn_Wout)
    x = x + _L0_ffn_ref(_layernorm(x, axis=-1), L0_ffn_W1, L0_ffn_b1, L0_ffn_W2, L0_ffn_b2, L0_ffn_Wr, L0_ffn_br, L0_ffn_gamma, L0_ffn_beta)
    x = x + _L1_attn_ref(_layernorm(x, axis=-1), L1_attn_key_in, L1_attn_value_in, L1_attn_ln_g, L1_attn_ln_b, L1_attn_Wu, L1_attn_bu, L1_attn_Wv, L1_attn_bv, L1_attn_Wb, L1_attn_bb, L1_attn_qqw, L1_attn_qqb, L1_attn_qkw, L1_attn_qkb, L1_attn_lqw, L1_attn_lqb, L1_attn_lkw, L1_attn_lkb, L1_attn_Wo, L1_attn_bo, L1_attn_w_rel)
    x = x + _L1_ffn_ref(_layernorm(x, axis=-1), L1_ffn_w_gate, L1_ffn_w_up, L1_ffn_w_down)
    return x

_drawn_inputs = setup_inputs


def setup_inputs(seed=0):
    import zlib

    import numpy as np

    out = dict(_drawn_inputs(seed))
    spreads = {'L0_attn_ln_scale': (1.0, 0.2),
     'L0_attn_ln_bias': (0.0, 0.1),
     'L0_attn_qn_scale': (1.0, 0.2),
     'L0_attn_qn_bias': (0.0, 0.419),
     'L0_attn_kn_scale': (1.0, 0.2),
     'L0_attn_kn_bias': (0.0, 2.0),
     'L0_ffn_b1': (0.0, 0.1),
     'L0_ffn_b2': (0.0, 0.1),
     'L0_ffn_br': (0.0, 0.523),
     'L0_ffn_gamma': (1.0, 0.2),
     'L0_ffn_beta': (0.0, 0.1),
     'L1_attn_ln_g': (1.0, 0.6),
     'L1_attn_ln_b': (0.0, 0.8),
     'L1_attn_bu': (0.0, 0.8),
     'L1_attn_bv': (0.0, 2.0),
     'L1_attn_bb': (0.0, 0.8),
     'L1_attn_qqb': (0.0, 0.8),
     'L1_attn_qkb': (0.0, 0.8),
     'L1_attn_lqb': (0.0, 0.1),
     'L1_attn_lkb': (0.0, 0.1),
     'L1_attn_bo': (0.0, 0.1)}
    factors = {'L0_ffn_Wr': 8.0,
     'L1_attn_Wu': 8.0,
     'L1_attn_Wv': 8.0,
     'L1_attn_Wb': 8.0,
     'L1_attn_qqw': 8.0,
     'L1_attn_qkw': 8.0,
     'L1_attn_Wo': 8.0,
     'L1_attn_w_rel': 8.0}
    for name, (base, spread) in spreads.items():
        noise = np.random.default_rng([zlib.crc32(name.encode()), seed]).standard_normal(out[name].shape)
        drawn = base * np.exp(spread * noise) if base else spread * noise
        out[name] = jnp.asarray(drawn.astype(out[name].dtype))
    for name, factor in factors.items():
        out[name] = (out[name] * factor).astype(out[name].dtype)
    return out
```

```python
from contextlib import ExitStack

import numpy as np

import concourse.bass as bass
from concourse import mybir

F32 = mybir.dt.float32
F32R = mybir.dt.float32r
I32 = mybir.dt.int32
U32 = mybir.dt.uint32
ALU = mybir.AluOpType
ACT = mybir.ActivationFunctionType
AX_X = mybir.AxisListType.X

P = 128
BATCH, SEQ, DIM = 2, 1024, 128
TILES = SEQ // P
HEADS, GROUPS, DH = 16, 4, 64
INNER, KV = HEADS * DH, GROUPS * DH
NORMED = HEADS + GROUPS
QKV = INNER + 2 * KV
EXPERTS, HID, TOP = 8, 512, 2
FT = HID // P
EH, S = 256, 128
UVB = 2 * EH + S
CHUNK = 64
HID1 = 384
HT = HID1 // P
SCALE1 = 1.0 / 127.0
LN_EPS, ATT_EPS = 1e-5, 1e-6

UNITS = HEADS * TILES
BLOCKS = UNITS // 4
BODY = 8
QB = 2 * P
FIRST = 1
T_LAG = 3
W_UVB, W_O, W_GATE, W_UP, W_DOWN, W_TILES = 0, 5, 7, 10, 13, 16


def column(v):
    return v.rearrange("(p a) -> p a", a=1)


def row(v):
    return v.rearrange("(a n) -> a n", a=1)


def everywhere(v, parts=P):
    return v.partition_broadcast(parts)


def over_last(t, n):
    return t.unsqueeze(2).broadcast_to([t.shape[0], t.shape[1], n])


def over_mid(t, m):
    return t.unsqueeze(1).broadcast_to([t.shape[0], m, t.shape[1]])


def build(nc, a, rope, out):
    with ExitStack() as ctx:
        def sb(name, shape, dt=F32, where=ctx):
            return where.enter_context(nc.sbuf_tensor(name, shape, dt))

        def sem(name):
            return ctx.enter_context(nc.semaphore(name))

        psum = ctx.enter_context(nc.psum_tensor("psum", [P, 4096], F32))
        x = sb("x", [P, BATCH, TILES, DIM])
        xv = [a["L0_attn_x"][b].rearrange("(p j) d -> p j d", j=TILES) for b in range(BATCH)]
        ident = sb("ident", [P, P])
        wt = sb("wt", [P, W_TILES * P])
        gamma = sb("gamma", [P, DIM])
        beta = sb("beta", [P, DIM])
        ones = sb("ones", [1, P])
        wr = sb("wr", [P, EXPERTS])
        br = sb("br", [1, EXPERTS])
        lng = sb("lng", [P, 1])
        lnb = sb("lnb", [P, 1])
        uvb_bias = sb("uvb_bias", [P, UVB])
        qk_w = sb("qk_w", [P, 2, S])
        qk_b = sb("qk_b", [P, 2, S])
        ropes = sb("ropes", [P, 2, S])
        bo = sb("bo", [P, DIM])
        rel = sb("rel", [P, 3])

        first_layer(nc, a, xv, x, ident, wt, psum, sb, sem, ctx,
                    dict(gamma=gamma, beta=beta, ones=ones, wr=wr, br=br, lng=lng, lnb=lnb, uvb_bias=uvb_bias,
                         qk_w=qk_w, qk_b=qk_b, ropes=ropes, bo=bo, rel=rel), rope)
        rest(nc, a, x, ident, wt, psum, sb, sem, out, gamma, beta, ones, wr, br, lng, lnb, uvb_bias,
             qk_w, qk_b, ropes, bo, rel)


def first_layer(nc, a, xv, x, ident, wt, psum, sb, sem, outer, c, rope):
    with ExitStack() as own:
        def mine(name, shape, dt=F32):
            return sb(name, shape, dt, own)

        wqkv = mine("wqkv", [P, QKV])
        wmean = mine("wmean", [P, NORMED])
        wout = mine("wout", [P, HEADS // 2, DIM])
        aln_s = mine("aln_s", [P, 1])
        aln_b = mine("aln_b", [P, 1])
        qk_s = mine("qk_s", [P, 2])
        qk_o = mine("qk_o", [P, 2])
        st = mine("st", [P, 4, TILES])
        hst = mine("hst", [P, 4, NORMED])
        qx = mine("qx", [P, HEADS // 2, 4, 2, QB], F32R)
        kh = mine("kh", [P, GROUPS, SEQ], F32R)
        kl = mine("kl", [P, GROUPS, SEQ], F32R)
        vb = mine("vb", [P, GROUPS, TILES, DH])
        qs = [mine(f"qs{i}", [P, 4, P], F32R) for i in range(2)]
        vs = [mine(f"vs{i}", [P, TILES, DH]) for i in range(2)]
        probs_all = mine("probs_all", [P, 4 * SEQ])
        pt_all = mine("pt_all", [P, 2 * 2 * TILES * QB])
        probs = [probs_all[:, i * SEQ:(i + 1) * SEQ] for i in range(4)]
        pt = [pt_all[:, i * 2 * TILES * QB:(i + 1) * 2 * TILES * QB].rearrange("p (h k q) -> p h k q", h=2, k=TILES)
              for i in range(2)]
        raw = probs_all[:, 0:W_TILES * P]
        rawi = probs_all[:, W_TILES * P:(2 * W_TILES - W_GATE) * P].bitcast(I32)
        at = 0
        spaces = []
        for size in (NORMED * DH, SEQ, NORMED * P, NORMED * P):
            spaces.append(pt_all[:, at:at + size])
            at += size
        cen = spaces[0][:, 0:SEQ].rearrange("p (j d) -> p j d", d=DIM)
        hsq = spaces[0]
        xnt = spaces[1]
        qn = spaces[2].rearrange("p (h t d) -> p h t d", t=2, d=DH)
        t1 = spaces[3].rearrange("p (h q) -> p h q", q=P)
        sq = spaces[3]
        ot = [mine(f"ot{i}", [P, QB]) for i in range(2)]
        nmx = mine("nmx", [P, 4])
        rsum = mine("rsum", [P, 4])
        rinv = mine("rinv", [P, 4])

        x_in = [sem(f"x_in{b}") for b in range(BATCH)]
        w_in = sem("w_in")
        c_in = sem("c_in")
        r_in = sem("r_in")
        ident_made = sem("ident_made")
        w_float = sem("w_float")
        w_turned = sem("w_turned")
        w_kept = sem("w_kept")
        dve_step = sem("dve_step")
        act_step = sem("act_step")
        pool_step = sem("pool_step")
        cen_made = sem("cen_made")
        sq_made = sem("sq_made")
        var_made = sem("var_made")
        root_made = sem("root_made")
        xn_made = sem("xn_made")
        xn_turned = sem("xn_turned")
        xnt_made = sem("xnt_made")
        w_centred = sem("w_centred")
        qkv_made = sem("qkv_made")
        hsq_made = sem("hsq_made")
        hvar_made = sem("hvar_made")
        hroot_made = sem("hroot_made")
        hsum = sem("hsum")
        qn_made = sem("qn_made")
        v_made = sem("v_made")
        twin_made = sem("twin_made")
        qn_turned = sem("qn_turned")
        t1_made = sem("t1_made")
        high_made = sem("high_made")
        low_made = sem("low_made")
        qs_in = [sem(f"qs_in{i}") for i in range(2)]
        vs_in = [sem(f"vs_in{i}") for i in range(2)]
        scored = sem("scored")
        max_made = sem("max_made")
        exp_made = sem("exp_made")
        rinv_made = sem("rinv_made")
        normed = sem("normed")
        turned_a = sem("turned_a")
        turned_b = sem("turned_b")
        kept_a = sem("kept_a")
        kept_b = sem("kept_b")
        pv_made = sem("pv_made")
        ot_made = sem("ot_made")
        y_made = sem("y_made")
        x_added = sem("x_added")

        small = [(c["gamma"][:, :], everywhere(a["L0_ffn_gamma"])), (c["beta"][:, :], everywhere(a["L0_ffn_beta"])),
                 (c["wr"][:, :], a["L0_ffn_Wr"]), (c["br"][:, :], row(a["L0_ffn_br"])),
                 (c["lng"][:, :], column(a["L1_attn_ln_g"])), (c["lnb"][:, :], column(a["L1_attn_ln_b"])),
                 (c["uvb_bias"][:, 0:EH], everywhere(a["L1_attn_bu"])),
                 (c["uvb_bias"][:, EH:2 * EH], everywhere(a["L1_attn_bv"])),
                 (c["uvb_bias"][:, 2 * EH:UVB], everywhere(a["L1_attn_bb"])),
                 (c["qk_w"][:, 0, :], everywhere(a["L1_attn_qqw"])), (c["qk_w"][:, 1, :], everywhere(a["L1_attn_qkw"])),
                 (c["qk_b"][:, 0, :], everywhere(a["L1_attn_qqb"])), (c["qk_b"][:, 1, :], everywhere(a["L1_attn_qkb"])),
                 (c["ropes"][:, 0, :], everywhere(rope[0])), (c["ropes"][:, 1, :], everywhere(rope[1])),
                 (c["bo"][:, :], everywhere(a["L1_attn_bo"])),
                 (c["rel"][:, 0:1], everywhere(a["L1_attn_w_rel"][CHUNK - 1:CHUNK])),
                 (c["rel"][:, 1:2], everywhere(a["L1_attn_w_rel"][CHUNK - 2:CHUNK - 1])),
                 (c["rel"][:, 2:3], everywhere(a["L1_attn_w_rel"][CHUNK - 1:CHUNK]))]
        mine_small = [(aln_s[:, :], column(a["L0_attn_ln_scale"])), (aln_b[:, :], column(a["L0_attn_ln_bias"])),
                      (wout[:, :, :], a["L0_attn_Wout"].rearrange("(h p) d -> p h d", p=P))]
        for half in range(2):
            rows = slice(half * DH, (half + 1) * DH)
            mine_small += [(qk_s[rows, 0:1], column(a["L0_attn_qn_scale"])), (qk_s[rows, 1:2], column(a["L0_attn_kn_scale"])),
                           (qk_o[rows, 0:1], column(a["L0_attn_qn_bias"])), (qk_o[rows, 1:2], column(a["L0_attn_kn_bias"]))]
        N_RAW, N_SMALL = 7, len(mine_small) + len(small)

        scores = [psum[:, SEQ * i:SEQ * (i + 1)] for i in range(2)]
        turned = psum[:, 2 * SEQ:3 * SEQ]
        outp = [psum[:, 3 * SEQ + 512 * i:3 * SEQ + 512 * (i + 1)] for i in range(2)]
        qkv = psum[:, 0:QKV]
        qnt = psum[:, QKV:QKV + NORMED * P]

        block = own.enter_context(nc.Block())

        @block.sync
        def _(sp):
            sp.dma_start(x[:, 0], xv[0]).then_inc(x_in[0], 16)
            sp.dma_start(wqkv[:, 0:INNER], a["L0_attn_Wq"]).then_inc(w_in, 16)
            sp.dma_start(wqkv[:, INNER:QKV], a["L0_attn_Wkv"]).then_inc(w_in, 16)
            sp.dma_start(x[:, 1], xv[1]).then_inc(x_in[1], 16)
            for dst, src in mine_small + small:
                sp.dma_start(dst, src).then_inc(c_in, 16)
            with sp.Fori(0, BATCH) as b:
                def load_q(n, par):
                    sp.dma_start(qs[par][:, :, :].rearrange("p u q -> p (u q)").bitcast(F32),
                                 qx[:, :, :, :, :].rearrange("p h b u q -> p (h b u q)")[:, bass.ds(n * 4 * P, 4 * P)].bitcast(F32)
                                 ).then_inc(qs_in[par], 16)

                def load_v(n, par):
                    sp.dma_start(vs[par][:, :, :], vb[:, n // 8, :, :]).then_inc(vs_in[par], 16)

                sp.wait_ge(high_made, TILES * (b + 1))
                sp.wait_ge(low_made, TILES * (b + 1))
                sp.wait_ge(v_made, TILES * (b + 1))
                load_q(0, 0)
                load_q(1, 1)
                load_v(0, 0)
                with sp.Fori(1, BLOCKS // 2) as i:
                    sp.wait_ge(scored, b * UNITS + i * BODY - 4)
                    load_q(2 * i, 0)
                    sp.wait_ge(pv_made, FIRST + b * BLOCKS + 2 * i - 2)
                    load_v(2 * i - 1, 1)
                    sp.wait_ge(scored, b * UNITS + i * BODY)
                    load_q(2 * i + 1, 1)
                    sp.wait_ge(pv_made, FIRST + b * BLOCKS + 2 * i - 1)
                    load_v(2 * i, 0)
                sp.wait_ge(pv_made, FIRST + b * BLOCKS + BLOCKS - 2)
                load_v(BLOCKS - 1, 1)

        @block.gpsimd
        def _(pool):
            pool.memset(ident[:, :], 0.0).then_inc(pool_step, 1)
            pool.memset(c["ones"][:, :], 1.0).then_inc(pool_step, 1)
            pool.wait_ge(pool_step, 1)
            pool.affine_select(out=ident[:, :], in_=ident[:, :], compare_op=ALU.not_equal, fill=1.0, base=0,
                               pattern=[[-1, P]], channel_multiplier=1).then_inc(ident_made, 1)
            with pool.Fori(0, BATCH) as b:
                for j in range(TILES):
                    at = slice((j % 2) * P, (j % 2) * P + P)
                    pool.wait_ge(qn_made, TILES * b + j + 1)
                    if j:
                        pool.wait_ge(qn_turned, TILES * b + j)
                    pool.sem_inc(pool_step, 1)
                    pool.tensor_scalar(qn[:, :, 1, :], qn[:, :, 0, :], 1.0, 0.0, ALU.mult, ALU.add).then_inc(twin_made, 1)
                    pool.wait_ge(t1_made, TILES * b + j + 1)
                    pool.sem_inc(pool_step, 1)
                    pool.tensor_scalar(kh[:, :, j * P:(j + 1) * P], t1[:, HEADS:, :], 1.0, 0.0, ALU.mult, ALU.add)
                    for h in range(2):
                        last = pool.tensor_scalar(qx[:, :, j // 2, h, at],
                                                  t1[:, 0:HEADS, :].rearrange("p (g h) q -> p g h q", h=2)[:, :, h, :],
                                                  1.0, 0.0, ALU.mult, ALU.add)
                    last.then_inc(high_made, 1)

                def norm(i, u):
                    pool.wait_ge(rinv_made, b * UNITS + i * BODY + u + 1)
                    pool.sem_inc(pool_step, 1)
                    pool.tensor_scalar(probs[u % 4], probs[u % 4], rinv[:, u % 4:u % 4 + 1], 1.0,
                                       ALU.mult, ALU.mult).then_inc(normed, 1)

                with pool.Fori(0, BLOCKS // 2) as i:
                    for u in range(BODY):
                        norm(i, u)

        @block.tensor
        def _(pe):
            pe.wait_ge(ident_made, 1)
            pe.wait_ge(r_in, 16 * N_RAW)
            pe.wait_ge(w_float, 1)
            for t in range(W_TILES):
                last = pe.transpose(psum[:, 2 * SEQ + t * P:2 * SEQ + (t + 1) * P], raw[:, t * P:(t + 1) * P], ident[:, :])
            last.then_inc(w_turned, 1)
            pe.wait_ge(w_kept, 1)
            pe.wait_ge(w_centred, 1)
            pe.sem_inc(pv_made, FIRST)
            with pe.Fori(0, BATCH) as b:
                pe.wait_ge(xn_made, b + 1)
                pe.wait_ge(x_added, FIRST + b * BLOCKS)
                for j in range(TILES):
                    last = pe.transpose(psum[:, j * P:(j + 1) * P], cen[:, j, :], ident[:, :])
                last.then_inc(xn_turned, 1)
                pe.wait_ge(xnt_made, b + 1)
                for j in range(TILES):
                    if j:
                        pe.wait_ge(qn_made, TILES * b + j)
                        pe.wait_ge(v_made, TILES * b + j)
                    for n in range(QKV // 512):
                        last = pe.matmul(qkv[:, n * 512:(n + 1) * 512], xnt[:, j * P:(j + 1) * P],
                                         wqkv[:, n * 512:(n + 1) * 512], start=True, stop=True)
                    last.then_inc(qkv_made, 1)
                    pe.wait_ge(qn_made, TILES * b + j + 1)
                    pe.wait_ge(twin_made, TILES * b + j + 1)
                    if j:
                        pe.wait_ge(t1_made, TILES * b + j)
                    for h in range(NORMED):
                        last = pe.transpose(qnt[:, h * P:(h + 1) * P],
                                            qn[:, h, :, :].rearrange("p t d -> p (t d)"), ident[:, :])
                    last.then_inc(qn_turned, 1)

                pe.wait_ge(t1_made, TILES * b + TILES)
                pe.wait_ge(high_made, TILES * b + TILES)
                pe.wait_ge(low_made, TILES * b + TILES)

                def slot(i, u, part):
                    unit = b * UNITS + i * BODY + u
                    if part != "last":
                        par, v = u // 4, u % 4
                        if v == 0:
                            pe.wait_ge(qs_in[par], 16 * (b * (BLOCKS // 2) + i + 1))
                        if not (part == "first" and u < 2):
                            pe.wait_ge(exp_made, unit - 1)
                        g = i // 4
                        for half in range(2):
                            cols = slice(half * 512, half * 512 + 512)
                            pe.matmul(scores[u % 2][:, cols], qs[par][:, v, :], kl[:, g, cols], start=True, stop=False)
                            last = pe.matmul(scores[u % 2][:, cols], qs[par][:, v, :], kh[:, g, cols],
                                             start=False, stop=True)
                        last.then_inc(scored, 1)
                    if u % 4 == 3 and part != "first":
                        par = u // 4
                        n = 2 * i - 2 + par
                        pe.wait_ge(ot_made, b * BLOCKS + n + 1)
                        for t in range(2):
                            last = pe.matmul(outp[par][:, QB + t * P:QB + (t + 1) * P], ot[par][:, t * P:(t + 1) * P],
                                             wout[:, (i - 1) // 2, :], start=True, stop=True)
                        last.then_inc(y_made, 1)
                    par, n, quarter = (0, 2 * i - 2, u + 1) if u < 3 else (1, 2 * i - 1, u - 3) if u < 7 else (0, 2 * i, 0)
                    if {"first": u == 7, "mid": True, "last": u < 7}[part]:
                        if quarter == 0:
                            pe.wait_ge(kept_a, b * UNITS + 4 * n + 4)
                            pe.wait_ge(kept_b, b * UNITS + 4 * n + 4)
                            pe.wait_ge(vs_in[par], 16 * (b * (BLOCKS // 2) + (i if par == 1 else i + 1)))
                            if part != "first":
                                pe.wait_ge(x_added, FIRST + b * BLOCKS + n - 1)
                        for kt in range(2 * quarter, 2 * quarter + 2):
                            for h in range(2):
                                last = pe.matmul(outp[par][h * DH:(h + 1) * DH, 0:QB], vs[par][:, kt, :], pt[par][:, h, kt, :],
                                                 start=(kt == 0), stop=(kt == TILES - 1))
                        if quarter == 3:
                            last.then_inc(pv_made, 1)
                    if {"first": u >= T_LAG, "mid": True, "last": u < T_LAG}[part]:
                        w = (u - T_LAG) % BODY
                        pe.wait_ge(normed, unit - T_LAG + 1)
                        if not (part == "first" and u == T_LAG):
                            pe.wait_ge(kept_a, unit - T_LAG)
                            pe.wait_ge(kept_b, unit - T_LAG)
                        for kt in range(TILES):
                            last = pe.transpose(turned[:, kt * P:(kt + 1) * P], probs[w % 4][:, kt * P:(kt + 1) * P], ident[:, :])
                            if kt == TILES // 2 - 1:
                                last.then_inc(turned_a, 1)
                        last.then_inc(turned_b, 1)

                for u in range(BODY):
                    slot(0, u, "first")
                with pe.Fori(1, BLOCKS // 2) as i:
                    for u in range(BODY):
                        slot(i, u, "mid")
                for u in range(BODY):
                    slot(BLOCKS // 2, u, "last")

        @block.scalar
        def _(act):
            act.dma_start(raw[:, 0:2 * P].rearrange("p (t d) -> p t d", t=2), a["L1_attn_Wu"].rearrange("(t p) d -> p t d", p=P)).then_inc(r_in, 16)
            act.dma_start(raw[:, 2 * P:4 * P].rearrange("p (t d) -> p t d", t=2), a["L1_attn_Wv"].rearrange("(t p) d -> p t d", p=P)).then_inc(r_in, 16)
            act.dma_start(raw[:, 4 * P:5 * P], a["L1_attn_Wb"]).then_inc(r_in, 16)
            act.dma_start(raw[:, W_O * P:W_GATE * P], a["L1_attn_Wo"]).then_inc(r_in, 16)
            act.dma_start(rawi[:, 0:HID1].rearrange("p (t d) -> p t d", t=HT), a["L1_ffn_w_gate"].rearrange("(t p) d -> p t d", p=P)).then_inc(r_in, 16)
            act.dma_start(rawi[:, HID1:2 * HID1].rearrange("p (t d) -> p t d", t=HT), a["L1_ffn_w_up"].rearrange("(t p) d -> p t d", p=P)).then_inc(r_in, 16)
            act.dma_start(rawi[:, 2 * HID1:3 * HID1], a["L1_ffn_w_down"]).then_inc(r_in, 16)
            act.wait_ge(w_turned, 1)
            act.activation(wt[:, 0:SEQ], psum[:, 2 * SEQ:3 * SEQ], ACT.Copy)
            act.activation(wt[:, SEQ:2 * SEQ], psum[:, 3 * SEQ:4 * SEQ], ACT.Copy).then_inc(w_kept, 1)
            act.wait_ge(c_in, 16 * N_SMALL)
            with act.Fori(0, BATCH) as b:
                act.wait_ge(cen_made, b + 1)
                act.activation(sq[:, 0:SEQ], cen[:, :, :].rearrange("p j d -> p (j d)"), ACT.Square).then_inc(sq_made, 1)
                act.wait_ge(var_made, b + 1)
                act.activation(st[:, 2, :], st[:, 1, :], ACT.Sqrt).then_inc(root_made, 1)
                act.wait_ge(xn_turned, b + 1)
                act.activation(xnt[:, :], psum[:, 0:SEQ], ACT.Identity, bias=aln_b[:, 0:1], scale=aln_s[:, 0:1]).then_inc(xnt_made, 1)
                for j in range(TILES):
                    act.wait_ge(qkv_made, TILES * b + j + 1)
                    if j:
                        act.wait_ge(hvar_made, TILES * b + j)
                    act.activation(hsq[:, :], qkv[:, 0:NORMED * DH], ACT.Square).then_inc(hsq_made, 1)
                    act.activation(vb[:, :, j, :], qkv[:, NORMED * DH:QKV].rearrange("p (g d) -> p g d", d=DH), ACT.Copy).then_inc(v_made, 1)
                    act.wait_ge(hvar_made, TILES * b + j + 1)
                    act.activation(hst[:, 2, :], hst[:, 1, :], ACT.Sqrt).then_inc(hroot_made, 1)
                    act.wait_ge(qn_turned, TILES * b + j + 1)
                    if j:
                        act.wait_ge(high_made, TILES * b + j)
                        act.wait_ge(low_made, TILES * b + j)
                    act.activation(t1[:, 0:HEADS, :].rearrange("p h q -> p (h q)"), qnt[:, 0:HEADS * P], ACT.Identity, bias=qk_o[:, 0:1], scale=qk_s[:, 0:1])
                    act.activation(t1[:, HEADS:, :].rearrange("p h q -> p (h q)"), qnt[:, HEADS * P:], ACT.Identity, bias=qk_o[:, 1:2], scale=qk_s[:, 1:2]).then_inc(t1_made, 1)

                def slot(i, u, part):
                    unit = b * UNITS + i * BODY + u
                    if u % 4 == 3 and part != "first":
                        par = u // 4
                        n = 2 * i - 2 + par
                        act.wait_ge(pv_made, FIRST + b * BLOCKS + n + 1)
                        act.activation(ot[par][:, :], outp[par][:, 0:QB], ACT.Copy).then_inc(ot_made, 1)
                    if {"first": u >= T_LAG, "mid": True, "last": u < T_LAG}[part]:
                        w = (u - T_LAG) % BODY
                        act.wait_ge(turned_a, unit - T_LAG + 1)
                        act.activation(pt[w // 4][:, (w % 4) // 2, 0:4, (w % 2) * P:(w % 2) * P + P],
                                       turned[:, 0:512].rearrange("p (k q) -> p k q", q=P), ACT.Copy).then_inc(kept_a, 1)
                    if part != "last":
                        act.wait_ge(max_made, unit + 1)
                        if not (part == "first" and u < 4):
                            act.wait_ge(turned_b, unit - 3)
                        act.activation(probs[u % 4], scores[u % 2], ACT.Exp, bias=nmx[:, u % 4:u % 4 + 1],
                                       accum_out=rsum[:, u % 4:u % 4 + 1]).then_inc(exp_made, 1)

                for u in range(BODY):
                    slot(0, u, "first")
                with act.Fori(1, BLOCKS // 2) as i:
                    for u in range(BODY):
                        slot(i, u, "mid")
                for u in range(BODY):
                    slot(BLOCKS // 2, u, "last")

        @block.vector
        def _(dve):
            dve.wait_ge(r_in, 16 * N_RAW)
            dve.tensor_scalar(raw[:, W_GATE * P:], rawi[:, :], SCALE1, None, ALU.mult).then_inc(w_float, 1)
            dve.wait_ge(w_in, 32)
            heads = wqkv[:, 0:NORMED * DH].rearrange("p (h d) -> p h d", d=DH)
            dve.tensor_reduce(wmean[:, :], heads, AX_X, ALU.add).then_inc(dve_step, 1)
            dve.wait_ge(dve_step, 1)
            dve.tensor_scalar(wmean[:, :], wmean[:, :], 1.0 / DH, None, ALU.mult).then_inc(dve_step, 1)
            dve.wait_ge(dve_step, 2)
            dve.tensor_tensor(heads, heads, over_last(wmean[:, :], DH), ALU.subtract).then_inc(w_centred, 1)
            dve.wait_ge(c_in, 16 * N_SMALL)
            dve.tensor_scalar(qk_s[:, 0:1], qk_s[:, 0:1], DH ** -0.5, None, ALU.mult).then_inc(dve_step, 1)
            dve.tensor_scalar(qk_o[:, 0:1], qk_o[:, 0:1], DH ** -0.5, None, ALU.mult).then_inc(dve_step, 1)
            dve.wait_ge(x_in[0], 16)
            dve.wait_ge(x_in[1], 16)
            dve.sem_inc(x_added, FIRST)
            with dve.Fori(0, BATCH) as b:
                base = 4 + 4 * b
                dve.wait_ge(dve_step, base)
                xb = x[:, b, :, :]
                dve.tensor_reduce(st[:, 0, :], xb, AX_X, ALU.add).then_inc(dve_step, 1)
                dve.wait_ge(dve_step, base + 1)
                dve.tensor_scalar(st[:, 0, :], st[:, 0, :], 1.0 / DIM, None, ALU.mult).then_inc(dve_step, 1)
                dve.wait_ge(dve_step, base + 2)
                dve.tensor_tensor(cen[:, :, :], xb, over_last(st[:, 0, :], DIM), ALU.subtract).then_inc(cen_made, 1)
                dve.wait_ge(sq_made, b + 1)
                dve.tensor_reduce(st[:, 1, :], sq[:, 0:SEQ].rearrange("p (j d) -> p j d", d=DIM), AX_X, ALU.add).then_inc(dve_step, 1)
                dve.wait_ge(dve_step, base + 3)
                dve.tensor_scalar(st[:, 1, :], st[:, 1, :], (1.0 + ATT_EPS) / DIM, ATT_EPS * LN_EPS, ALU.mult, ALU.add).then_inc(var_made, 1)
                dve.wait_ge(root_made, b + 1)
                dve.reciprocal(st[:, 3, :], st[:, 2, :]).then_inc(dve_step, 1)
                dve.wait_ge(dve_step, base + 4)
                dve.tensor_tensor(cen[:, :, :], cen[:, :, :], over_last(st[:, 3, :], DIM), ALU.mult).then_inc(xn_made, 1)

                def low(j):
                    at = slice((j % 2) * P, (j % 2) * P + P)
                    dve.wait_ge(high_made, TILES * b + j + 1)
                    for h in range(2):
                        part = qx[DH:P, :, j // 2, h, at]
                        dve.tensor_tensor(part, t1[DH:P, 0:HEADS, :].rearrange("p (g h) q -> p g h q", h=2)[:, :, h, :],
                                          part.bitcast(F32), ALU.subtract)
                    dve.tensor_tensor(kl[:, :, j * P:(j + 1) * P], t1[:, HEADS:, :], kh[:, :, j * P:(j + 1) * P].bitcast(F32),
                                      ALU.subtract).then_inc(low_made, 1)

                for j in range(TILES):
                    n = TILES * b + j
                    dve.wait_ge(hsq_made, n + 1)
                    dve.tensor_reduce(hst[:, 0, :], hsq.rearrange("p (h d) -> p h d", d=DH), AX_X, ALU.add)\
                       .then_inc(hsum, 1)
                    dve.wait_ge(hsum, 2 * n + 1)
                    dve.tensor_scalar(hst[:, 1, :], hst[:, 0, :], 1.0 / DH, ATT_EPS, ALU.mult, ALU.add).then_inc(hvar_made, 1)
                    dve.wait_ge(hroot_made, n + 1)
                    dve.reciprocal(hst[:, 3, :], hst[:, 2, :]).then_inc(hsum, 1)
                    dve.wait_ge(hsum, 2 * n + 2)
                    if j:
                        dve.wait_ge(qn_turned, n)
                    dve.tensor_tensor(qn[:, :, 0, :], qkv[:, 0:NORMED * DH].rearrange("p (h d) -> p h d", d=DH),
                                      over_last(hst[:, 3, :], DH), ALU.mult).then_inc(qn_made, 1)
                    if j:
                        low(j - 1)
                low(TILES - 1)

                def slot(i, u, part):
                    unit = b * UNITS + i * BODY + u
                    if part != "last":
                        dve.wait_ge(scored, unit + 1)
                        dve.tensor_reduce(nmx[:, u % 4:u % 4 + 1], scores[u % 2], AX_X, ALU.max, negate=True).then_inc(max_made, 1)
                    if {"first": u > 0, "mid": True, "last": u == 0}[part]:
                        w = (u - 1) % 4
                        dve.wait_ge(exp_made, unit)
                        dve.reciprocal(rinv[:, w:w + 1], rsum[:, w:w + 1]).then_inc(rinv_made, 1)
                    if {"first": u >= T_LAG, "mid": True, "last": u < T_LAG}[part]:
                        w = (u - T_LAG) % BODY
                        dve.wait_ge(turned_b, unit - T_LAG + 1)
                        dve.tensor_copy(pt[w // 4][:, (w % 4) // 2, 4:8, (w % 2) * P:(w % 2) * P + P],
                                        turned[:, 512:1024].rearrange("p (k q) -> p k q", q=P)).then_inc(kept_b, 1)
                    if u % 4 == 3 and part != "first":
                        par = u // 4
                        n = 2 * i - 2 + par
                        dve.wait_ge(y_made, b * BLOCKS + n + 1)
                        dve.wait_ge(x_added, FIRST + b * BLOCKS + n)
                        at = x[:, b, bass.ds(2 * (2 * ((i - 1) % 2) + par), 2), :]
                        dve.tensor_tensor(at, at, outp[par][:, QB:2 * QB].rearrange("p (t d) -> p t d", d=DIM), ALU.add)\
                           .then_inc(x_added, 1)

                for u in range(BODY):
                    slot(0, u, "first")
                with dve.Fori(1, BLOCKS // 2) as i:
                    for u in range(BODY):
                        slot(i, u, "mid")
                for u in range(BODY):
                    slot(BLOCKS // 2, u, "last")


def rest(nc, a, x, ident, wt, psum, sb, sem, out, gamma, beta, ones, wr, br, lng, lnb, uvb_bias, qk_w, qk_b, ropes, bo, rel):
    with ExitStack() as own:
        def mine(name, shape, dt=F32):
            return sb(name, shape, dt, own)

        cen = mine("cen2", [P, BATCH, TILES, DIM])
        sq = mine("sq2", [P, SEQ])
        st = mine("st2", [P, 2 * 4 * BATCH, 2, TILES])
        sm = mine("sm2", [P, 2 * 4 * BATCH, 2, TILES])
        y0 = mine("y0", [P, BATCH, TILES, DIM])
        turned = mine("turned_rows", [P, BATCH, SEQ])
        ysum = mine("ysum", [P, BATCH])
        router = mine("router", [1, BATCH, 8, EXPERTS])
        chosen = mine("chosen", [1, BATCH, EXPERTS], U32)
        wv = mine("wv", [1, BATCH, 4])
        wb = mine("wb", [P, BATCH, TOP])
        w1s = mine("w1s", [P, BATCH, TOP, HID])
        w2s = mine("w2s", [P, BATCH, TOP, FT, DIM])
        b1s = mine("b1s", [P, BATCH, TOP, FT])
        b2s = mine("b2s", [1, BATCH, TOP, DIM])
        b2w = mine("b2w", [1, BATCH, 2, DIM])
        hid = [mine(f"hid{i}", [P, TOP * FT, 512]) for i in range(2)]
        pre = [mine(f"pre{i}", [P, 2, UVB]) for i in range(2)]
        uv = mine("uv", [P, TILES, 2, UVB])
        qk = mine("qk", [P, 2, 2, S])
        rq = mine("rq", [P, 3, S])
        junk = mine("junk", [P, 3, S])
        dots = mine("dots", [P, TILES, 3])
        kern = mine("kern", [P, TILES, 3])
        mix = [mine(f"mix{i}", [P, 2, EH]) for i in range(2)]
        mixa = mine("mixa", [P, 2, EH])
        mixt = [mine(f"mixt{i}", [P, 2 * EH]) for i in range(2)]
        short = mine("short", [P, BATCH, TILES, DIM])
        gate = [mine(f"gate{i}", [P, HT, 512]) for i in range(2)]
        hid1 = [mine(f"hid1{i}", [P, HT, 512]) for i in range(2)]

        step = sem("step")
        cen_made = sem("cen2_made")
        sq_made = sem("sq2_made")
        var_made = sem("var2_made")
        root_made = sem("root2_made")
        rows_made = sem("rows_made")
        rows_turned = sem("rows_turned")
        rows_kept = sem("rows_kept")
        ysum_made = sem("ysum_made")
        logits_made = sem("logits_made")
        shifted = sem("shifted")
        exp_made = sem("exp2_made")
        chosen_made = sem("chosen_made")
        wv_made = sem("wv_made")
        wb_spread = sem("wb_spread")
        exp_w = sem("exp_w")
        experts_in = [sem(f"experts_in{b}") for b in range(BATCH)]
        w2_scaled = sem("w2_scaled")
        hid_made = sem("hid_made")
        gelu_made = sem("gelu_made")
        ffn_made = sem("ffn_made")
        ffn_taken = sem("ffn_taken")
        uvb_made = sem("uvb_made")
        pre_made = sem("pre_made")
        silu_made = sem("silu_made")
        mix_made = sem("mix_made")
        mix_turned = sem("mix_turned")
        mix_kept = sem("mix_kept")
        gau_made = sem("gau_made")
        gau_taken = sem("gau_taken")
        pair_made = sem("pair_made")
        gate_made = sem("gate_made")
        up_taken = sem("up_taken")
        down_made = sem("down_made")
        down_taken = sem("down_taken")
        stored = sem("stored")

        CHUNKS = 4
        EXPERT_DMAS = 4 * TOP

        def uvb_psum(j, l):
            return psum[:, ((j % 2) * 2 + l) * SEQ:((j % 2) * 2 + l) * SEQ + UVB]

        def gau_dots(dve, link, j):
            dve.wait_ge(silu_made, j + 1)
            for l in range(2):
                last = dve.tensor_tensor(qk[:, l, :, :], over_mid(uv[:, j, l, 2 * EH:UVB], 2), qk_w[:, :, :], ALU.mult)
            link(last)
            for l in range(2):
                last = dve.tensor_tensor(qk[:, l, :, :], qk[:, l, :, :], qk_b[:, :, :], ALU.add)
            link(last)
            h = S // 2
            q1 = qk[:, 1, 0, :]
            dve.tensor_tensor(rq[:, 0, 0:h], q1[:, h:S], ropes[:, 1, 0:h], ALU.mult)
            dve.tensor_tensor(rq[:, 0, h:S], q1[:, 0:h], ropes[:, 1, h:S], ALU.mult)
            link(dve.tensor_tensor(rq[:, 1, :], q1, ropes[:, 0, :], ALU.mult))
            link(dve.tensor_tensor(rq[:, 2, :], rq[:, 0, :], rq[:, 1, :], ALU.add))
            for n, (q, k) in enumerate(((qk[:, 0, 0, :], qk[:, 0, 1, :]), (rq[:, 2, :], qk[:, 0, 1, :]), (q1, qk[:, 1, 1, :]))):
                last = dve.tensor_tensor_reduce(junk[:, n, :], q, k, 1.0, 0.0, ALU.mult, ALU.add, dots[:, j, n:n + 1])
            link(last)

        def gau_take(dve, j):
            dve.wait_ge(gau_made, j + 1)
            dve.tensor_tensor(x[:, :, j, :], psum[:, SEQ + (j % 2) * 512:SEQ + (j % 2) * 512 + 2 * P].rearrange("p (l d) -> p l d", d=DIM),
                              short[:, :, j, :], ALU.add).then_inc(gau_taken, 1)

        def down_take(dve, c):
            b, t = c // 2, 4 * (c % 2)
            dve.wait_ge(down_made, c + 1)
            dve.tensor_tensor(x[:, b, t:t + 4, :], psum[:, 2 * SEQ + (c % 2) * 512:2 * SEQ + (c % 2 + 1) * 512].rearrange("p (t d) -> p t d", d=DIM),
                              x[:, b, t:t + 4, :], ALU.add).then_inc(down_taken, 1)

        block = own.enter_context(nc.Block())

        @block.sync
        def _(sp):
            for b in range(BATCH):
                sp.wait_ge(chosen_made, b + 1)
                for k in range(TOP):
                    e = sp.value_load(chosen[0:1, b, k:k + 1], min_val=0, max_val=EXPERTS - 1)
                    sp.dma_start(w1s[:, b, k, :], a["L0_ffn_W1"][bass.ds(e, 1), :, :].rearrange("e d f -> d (e f)")).then_inc(experts_in[b], 16)
                    sp.dma_start(w2s[:, b, k, :, :], a["L0_ffn_W2"][bass.ds(e, 1), :, :].rearrange("e (t f) d -> f (e t) d", f=P)).then_inc(experts_in[b], 16)
                    sp.dma_start(b1s[:, b, k, :], a["L0_ffn_b1"][bass.ds(e, 1), :].rearrange("e (t f) -> f (e t)", f=P), allow_slow_non_contiguous=True).then_inc(experts_in[b], 16)
                    sp.dma_start(b2s[:, b, k, :], a["L0_ffn_b2"][bass.ds(e, 1), :]).then_inc(experts_in[b], 16)
            for c in range(CHUNKS):
                sp.wait_ge(down_taken, c + 1)
                b, t = c // 2, 4 * (c % 2)
                sp.dma_start(out[b].rearrange("(p j) d -> p j d", j=TILES)[:, t:t + 4, :], x[:, b, t:t + 4, :]).then_inc(stored, 16)
            sp.wait_ge(stored, 16 * CHUNKS)

        @block.tensor
        def _(pe):
            def turn(k, b):
                pe.wait_ge(rows_made, 2 * k + b + 1)
                for j in range(TILES):
                    last = pe.transpose(psum[:, b * SEQ + j * P:b * SEQ + (j + 1) * P], y0[:, b, j, :], ident[:, :])
                last.then_inc(rows_turned, 1)

            for b in range(BATCH):
                turn(0, b)
            for b in range(BATCH):
                pe.wait_ge(ysum_made, b + 1)
                at = psum[:, 2 * SEQ + b * 512:2 * SEQ + (b + 1) * 512]
                pe.matmul(at[0:1, 0:EXPERTS], ysum[:, b:b + 1], wr[:, :], start=True, stop=True).then_inc(logits_made, 1)
            for b in range(BATCH):
                pe.wait_ge(wv_made, b + 1)
                at = psum[:, 3 * SEQ + b * 512:3 * SEQ + (b + 1) * 512]
                pe.matmul(at[:, 0:TOP], ones[0:1, :], wv[:, b, 0:TOP], start=True, stop=True).then_inc(wb_spread, 1)

            def ffn_up(c):
                b, at = c // 2, slice((c % 2) * 512, (c % 2) * 512 + 512)
                if c % 2 == 0:
                    pe.wait_ge(experts_in[b], 16 * EXPERT_DMAS)
                for n in range(TOP * FT):
                    m = c * TOP * FT + n
                    if m >= 4:
                        pe.wait_ge(gelu_made, m - 3)
                    pe.matmul(psum[:, (m % 4) * 512:(m % 4 + 1) * 512], w1s[:, b, n // FT, (n % FT) * P:(n % FT + 1) * P],
                              turned[:, b, at], start=True, stop=True).then_inc(hid_made, 1)

            def ffn_down(c):
                b = c // 2
                pe.wait_ge(gelu_made, (c + 1) * TOP * FT)
                pe.wait_ge(w2_scaled, b + 1)
                if c >= 2:
                    pe.wait_ge(ffn_taken, c - 1)
                at = psum[:, 2 * SEQ + (c % 2) * 512:2 * SEQ + (c % 2 + 1) * 512]
                for t in range(4):
                    o = at[:, t * P:(t + 1) * P]
                    pe.matmul(o, ones[0:1, :], b2w[:, b, 1, :], start=True, stop=False)
                    for n in range(TOP * FT):
                        last = pe.matmul(o, hid[c % 2][:, n, t * P:(t + 1) * P], w2s[:, b, n // FT, n % FT, :],
                                         start=False, stop=(n == TOP * FT - 1))
                last.then_inc(ffn_made, 1)

            pe.wait_ge(rows_kept, 2)
            pe.wait_ge(w2_scaled, 1)
            for c in range(CHUNKS):
                ffn_up(c)
                if c:
                    ffn_down(c - 1)
            ffn_down(CHUNKS - 1)

            for b in range(BATCH):
                turn(1, b)
            pe.wait_ge(rows_kept, 4)
            def gau_in(j):
                if j >= 2:
                    pe.wait_ge(pre_made, j - 1)
                for l in range(2):
                    at = uvb_psum(j, l)
                    rows = turned[:, l, j * P:(j + 1) * P]
                    pe.matmul(at[:, 0:512], rows, wt[:, 0:512], start=True, stop=True)
                    last = pe.matmul(at[:, 512:UVB], rows, wt[:, 512:UVB], start=True, stop=True)
                last.then_inc(uvb_made, 1)

            for j in range(TILES):
                gau_in(j)
            for j in range(TILES):
                pe.wait_ge(mix_made, j + 1)
                if j == 0:
                    pe.wait_ge(pre_made, TILES)
                if j >= 2:
                    pe.wait_ge(mix_kept, j - 1)
                at = psum[:, (j % 2) * 512:(j % 2 + 1) * 512]
                for n in range(4):
                    last = pe.transpose(at[:, n * P:(n + 1) * P], mix[j % 2][:, n // 2, (n % 2) * P:(n % 2 + 1) * P], ident[:, :])
                last.then_inc(mix_turned, 1)
                pe.wait_ge(mix_kept, j + 1)
                if j >= 2:
                    pe.wait_ge(gau_taken, j - 1)
                at = psum[:, SEQ + (j % 2) * 512:SEQ + (j % 2 + 1) * 512]
                for l in range(2):
                    for e in range(2):
                        last = pe.matmul(at[:, l * P:(l + 1) * P], mixt[j % 2][:, (2 * l + e) * P:(2 * l + e + 1) * P],
                                         wt[:, (W_O + e) * P:(W_O + e + 1) * P], start=(e == 0), stop=(e == 1))
                last.then_inc(gau_made, 1)

            for b in range(BATCH):
                turn(2, b)
            pe.wait_ge(rows_kept, 6)

            def gate_up(c):
                b, at = c // 2, slice((c % 2) * 512, (c % 2) * 512 + 512)
                for n in range(HT):
                    m = c * HT + n
                    if m >= 2:
                        pe.wait_ge(up_taken, m - 1)
                    for k, w in enumerate((W_GATE, W_UP)):
                        last = pe.matmul(psum[:, ((m % 2) * 2 + k) * 512:((m % 2) * 2 + k + 1) * 512],
                                         wt[:, (w + n) * P:(w + n + 1) * P], turned[:, b, at], start=True, stop=True)
                    last.then_inc(pair_made, 1)

            def down(c):
                pe.wait_ge(up_taken, (c + 1) * HT)
                if c >= 2:
                    pe.wait_ge(down_taken, c - 1)
                for t in range(4):
                    for n in range(HT):
                        last = pe.matmul(psum[:, 2 * SEQ + (c % 2) * 512 + t * P:2 * SEQ + (c % 2) * 512 + (t + 1) * P],
                                         hid1[c % 2][:, n, t * P:(t + 1) * P], wt[:, (W_DOWN + n) * P:(W_DOWN + n + 1) * P],
                                         start=(n == 0), stop=(n == HT - 1))
                last.then_inc(down_made, 1)

            for c in range(CHUNKS):
                gate_up(c)
                if c:
                    down(c - 1)
            down(CHUNKS - 1)

        @block.scalar
        def _(act):
            def ln(k):
                act.wait_ge(cen_made, k + 1)
                if k:
                    act.wait_ge(var_made, k)
                act.activation(sq[:, :], cen[:, k % 2, :, :].rearrange("p j d -> p (j d)"), ACT.Square).then_inc(sq_made, 1)
                act.wait_ge(var_made, k + 1)
                act.activation(sm[:, k, :, :], st[:, k, :, :], ACT.Sqrt).then_inc(root_made, 1)

            def keep(k, b, scale=None, bias=None):
                act.wait_ge(rows_turned, 2 * k + b + 1)
                src = psum[:, b * SEQ:(b + 1) * SEQ]
                if scale is None:
                    act.activation(turned[:, b, :], src, ACT.Copy).then_inc(rows_kept, 1)
                else:
                    act.activation(turned[:, b, :], src, ACT.Identity, bias=bias, scale=scale).then_inc(rows_kept, 1)

            for b in range(BATCH):
                ln(b)
            for b in range(BATCH):
                keep(0, b)
            for b in range(BATCH):
                act.wait_ge(shifted, 2 * b + 1)
                act.activation(router[:, b, 2, :], router[:, b, 1, :], ACT.Exp, accum_out=wv[:, b, 2:3]).then_inc(exp_made, 1)
                act.wait_ge(shifted, 2 * b + 2)
                act.activation(router[:, b, 6, 0:1], router[:, b, 5, 0:1], ACT.Exp).then_inc(exp_w, 1)
            for m in range(CHUNKS * TOP * FT):
                c, n = m // (TOP * FT), m % (TOP * FT)
                b = c // 2
                act.wait_ge(hid_made, m + 1)
                if n == 0:
                    act.wait_ge(experts_in[b], 16 * EXPERT_DMAS)
                    if c >= 2:
                        act.wait_ge(ffn_made, c - 1)
                act.activation(hid[c % 2][:, n, :], psum[:, (m % 4) * 512:(m % 4 + 1) * 512], ACT.Gelu,
                               bias=b1s[:, b, n // FT, n % FT:n % FT + 1]).then_inc(gelu_made, 1)
            for k in (2, 3, 4, 5):
                ln(k)
            for b in range(BATCH):
                keep(1, b, lng[:, 0:1], lnb[:, 0:1])
            for j in range(TILES):
                act.wait_ge(pre_made, j + 1)
                act.activation(uv[:, j, :, :], pre[j % 2][:, :, :], ACT.Silu).then_inc(silu_made, 1)
            for j in range(TILES):
                act.wait_ge(mix_turned, j + 1)
                if j >= 2:
                    act.wait_ge(gau_made, j - 1)
                act.activation(mixt[j % 2][:, :], psum[:, (j % 2) * 512:(j % 2 + 1) * 512], ACT.Copy).then_inc(mix_kept, 1)
            for k in (6, 7):
                ln(k)
            for b in range(BATCH):
                keep(2, b)
            for m in range(CHUNKS * HT):
                c, n = m // HT, m % HT
                act.wait_ge(pair_made, m + 1)
                if m >= 2 * HT:
                    act.wait_ge(up_taken, m - 2 * HT + 1)
                act.activation(gate[c % 2][:, n, :], psum[:, (m % 2) * 2 * 512:((m % 2) * 2 + 1) * 512], ACT.Silu).then_inc(gate_made, 1)

        @block.vector
        def _(dve):
            steps = [0]

            def link(ins):
                steps[0] += 1
                ins.then_inc(step, 1)
                dve.wait_ge(step, steps[0])

            def ln(k, src, eps, outer=None):
                cb = cen[:, k % 2, :, :]
                link(dve.tensor_reduce(sm[:, k, 0, :], src, AX_X, ALU.add))
                link(dve.tensor_scalar(sm[:, k, 0, :], sm[:, k, 0, :], 1.0 / DIM, None, ALU.mult))
                dve.tensor_tensor(cb, src, over_last(sm[:, k, 0, :], DIM), ALU.subtract).then_inc(cen_made, 1)
                dve.wait_ge(sq_made, k + 1)
                link(dve.tensor_reduce(st[:, k, 0, :], sq[:, :].rearrange("p (j d) -> p j d", d=DIM), AX_X, ALU.add))
                second = outer if outer is not None else 0.0
                link(dve.tensor_scalar(st[:, k, 1, :], st[:, k, 0, :], (1.0 + second) / DIM, second * eps if second else eps, ALU.mult, ALU.add))
                dve.tensor_scalar(st[:, k, 0, :], st[:, k, 0, :], 1.0 / DIM, eps, ALU.mult, ALU.add).then_inc(var_made, 1)
                dve.wait_ge(root_made, k + 1)
                link(dve.reciprocal(sm[:, k, :, :], sm[:, k, :, :]))

            def ready(last):
                last.then_inc(rows_made, 1)

            for b in range(BATCH):
                ln(b, x[:, b, :, :], LN_EPS)
                ready(dve.tensor_tensor(y0[:, b, :, :], cen[:, b, :, :], over_last(sm[:, b, 0, :], DIM), ALU.mult))
            for b in range(BATCH):
                dve.wait_ge(rows_kept, b + 1)
                dve.tensor_reduce(ysum[:, b:b + 1], turned[:, b, :], AX_X, ALU.add).then_inc(ysum_made, 1)
            for b in range(BATCH):
                r = router[:, b, :, :]
                dve.wait_ge(logits_made, b + 1)
                link(dve.scalar_tensor_tensor(out=r[:, 0, :], in0=psum[0:1, 2 * SEQ + b * 512:2 * SEQ + b * 512 + EXPERTS], scalar=1.0 / SEQ,
                                              in1=br[:, :], op0=ALU.mult, op1=ALU.add))
                link(dve.tensor_reduce(wv[:, b, 3:4], r[:, 0, :], AX_X, ALU.max))
                dve.tensor_scalar(r[:, 1, :], r[:, 0, :], wv[:, b, 3:4], None, ALU.subtract).then_inc(shifted, 1)
                dve.wait_ge(exp_made, b + 1)
                link(dve.reciprocal(wv[:, b, 2:3], wv[:, b, 2:3]))
                link(dve.tensor_scalar(r[:, 3, :], r[:, 2, :], wv[:, b, 2:3], None, ALU.mult))
                link(dve.max(r[:, 4, :], r[:, 3, :]))
                dve.max_index(chosen[:, b, :], r[:, 4, :], r[:, 3, :]).then_inc(chosen_made, 1)
                dve.tensor_tensor(r[:, 5, 0:1], r[:, 4, 1:2], r[:, 4, 0:1], ALU.subtract).then_inc(shifted, 1)
                dve.wait_ge(exp_w, b + 1)
                link(dve.tensor_scalar(r[:, 6, 1:2], r[:, 6, 0:1], 1.0, None, ALU.add))
                link(dve.reciprocal(wv[:, b, 0:1], r[:, 6, 1:2]))
                dve.tensor_tensor(wv[:, b, 1:2], wv[:, b, 0:1], r[:, 6, 0:1], ALU.mult).then_inc(wv_made, 1)
            for b in range(BATCH):
                dve.wait_ge(wb_spread, b + 1)
                link(dve.tensor_copy(wb[:, b, :], psum[:, 3 * SEQ + b * 512:3 * SEQ + b * 512 + TOP]))
                dve.wait_ge(experts_in[b], 16 * EXPERT_DMAS)
                dve.wait_ge(wv_made, b + 1)
                for k in range(TOP):
                    dve.tensor_scalar(w2s[:, b, k, :, :], w2s[:, b, k, :, :], wb[:, b, k:k + 1], None, ALU.mult)
                link(dve.tensor_scalar(b2w[:, b, 0, :], b2s[:, b, 0, :], wv[:, b, 0:1], None, ALU.mult))
                dve.scalar_tensor_tensor(out=b2w[:, b, 1, :], in0=b2s[:, b, 1, :], scalar=wv[:, b, 1:2], in1=b2w[:, b, 0, :],
                                         op0=ALU.mult, op1=ALU.add).then_inc(w2_scaled, 1)
            for c in range(CHUNKS):
                b, t = c // 2, 4 * (c % 2)
                dve.wait_ge(ffn_made, c + 1)
                dve.tensor_tensor(y0[:, b, t:t + 4, :], psum[:, 2 * SEQ + (c % 2) * 512:2 * SEQ + (c % 2 + 1) * 512].rearrange("p (t d) -> p t d", d=DIM),
                                  y0[:, b, t:t + 4, :], ALU.add).then_inc(ffn_taken, 1)
            for b in range(BATCH):
                k = 2 + b
                dve.wait_ge(ffn_taken, 2 * (b + 1))
                ln(k, y0[:, b, :, :], LN_EPS)
                cb = cen[:, b, :, :]
                link(dve.tensor_tensor(cb, cb, over_last(sm[:, k, 0, :], DIM), ALU.mult))
                link(dve.tensor_tensor(cb, cb, over_mid(gamma[:, :], TILES), ALU.mult))
                link(dve.tensor_tensor(cb, cb, over_mid(beta[:, :], TILES), ALU.add))
                link(dve.tensor_tensor(x[:, b, :, :], x[:, b, :, :], cb, ALU.add))
            for b in range(BATCH):
                k = 4 + b
                ln(k, x[:, b, :, :], LN_EPS, LN_EPS)
                cb = cen[:, b, :, :]
                ready(dve.tensor_tensor(y0[:, b, :, :], cb, over_last(sm[:, k, 1, :], DIM), ALU.mult))
                link(dve.tensor_tensor(cb, cb, over_last(sm[:, k, 0, :], DIM), ALU.mult))
                link(dve.tensor_tensor(cb, cb, over_mid(bo[:, :], TILES), ALU.add))
                link(dve.tensor_tensor(short[:, b, :, :], cb, x[:, b, :, :], ALU.add))
            for j in range(TILES):
                dve.wait_ge(uvb_made, j + 1)
                if j >= 2:
                    dve.wait_ge(silu_made, j - 1)
                for l in range(2):
                    last = dve.tensor_tensor(pre[j % 2][:, l, :], uvb_psum(j, l), uvb_bias[:, :], ALU.add)
                last.then_inc(pre_made, 1)
                if j:
                    gau_dots(dve, link, j - 1)
            gau_dots(dve, link, TILES - 1)
            link(dve.scalar_tensor_tensor(out=kern[:, :, :], in0=dots[:, :, :], scalar=1.0 / CHUNK, in1=over_mid(rel[:, :], TILES), op0=ALU.mult, op1=ALU.add))
            link(dve.tensor_scalar(kern[:, :, :], kern[:, :, :], 0.0, None, ALU.max))
            link(dve.tensor_tensor(kern[:, :, :], kern[:, :, :], kern[:, :, :], ALU.mult))
            for j in range(TILES):
                if j >= 2:
                    dve.wait_ge(mix_turned, j - 1)
                u = [uv[:, j, l, 0:EH] for l in range(2)]
                v = [uv[:, j, l, EH:2 * EH] for l in range(2)]
                dve.scalar_tensor_tensor(out=mix[j % 2][:, 0, :], in0=v[0], scalar=kern[:, j, 0:1], in1=u[0], op0=ALU.mult, op1=ALU.mult)
                link(dve.tensor_scalar(mixa[:, 0, :], v[0], kern[:, j, 1:2], None, ALU.mult))
                link(dve.scalar_tensor_tensor(out=mixa[:, 1, :], in0=v[1], scalar=kern[:, j, 2:3], in1=mixa[:, 0, :], op0=ALU.mult, op1=ALU.add))
                dve.tensor_tensor(mix[j % 2][:, 1, :], mixa[:, 1, :], u[1], ALU.mult).then_inc(mix_made, 1)
                if j:
                    gau_take(dve, j - 1)
            gau_take(dve, TILES - 1)
            for b in range(BATCH):
                k = 6 + b
                dve.wait_ge(gau_taken, TILES)
                ln(k, x[:, b, :, :], LN_EPS)
                ready(dve.tensor_tensor(y0[:, b, :, :], cen[:, b, :, :], over_last(sm[:, k, 0, :], DIM), ALU.mult))
            for m in range(CHUNKS * HT):
                c, n = m // HT, m % HT
                dve.wait_ge(gate_made, m + 1)
                if n == 0 and c >= 2:
                    dve.wait_ge(down_made, c - 1)
                dve.tensor_tensor(hid1[c % 2][:, n, :], psum[:, ((m % 2) * 2 + 1) * 512:((m % 2) * 2 + 2) * 512], gate[c % 2][:, n, :], ALU.mult)\
                   .then_inc(up_taken, 1)
                if n == HT - 1 and c:
                    down_take(dve, c - 1)
            down_take(dve, CHUNKS - 1)


_OUTS = [((BATCH, SEQ, DIM), "float32")]


def rope_rows():
    half = S // 2
    angle = np.float32(10000.0) ** (-np.arange(half, dtype=np.float32) / np.float32(half))
    cos, sin = np.cos(angle), np.sin(angle)
    return np.stack([np.concatenate([cos, cos]), np.concatenate([-sin, sin])]).astype(np.float32)


def kernel(**inputs):
    import concourse.bacc as _bacc
    from concourse.bass_utils import run_bass_kernel_spmd as _run

    nc = _bacc.Bacc("TRN2", target_bir_lowering=False, num_devices=1)
    arrays, args = {}, {}
    for name, value in inputs.items():
        v = np.ascontiguousarray(value)
        arrays[f"in_{name}"] = v
        args[name] = nc.dram_tensor(f"in_{name}", v.shape, mybir.dt.from_np(v.dtype), kind="ExternalInput").ap()
    rope = rope_rows()
    arrays["rope"] = rope
    rope_ap = nc.dram_tensor("rope", rope.shape, F32, kind="ExternalInput").ap()
    shape, dtype = _OUTS[0]
    out = nc.dram_tensor("out_0", shape, mybir.dt.from_np(np.dtype(dtype)), kind="ExternalOutput").ap()
    build(nc, args, rope_ap, out)
    r = _run(nc, [arrays], core_ids=[0])
    return r.results[0]["out_0"]
```

```python
from contextlib import ExitStack

import numpy as np

import concourse.bass as bass
from concourse import mybir

F32 = mybir.dt.float32
F32R = mybir.dt.float32r
I32 = mybir.dt.int32
U32 = mybir.dt.uint32
ALU = mybir.AluOpType
ACT = mybir.ActivationFunctionType
AX_X = mybir.AxisListType.X

P = 128
BATCH, SEQ, DIM = 2, 1024, 128
TILES = SEQ // P
HEADS, GROUPS, DH = 16, 4, 64
INNER, KV = HEADS * DH, GROUPS * DH
NORMED = HEADS + GROUPS
QKV = INNER + 2 * KV
EXPERTS, HID, TOP = 8, 512, 2
FT = HID // P
EH, S = 256, 128
UVB = 2 * EH + S
CHUNK = 64
HID1 = 384
HT = HID1 // P
SCALE1 = 1.0 / 127.0
LN_EPS, ATT_EPS = 1e-5, 1e-6

UNITS = 4
BLOCKS = HEADS // 2 * TILES // 2
BODY = 4
BODIES = BLOCKS // BODY
QB = 2 * P
KR = DH + UNITS
FIRST = 1
T = 4
CW = T * P
CHUNKS = BATCH * TILES // T
PAIRED = [0, 2, 1, 3]
LNS = 4 * CHUNKS
W_UVB, W_O, W_GATE, W_UP, W_DOWN, W_TILES = 0, 5, 7, 10, 13, 16


def column(v):
    return v.rearrange("(p a) -> p a", a=1)


def row(v):
    return v.rearrange("(a n) -> a n", a=1)


def everywhere(v, parts=P):
    return v.partition_broadcast(parts)


def over_last(t, n):
    return t.unsqueeze(2).broadcast_to([t.shape[0], t.shape[1], n])


def over_mid(t, m):
    return t.unsqueeze(1).broadcast_to([t.shape[0], m, t.shape[1]])


def build(nc, a, turn, out):
    with ExitStack() as ctx:
        def sb(name, shape, dt=F32, where=ctx):
            return where.enter_context(nc.sbuf_tensor(name, shape, dt))

        def sem(name):
            return ctx.enter_context(nc.semaphore(name))

        psum = ctx.enter_context(nc.psum_tensor("psum", [P, 4096], F32))
        x = sb("x", [P, BATCH, TILES, DIM])
        xv = [a["L0_attn_x"][b].rearrange("(p j) d -> p j d", j=TILES) for b in range(BATCH)]
        ident = sb("ident", [P, P])
        wt = sb("wt", [P, W_TILES * P])
        gamma = sb("gamma", [P, DIM])
        beta = sb("beta", [P, DIM])
        wr = sb("wr", [P, EXPERTS])
        br = sb("br", [1, EXPERTS])
        lng = sb("lng", [P, 1])
        lnb = sb("lnb", [P, 1])
        uvb_bias = sb("uvb_bias", [P, UVB // P])
        qk_cols = sb("qk_cols", [P, 4])
        ones_square = sb("ones_square", [P, P])
        bo = sb("bo", [P, DIM])
        rel = sb("rel", [P, 3])

        shared = dict(gamma=gamma, beta=beta, wr=wr, br=br, lng=lng, lnb=lnb, uvb_bias=uvb_bias, qk_cols=qk_cols,
                      ones_square=ones_square, bo=bo, rel=rel)
        first_layer(nc, a, xv, x, ident, wt, psum, sb, sem, shared)
        rest(nc, a, x, ident, wt, psum, sb, sem, out, shared, turn)


def first_layer(nc, a, xv, x, ident, wt, psum, sb, sem, c):
    with ExitStack() as own:
        def mine(name, shape, dt=F32):
            return sb(name, shape, dt, own)

        wqkv = mine("wqkv", [P, QKV])
        wmean = mine("wmean", [P, NORMED])
        wout = mine("wout", [P, HEADS // 2, DIM])
        aln_s = mine("aln_s", [P, 1])
        aln_b = mine("aln_b", [P, 1])
        qk_s = mine("qk_s", [P, 2])
        qk_o = mine("qk_o", [P, 2])
        st = mine("st", [P, BATCH, 4, TILES])
        hst = mine("hst", [P, 4, NORMED])
        qx = mine("qx", [P, HEADS // 2, 4, 2, QB], F32R)
        kh = mine("kh", [P, GROUPS, SEQ], F32R)
        kl = mine("kl", [P, GROUPS, SEQ], F32R)
        vb = mine("vb", [P, GROUPS, TILES, DH])
        qs = [mine(f"qs{i}", [P, UNITS, P], F32R) for i in range(BODY)]
        qm = [mine(f"qm{i}", [P, UNITS, P], F32R) for i in range(BODY)]
        kg = mine("kg", [P, SEQ], F32R)
        kgl = mine("kgl", [P, SEQ], F32R)
        vg = mine("vg", [P, TILES, DH])
        PT = TILES * 2 * QB
        space = mine("space", [P, 12 * SEQ])
        pt = [space[:, i * PT:(i + 1) * PT].rearrange("p (k q) -> p k q", k=TILES) for i in range(2)]
        work = space[:, 2 * PT:]
        acc = [work[:, i * 2 * QB:(i + 1) * 2 * QB] for i in range(2)]
        ot = [work[:, (4 + i) * QB:(5 + i) * QB] for i in range(2)]
        rinv = work[:, 6 * QB:7 * QB]
        xkeep = space[:, 11 * SEQ:]
        nmx = mine("nmx", [P, UNITS])
        raw = space[:, 0:W_TILES * P]
        rawi = work[:, 0:(W_TILES - W_GATE) * P].bitcast(I32)
        at = 0
        spaces = []
        for size in (NORMED * DH, SEQ, NORMED * P, NORMED * P, NORMED * P, NORMED * DH):
            spaces.append(space[:, at:at + size])
            at += size
        hsq = spaces[0]
        xnt = spaces[1]
        qn = spaces[2].rearrange("p (h t d) -> p h t d", t=2, d=DH)
        t1 = [t.rearrange("p (h q) -> p h q", q=P) for t in spaces[3:5]]
        qk_raw = spaces[5]
        cen = [spaces[2][:, i * SEQ:(i + 1) * SEQ].rearrange("p (j d) -> p j d", d=DIM) for i in range(BATCH)]
        sq = [spaces[3][:, i * SEQ:(i + 1) * SEQ] for i in range(BATCH)]
        x_in = [sem(f"x_in{b}") for b in range(BATCH)]
        w_in = sem("w_in")
        c_in = sem("c_in")
        r_in = sem("r_in")
        ident_made = sem("ident_made")
        w_float = sem("w_float")
        w_turned = sem("w_turned")
        w_kept = sem("w_kept")
        dve_step = sem("dve_step")
        act_step = sem("act_step")
        pool_step = sem("pool_step")
        cen_made = sem("cen_made")
        sq_made = sem("sq_made")
        var_made = sem("var_made")
        root_made = sem("root_made")
        xn_made = sem("xn_made")
        xn_turned = sem("xn_turned")
        xnt_made = sem("xnt_made")
        w_centred = sem("w_centred")
        qkv_made = sem("qkv_made")
        hsq_made = sem("hsq_made")
        hvar_made = sem("hvar_made")
        hroot_made = sem("hroot_made")
        hsum = sem("hsum")
        raw_made = sem("raw_made")
        keep_made = sem("keep_made")
        qn_made = sem("qn_made")
        v_made = sem("v_made")
        twin_made = sem("twin_made")
        qn_turned = sem("qn_turned")
        t1_made = sem("t1_made")
        high_made = sem("high_made")
        low_made = sem("low_made")
        q_in = [sem(f"q_in{i}") for i in range(BODY)]
        k_in = [sem(f"k_in{i}") for i in range(4)]
        v_in = [sem(f"v_in{i}") for i in range(4)]
        scored = sem("scored")
        max_made = sem("max_made")
        max_turned = sem("max_turned")
        max_placed = sem("max_placed")
        key_scored = sem("key_scored")
        exp_made = sem("exp_made")
        pool_added = sem("pool_added")
        pv_made = sem("pv_made")
        sums_made = sem("sums_made")
        rinv_made = sem("rinv_made")
        ot_made = sem("ot_made")
        y_made = sem("y_made")
        x_added = sem("x_added")

        small = [(c["gamma"][:, :], everywhere(a["L0_ffn_gamma"])), (c["beta"][:, :], everywhere(a["L0_ffn_beta"])),
                 (c["wr"][:, :], a["L0_ffn_Wr"]), (c["br"][:, :], row(a["L0_ffn_br"])),
                 (c["lng"][:, :], column(a["L1_attn_ln_g"])), (c["lnb"][:, :], column(a["L1_attn_ln_b"])),
                 (c["bo"][:, :], everywhere(a["L1_attn_bo"])),
                 (c["rel"][:, 0:1], everywhere(a["L1_attn_w_rel"][CHUNK - 1:CHUNK])),
                 (c["rel"][:, 1:2], everywhere(a["L1_attn_w_rel"][CHUNK - 2:CHUNK - 1])),
                 (c["rel"][:, 2:3], everywhere(a["L1_attn_w_rel"][CHUNK - 1:CHUNK]))]
        biases = [a["L1_attn_bu"][0:P], a["L1_attn_bu"][P:EH], a["L1_attn_bv"][0:P], a["L1_attn_bv"][P:EH], a["L1_attn_bb"]]
        small += [(c["uvb_bias"][:, e:e + 1], column(v)) for e, v in enumerate(biases)]
        small += [(c["qk_cols"][:, n:n + 1], column(a[f"L1_attn_{v}"])) for n, v in enumerate(("qqw", "qkw", "qqb", "qkb"))]
        mine_small = [(aln_s[:, :], column(a["L0_attn_ln_scale"])), (aln_b[:, :], column(a["L0_attn_ln_bias"])),
                      (wout[:, :, :], a["L0_attn_Wout"].rearrange("(h p) d -> p h d", p=P))]
        for half in range(2):
            rows = slice(half * DH, (half + 1) * DH)
            mine_small += [(qk_s[rows, 0:1], column(a["L0_attn_qn_scale"])), (qk_s[rows, 1:2], column(a["L0_attn_kn_scale"])),
                           (qk_o[rows, 0:1], column(a["L0_attn_qn_bias"])), (qk_o[rows, 1:2], column(a["L0_attn_kn_bias"]))]
        N_RAW, N_SMALL = 7, len(mine_small) + len(small)

        scores = [psum[:, SEQ * i:SEQ * (i + 1)] for i in range(2)]
        key_scores = [psum[:, 2 * SEQ + 512 * i:2 * SEQ + 512 * (i + 1)] for i in range(2)]
        outp = [psum[:, 3 * SEQ + 512 * i:3 * SEQ + 512 * (i + 1)] for i in range(2)]
        qkv = psum[:, 0:QKV]
        qnt = psum[:, QKV:QKV + NORMED * P]

        def exists(beta, part, back):
            return {"first": beta >= back, "mid": True, "last": beta < back}[part]

        block = own.enter_context(nc.Block())

        @block.sync
        def _(sp):
            sp.dma_start(x[:, 0], xv[0]).then_inc(x_in[0], 16)
            sp.dma_start(wqkv[:, 0:INNER], a["L0_attn_Wq"]).then_inc(w_in, 16)
            sp.dma_start(wqkv[:, INNER:QKV], a["L0_attn_Wkv"]).then_inc(w_in, 16)
            sp.dma_start(x[:, 1], xv[1]).then_inc(x_in[1], 16)
            for dst, src in mine_small + small:
                sp.dma_start(dst, src).then_inc(c_in, 16)
            with sp.Fori(0, BATCH) as b:
                def load_q(i, beta, wait=True):
                    n = BODY * i + beta
                    to = beta % BODY
                    if wait:
                        sp.wait_ge(key_scored, (b * BLOCKS + n - BODY + 1) * TILES)
                    queries = qx[:, :, :, :, :].rearrange("p h b u q -> p (h b u q)")
                    sp.dma_start(qs[to][:, :, :].rearrange("p u q -> p (u q)").bitcast(F32),
                                 queries[:, bass.ds(n * UNITS * P, UNITS * P)].bitcast(F32)).then_inc(q_in[to], 16)
                    sp.dma_start(qm[to][0:DH, :, :].rearrange("p u q -> p (u q)").bitcast(F32),
                                 queries[0:DH, bass.ds(n * UNITS * P, UNITS * P)].bitcast(F32)).then_inc(q_in[to], 16)

                def load_k(i, quarter, wait=True):
                    if wait:
                        sp.wait_ge(key_scored, (b * BLOCKS + BODY * i - 1) * TILES + 2 * quarter + 2)
                    at = slice(quarter * QB, (quarter + 1) * QB)
                    sp.dma_start(kg[:, at].bitcast(F32), kh[:, :, at].bitcast(F32)[:, bass.ds(i // 2, 1), :].rearrange("p g k -> p (g k)")).then_inc(k_in[quarter], 16)
                    sp.dma_start(kgl[0:KR, at].bitcast(F32), kl[0:KR, :, at].bitcast(F32)[:, bass.ds(i // 2, 1), :].rearrange("p g k -> p (g k)")).then_inc(k_in[quarter], 16)

                def load_v(i, quarter, wait=True):
                    if wait:
                        sp.wait_ge(pv_made, (b * BLOCKS + BODY * i - 1) * TILES + 2 * quarter + 2)
                    at = slice(2 * quarter, 2 * quarter + 2)
                    sp.dma_start(vg[:, at, :], vb[:, i // 2, at, :]).then_inc(v_in[quarter], 16)

                def body(i, last):
                    load_q(i, 2)
                    for quarter in range(4):
                        load_k(i, quarter)
                        if quarter:
                            load_v(i, quarter - 1)
                    load_q(i, 3)
                    load_v(i, 3)
                    if not last:
                        load_q(i, 4)
                        load_q(i, 5)

                sp.wait_ge(high_made, TILES * (b + 1))
                sp.wait_ge(low_made, TILES * (b + 1))
                sp.wait_ge(v_made, TILES * (b + 1))
                load_q(0, 0, wait=False)
                for quarter in range(4):
                    load_k(0, quarter, wait=False)
                load_q(0, 1, wait=False)
                for quarter in range(4):
                    load_v(0, quarter, wait=False)
                load_q(0, 2, wait=False)
                load_q(0, 3, wait=False)
                load_q(0, 4)
                load_q(0, 5)
                with sp.Fori(1, BODIES - 1) as i:
                    body(i, last=False)
                body(BODIES - 1, last=True)

        @block.gpsimd
        def _(pool):
            pool.memset(ident[:, :], 0.0).then_inc(pool_step, 1)
            pool.memset(c["ones_square"][:, :], 1.0).then_inc(pool_step, 1)
            pool.wait_ge(pool_step, 1)
            pool.affine_select(out=ident[:, :], in_=ident[:, :], compare_op=ALU.not_equal, fill=1.0, base=0,
                               pattern=[[-1, P]], channel_multiplier=1).then_inc(ident_made, 1)
            with pool.Fori(0, BATCH) as b:
                def high(j):
                    at = slice((j % 2) * P, (j % 2) * P + P)
                    pool.wait_ge(t1_made, TILES * b + j + 1)
                    pool.sem_inc(pool_step, 1)
                    pool.tensor_scalar(kh[:, :, j * P:(j + 1) * P], t1[j % 2][:, HEADS:, :], 1.0, 0.0, ALU.mult, ALU.add)
                    for h in range(2):
                        last = pool.tensor_scalar(qx[:, :, j // 2, h, at],
                                                  t1[j % 2][:, 0:HEADS, :].rearrange("p (g h) q -> p g h q", h=2)[:, :, h, :],
                                                  1.0, 0.0, ALU.mult, ALU.add)
                    last.then_inc(high_made, 1)

                for j in range(TILES):
                    pool.wait_ge(qn_made, TILES * b + j + 1)
                    pool.sem_inc(pool_step, 1)
                    pool.tensor_scalar(qn[:, :, 1, :], qn[:, :, 0, :], 1.0, 0.0, ALU.mult, ALU.add).then_inc(twin_made, 1)
                    if j:
                        high(j - 1)
                high(TILES - 1)

                def slot(i, beta, part):
                    if not exists(beta, part, 1):
                        return
                    m = b * BLOCKS + BODY * i + beta - 1
                    par = (beta - 1) % 2
                    for kt in range(1, TILES):
                        pool.wait_ge(exp_made, m * TILES + kt + 1)
                        if kt == 1:
                            if exists(beta, part, 3):
                                pool.wait_ge(sums_made, m - 1)
                        else:
                            pool.wait_ge(pool_added, m * (TILES - 1) + kt - 1)
                        pool.tensor_tensor(acc[par], pt[par][:, 0, :] if kt == 1 else acc[par], pt[par][:, kt, :], ALU.add)\
                            .then_inc(pool_added, 1)

                for beta in range(BODY):
                    slot(0, beta, "first")
                with pool.Fori(1, BODIES) as i:
                    for beta in range(BODY):
                        slot(i, beta, "mid")
                slot(BODIES, 0, "last")

        @block.tensor
        def _(pe):
            pe.wait_ge(ident_made, 1)
            pe.wait_ge(r_in, 16 * N_RAW)
            pe.wait_ge(w_float, 1)
            for t in range(W_TILES):
                last = pe.transpose(psum[:, 2 * SEQ + t * P:2 * SEQ + (t + 1) * P], raw[:, t * P:(t + 1) * P], ident[:, :])
            last.then_inc(w_turned, 1)
            pe.wait_ge(w_kept, 1)
            pe.wait_ge(w_centred, 1)
            for b in range(BATCH):
                pe.wait_ge(xn_made, b + 1)
                for j in range(TILES):
                    last = pe.transpose(psum[:, b * SEQ + j * P:b * SEQ + (j + 1) * P], cen[b][:, j, :], ident[:, :])
                last.then_inc(xn_turned, 1)
            pe.wait_ge(keep_made, 1)
            with pe.Fori(0, BATCH) as b:
                def project(j):
                    if j:
                        pe.wait_ge(raw_made, TILES * b + j)
                        pe.wait_ge(v_made, TILES * b + j)
                    for n in range(QKV // 512):
                        last = pe.matmul(qkv[:, n * 512:(n + 1) * 512], xnt[:, j * P:(j + 1) * P],
                                         wqkv[:, n * 512:(n + 1) * 512], start=True, stop=True)
                    last.then_inc(qkv_made, 1)

                pe.wait_ge(xnt_made, b + 1)
                pe.wait_ge(x_added, FIRST + b * BLOCKS)
                project(0)
                for j in range(TILES):
                    if j < TILES - 1:
                        project(j + 1)
                    pe.wait_ge(qn_made, TILES * b + j + 1)
                    pe.wait_ge(twin_made, TILES * b + j + 1)
                    if j:
                        pe.wait_ge(t1_made, TILES * b + j)
                    for h in range(NORMED):
                        last = pe.transpose(qnt[:, h * P:(h + 1) * P],
                                            qn[:, h, :, :].rearrange("p t d -> p (t d)"), ident[:, :])
                    last.then_inc(qn_turned, 1)

                pe.wait_ge(t1_made, TILES * b + TILES)
                pe.wait_ge(high_made, TILES * b + TILES)
                pe.wait_ge(low_made, TILES * b + TILES)

                def slot(i, beta, part):
                    n = b * BLOCKS + BODY * i + beta
                    g = i // 2
                    for sub in range(TILES):
                        if part != "last" and sub < UNITS:
                            if sub == 0:
                                pe.wait_ge(q_in[beta], 32 * (b * BODIES + i + 1))
                                if not (part == "first" and beta == 0):
                                    pe.wait_ge(max_placed, n)
                            if not (part == "first" and beta == 0 and sub < 2):
                                pe.wait_ge(max_made, n * UNITS + sub - 1)
                            for half in range(2):
                                cols = slice(half * 512, half * 512 + 512)
                                last = pe.matmul(scores[sub % 2][:, cols], qs[beta][:, sub, :], kh[:, g, cols], start=True, stop=True)
                            last.then_inc(scored, 1)
                        if exists(beta, part, 1):
                            m, to = n - 1, (beta - 1) % BODY
                            if sub == 0:
                                pe.wait_ge(max_placed, m + 1)
                            if sub % 2 == 0:
                                pe.wait_ge(k_in[sub // 2], 32 * (b * BODIES + (i if beta else i - 1) + 1))
                            if not (part == "first" and beta == 1 and sub < 2):
                                pe.wait_ge(exp_made, m * TILES + sub - 1)
                            keys = slice(sub * P, (sub + 1) * P)
                            pe.matmul(key_scores[sub % 2], kg[:, keys], qs[to][:, :, :].rearrange("p u q -> p (u q)"), start=True, stop=False)
                            pe.matmul(key_scores[sub % 2], kgl[0:KR, keys], qm[to][0:KR, :, :].rearrange("p u q -> p (u q)"),
                                      start=False, stop=True).then_inc(key_scored, 1)
                        back, kt = (2, TILES - 2 + sub) if sub < 2 else (1, sub - 2)
                        if exists(beta, part, back):
                            m, par = n - back, (beta - back) % 2
                            if not exists(beta, part, 1) or (part == "first" and beta == 1):
                                pe.wait_ge(exp_made, m * TILES + kt + 1)
                            if kt % 2 == 0:
                                pe.wait_ge(v_in[kt // 2], 16 * (b * BODIES + (i if beta >= back else i - 1) + 1))
                            if kt == 0 and exists(beta, part, 3):
                                pe.wait_ge(x_added, FIRST + m - 1)
                            for h in range(2):
                                last = pe.matmul(outp[par][h * DH:(h + 1) * DH, 0:QB], vg[:, kt, :], pt[par][:, kt, h * QB:(h + 1) * QB],
                                                 start=(kt == 0), stop=(kt == TILES - 1))
                            last.then_inc(pv_made, 1)
                        if sub == 3 and exists(beta, part, 2):
                            m, par = n - 2, (beta - 2) % 2
                            pe.wait_ge(pool_added, (m + 1) * (TILES - 1))
                            for h in range(2):
                                last = pe.matmul(outp[par][h * DH:(h + 1) * DH, QB:2 * QB], c["ones_square"][:, 0:DH],
                                                 acc[par][:, h * QB:(h + 1) * QB], start=True, stop=True)
                            last.then_inc(sums_made, 1)
                        if sub == 5 and part != "last":
                            pe.wait_ge(max_made, (n + 1) * UNITS)
                            pe.matmul(scores[0][DH:KR, 0:P], nmx[:, :], ident[:, :], start=True, stop=True).then_inc(max_turned, 1)
                        if sub == TILES - 1 and exists(beta, part, 2):
                            m, par = n - 2, (beta - 2) % 2
                            pe.wait_ge(ot_made, m + 1)
                            for t in range(2):
                                last = pe.matmul(outp[par][:, QB + t * P:QB + (t + 1) * P], ot[par][:, t * P:(t + 1) * P],
                                                 wout[:, (i if beta >= 2 else i - 1), :], start=True, stop=True)
                            last.then_inc(y_made, 1)

                for beta in range(BODY):
                    slot(0, beta, "first")
                with pe.Fori(1, BODIES) as i:
                    for beta in range(BODY):
                        slot(i, beta, "mid")
                for beta in range(2):
                    slot(BODIES, beta, "last")

        @block.scalar
        def _(act):
            act.dma_start(raw[:, 0:2 * P].rearrange("p (t d) -> p t d", t=2), a["L1_attn_Wu"].rearrange("(t p) d -> p t d", p=P)).then_inc(r_in, 16)
            act.dma_start(raw[:, 2 * P:4 * P].rearrange("p (t d) -> p t d", t=2), a["L1_attn_Wv"].rearrange("(t p) d -> p t d", p=P)).then_inc(r_in, 16)
            act.dma_start(raw[:, 4 * P:5 * P], a["L1_attn_Wb"]).then_inc(r_in, 16)
            act.dma_start(raw[:, W_O * P:W_GATE * P], a["L1_attn_Wo"]).then_inc(r_in, 16)
            act.dma_start(rawi[:, 0:HID1].rearrange("p (t d) -> p t d", t=HT), a["L1_ffn_w_gate"].rearrange("(t p) d -> p t d", p=P)).then_inc(r_in, 16)
            act.dma_start(rawi[:, HID1:2 * HID1].rearrange("p (t d) -> p t d", t=HT), a["L1_ffn_w_up"].rearrange("(t p) d -> p t d", p=P)).then_inc(r_in, 16)
            act.dma_start(rawi[:, 2 * HID1:3 * HID1], a["L1_ffn_w_down"]).then_inc(r_in, 16)
            act.wait_ge(w_turned, 1)
            act.activation(wt[:, 0:SEQ], psum[:, 2 * SEQ:3 * SEQ], ACT.Copy)
            act.activation(wt[:, SEQ:2 * SEQ], psum[:, 3 * SEQ:4 * SEQ], ACT.Copy).then_inc(w_kept, 1)
            act.wait_ge(c_in, 16 * N_SMALL)
            for b in range(BATCH):
                act.wait_ge(cen_made, b + 1)
                act.activation(sq[b], cen[b].rearrange("p j d -> p (j d)"), ACT.Square).then_inc(sq_made, 1)
            for b in range(BATCH):
                act.wait_ge(var_made, b + 1)
                act.activation(st[:, b, 2, :], st[:, b, 1, :], ACT.Sqrt).then_inc(root_made, 1)
            for b in range(BATCH):
                act.wait_ge(xn_turned, b + 1)
                act.activation((xnt, xkeep)[b], psum[:, b * SEQ:(b + 1) * SEQ], ACT.Identity, bias=aln_b[:, 0:1], scale=aln_s[:, 0:1])\
                   .then_inc((xnt_made, keep_made)[b], 1)
            with act.Fori(0, BATCH) as b:
                def scale(j):
                    act.wait_ge(qn_turned, TILES * b + j + 1)
                    if j >= 2:
                        act.wait_ge(high_made, TILES * b + j - 1)
                        act.wait_ge(low_made, TILES * b + j - 1)
                    act.activation(t1[j % 2][:, 0:HEADS, :].rearrange("p h q -> p (h q)"), qnt[:, 0:HEADS * P], ACT.Identity,
                                   bias=qk_o[:, 0:1], scale=qk_s[:, 0:1])
                    act.activation(t1[j % 2][:, HEADS:, :].rearrange("p h q -> p (h q)"), qnt[:, HEADS * P:], ACT.Identity,
                                   bias=qk_o[:, 1:2], scale=qk_s[:, 1:2]).then_inc(t1_made, 1)

                for j in range(TILES):
                    act.wait_ge(qkv_made, TILES * b + j + 1)
                    if j:
                        act.wait_ge(hvar_made, TILES * b + j)
                    act.activation(hsq, qkv[:, 0:NORMED * DH], ACT.Square).then_inc(hsq_made, 1)
                    act.activation(vb[:, :, j, :], qkv[:, NORMED * DH:QKV].rearrange("p (g d) -> p g d", d=DH), ACT.Copy).then_inc(v_made, 1)
                    if j:
                        act.wait_ge(qn_made, TILES * b + j)
                    act.activation(qk_raw, qkv[:, 0:NORMED * DH], ACT.Copy).then_inc(raw_made, 1)
                    act.wait_ge(hvar_made, TILES * b + j + 1)
                    act.activation(hst[:, 2, :], hst[:, 1, :], ACT.Sqrt).then_inc(hroot_made, 1)
                    if j:
                        scale(j - 1)
                scale(TILES - 1)

                def slot(i, beta, part):
                    if not exists(beta, part, 1):
                        return
                    m = b * BLOCKS + BODY * i + beta - 1
                    par = (beta - 1) % 2
                    for kt in range(TILES):
                        act.wait_ge(key_scored, m * TILES + kt + 1)
                        if exists(beta, part, 3):
                            if kt == 0:
                                act.wait_ge(pool_added, (m - 1) * (TILES - 1))
                            act.wait_ge(pv_made, (m - 2) * TILES + kt + 1)
                        act.activation(pt[par][:, kt, :], key_scores[kt % 2], ACT.Exp).then_inc(exp_made, 1)

                for beta in range(BODY):
                    slot(0, beta, "first")
                with act.Fori(1, BODIES) as i:
                    for beta in range(BODY):
                        slot(i, beta, "mid")
                slot(BODIES, 0, "last")

        @block.vector
        def _(dve):
            dve.memset(kl[DH:KR, :, :].bitcast(F32), 1.0)
            dve.wait_ge(r_in, 16 * N_RAW)
            dve.tensor_scalar(raw[:, W_GATE * P:], rawi[:, :], SCALE1, None, ALU.mult).then_inc(w_float, 1)
            dve.wait_ge(w_in, 32)
            heads = wqkv[:, 0:NORMED * DH].rearrange("p (h d) -> p h d", d=DH)
            dve.tensor_reduce(wmean[:, :], heads, AX_X, ALU.add).then_inc(dve_step, 1)
            dve.wait_ge(dve_step, 1)
            dve.tensor_scalar(wmean[:, :], wmean[:, :], 1.0 / DH, None, ALU.mult).then_inc(dve_step, 1)
            dve.wait_ge(dve_step, 2)
            dve.tensor_tensor(heads, heads, over_last(wmean[:, :], DH), ALU.subtract).then_inc(w_centred, 1)
            dve.wait_ge(c_in, 16 * N_SMALL)
            dve.tensor_scalar(qk_s[:, 0:1], qk_s[:, 0:1], DH ** -0.5, None, ALU.mult).then_inc(dve_step, 1)
            dve.tensor_scalar(qk_o[:, 0:1], qk_o[:, 0:1], DH ** -0.5, None, ALU.mult).then_inc(dve_step, 1)
            dve.wait_ge(x_in[0], 16)
            dve.wait_ge(x_in[1], 16)
            dve.sem_inc(x_added, FIRST)
            steps = 4
            for b in range(BATCH):
                xb = x[:, b, :, :]
                dve.tensor_reduce(st[:, b, 0, :], xb, AX_X, ALU.add).then_inc(dve_step, 1)
                dve.wait_ge(dve_step, steps + 1)
                dve.tensor_scalar(st[:, b, 0, :], st[:, b, 0, :], 1.0 / DIM, None, ALU.mult).then_inc(dve_step, 1)
                dve.wait_ge(dve_step, steps + 2)
                dve.tensor_tensor(cen[b], xb, over_last(st[:, b, 0, :], DIM), ALU.subtract).then_inc(cen_made, 1)
                steps += 2
            for b in range(BATCH):
                dve.wait_ge(sq_made, b + 1)
                dve.tensor_reduce(st[:, b, 1, :], sq[b].rearrange("p (j d) -> p j d", d=DIM), AX_X, ALU.add).then_inc(dve_step, 1)
                steps += 1
                dve.wait_ge(dve_step, steps)
                dve.tensor_scalar(st[:, b, 1, :], st[:, b, 1, :], (1.0 + ATT_EPS) / DIM, ATT_EPS * LN_EPS, ALU.mult, ALU.add).then_inc(var_made, 1)
            for b in range(BATCH):
                dve.wait_ge(root_made, b + 1)
                dve.reciprocal(st[:, b, 3, :], st[:, b, 2, :]).then_inc(dve_step, 1)
                steps += 1
                dve.wait_ge(dve_step, steps)
                dve.tensor_tensor(cen[b], cen[b], over_last(st[:, b, 3, :], DIM), ALU.mult).then_inc(xn_made, 1)
            dve.wait_ge(keep_made, 1)
            with dve.Fori(0, BATCH) as b:
                def low(j):
                    at = slice((j % 2) * P, (j % 2) * P + P)
                    dve.wait_ge(high_made, TILES * b + j + 1)
                    for h in range(2):
                        part = qx[DH:P, :, j // 2, h, at]
                        dve.tensor_tensor(part, t1[j % 2][DH:P, 0:HEADS, :].rearrange("p (g h) q -> p g h q", h=2)[:, :, h, :],
                                          part.bitcast(F32), ALU.subtract)
                    dve.tensor_tensor(kl[0:DH, :, j * P:(j + 1) * P], t1[j % 2][0:DH, HEADS:, :], kh[0:DH, :, j * P:(j + 1) * P].bitcast(F32),
                                      ALU.subtract).then_inc(low_made, 1)

                for j in range(TILES):
                    n = TILES * b + j
                    dve.wait_ge(hsq_made, n + 1)
                    dve.tensor_reduce(hst[:, 0, :], hsq.rearrange("p (h d) -> p h d", d=DH), AX_X, ALU.add)\
                       .then_inc(hsum, 1)
                    dve.wait_ge(hsum, 2 * n + 1)
                    dve.tensor_scalar(hst[:, 1, :], hst[:, 0, :], 1.0 / DH, ATT_EPS, ALU.mult, ALU.add).then_inc(hvar_made, 1)
                    dve.wait_ge(hroot_made, n + 1)
                    dve.reciprocal(hst[:, 3, :], hst[:, 2, :]).then_inc(hsum, 1)
                    dve.wait_ge(hsum, 2 * n + 2)
                    if j:
                        dve.wait_ge(qn_turned, n)
                    dve.wait_ge(raw_made, n + 1)
                    dve.tensor_tensor(qn[:, :, 0, :], qk_raw.rearrange("p (h d) -> p h d", d=DH),
                                      over_last(hst[:, 3, :], DH), ALU.mult).then_inc(qn_made, 1)
                    if j >= 2:
                        low(j - 2)
                low(TILES - 2)
                low(TILES - 1)

                def slot(i, beta, part):
                    n = b * BLOCKS + BODY * i + beta

                    def add(m, par):
                        dve.wait_ge(y_made, m + 1)
                        dve.wait_ge(x_added, FIRST + m)
                        c_at = (beta - 3) % BODY
                        at = x[:, b, 2 * c_at:2 * c_at + 2, :]
                        dve.tensor_tensor(at, at, outp[par][:, QB:2 * QB].rearrange("p (t d) -> p t d", d=DIM), ALU.add)\
                           .then_inc(x_added, 1)

                    if part != "last":
                        for u in range(UNITS):
                            dve.wait_ge(scored, n * UNITS + u + 1)
                            if u == 0 and not (part == "first" and beta == 0):
                                dve.wait_ge(max_turned, n)
                            dve.tensor_reduce(nmx[:, u:u + 1], scores[u % 2], AX_X, ALU.max, negate=True).then_inc(max_made, 1)
                            if u == 0 and exists(beta, part, 3):
                                add(n - 3, (beta - 3) % 2)
                    elif exists(beta, part, 3):
                        add(n - 3, (beta - 3) % 2)
                    if exists(beta, part, 2):
                        m, par = n - 2, (beta - 2) % 2
                        dve.wait_ge(sums_made, m + 1)
                        dve.reciprocal(rinv, outp[par][:, QB:2 * QB]).then_inc(rinv_made, 1)
                    if exists(beta, part, 2):
                        m, par = n - 2, (beta - 2) % 2
                        dve.wait_ge(rinv_made, m + 1)
                        dve.wait_ge(pv_made, (m + 1) * TILES)
                        if exists(beta, part, 4):
                            dve.wait_ge(y_made, m - 1)
                        dve.tensor_tensor(ot[par], outp[par][:, 0:QB], rinv, ALU.mult).then_inc(ot_made, 1)
                    if part != "last":
                        dve.wait_ge(max_turned, n + 1)
                        dve.tensor_tensor(qm[beta][DH:KR, :, :], over_mid(scores[0][DH:KR, 0:P], UNITS),
                                          over_last(ident[DH:KR, DH:KR], P), ALU.mult).then_inc(max_placed, 1)

                for beta in range(BODY):
                    slot(0, beta, "first")
                with dve.Fori(1, BODIES) as i:
                    for beta in range(BODY):
                        slot(i, beta, "mid")
                for beta in range(3):
                    slot(BODIES, beta, "last")
                dve.wait_ge(x_added, FIRST + (b + 1) * BLOCKS)
                dve.tensor_copy(xnt, xkeep).then_inc(xnt_made, 1)


def rest(nc, a, x, ident, wt, psum, sb, sem, out, c, turn):
    gamma, beta, bo, ones, br, wr = c["gamma"], c["beta"], c["bo"], c["ones_square"], c["br"], c["wr"]
    with ExitStack() as own:
        def mine(name, shape, dt=F32):
            return sb(name, shape, dt, own)

        stats = mine("stats", [P, LNS, T, 6])
        mv = mine("mv", [P, LNS, T, 2])
        inv = mine("inv", [P, LNS, 2, T])
        half_power = mine("half_power", [P, 2 * T])
        y0 = mine("y0", [P, CHUNKS, T, DIM])
        yb = mine("yb", [P, T, DIM])
        xb = mine("xb", [P, CHUNKS, T, DIM])
        turned = mine("turned_rows", [P, CHUNKS, CW])
        ysum = mine("ysum", [P, CHUNKS])
        turn_q = mine("turn_q", [P, S])
        router = mine("router", [1, BATCH, 8, EXPERTS])
        chosen = mine("chosen", [1, BATCH, EXPERTS], U32)
        wv = mine("wv", [1, BATCH, 4])
        wb = mine("wb", [P, BATCH, TOP])
        w1s = mine("w1s", [P, BATCH, TOP, HID])
        w2s = mine("w2s", [P, BATCH, TOP, FT, DIM])
        b1s = mine("b1s", [P, BATCH, TOP, FT])
        b2s = mine("b2s", [1, BATCH, TOP, DIM])
        b2w = mine("b2w", [1, BATCH, 2, DIM])
        hid = [mine(f"hid{i}", [P, TOP * FT, CW]) for i in range(2)]
        uvb = mine("uvb", [P, CHUNKS, UVB // P, CW])
        heads = mine("heads", [P, BATCH, 2, CW])
        prod = mine("prod", [P, 3, CW])
        kern = mine("kern", [P, 3, CW])
        vu = mine("vu", [P, 3, 2, CW])
        mix = mine("mix", [P, BATCH, 2, CW])
        gate = [hid[i][:, 0:HT, :] for i in range(2)]
        hid1 = [hid[i][:, HT:2 * HT, :] for i in range(2)]

        step = sem("step")
        pool_step = sem("pool_step2")
        var_made = sem("var2_made")
        inv_made = sem("inv_made")
        rows_made = sem("rows_made")
        rows_turned = sem("rows_turned")
        rows_kept = sem("rows_kept")
        logits_made = sem("logits_made")
        shifted = sem("shifted")
        exp_made = sem("exp2_made")
        chosen_made = sem("chosen_made")
        wv_made = sem("wv_made")
        wb_spread = sem("wb_spread")
        exp_w = sem("exp_w")
        experts_in = [sem(f"experts_in{b}") for b in range(BATCH)]
        w2_scaled = sem("w2_scaled")
        hid_made = sem("hid_made")
        gelu_made = sem("gelu_made")
        beta_added = sem("beta_added")
        ffn_made = sem("ffn_made")
        new_x = sem("new_x")
        short_made = sem("short_made")
        token_out = sem("token_out")
        uvb_made = sem("uvb_made")
        silu_made = sem("silu_made")
        heads_made = sem("heads_made")
        turned_q = sem("turned_q")
        prod_made = sem("prod_made")
        dots_made = sem("dots_made")
        relu_made = sem("relu_made")
        vu_made = sem("vu_made")
        mix_made = sem("mix_made")
        gau_made = sem("gau_made")
        pair_made = sem("pair_made")
        gate_made = sem("gate_made")
        up_taken = sem("up_taken")
        down_made = sem("down_made")
        x_final = sem("x_final")
        turn_in = sem("turn_in")
        stored = sem("stored")

        EXPERT_DMAS = 4 * TOP
        UP = TOP * FT
        IN = UVB // P

        def batch_half(ch):
            return ch // 2, ch % 2

        def xc(ch):
            b, h = batch_half(ch)
            return x[:, b, T * h:T * (h + 1), :]

        def wide(m):
            return psum[:, (m % 4) * CW:(m % 4 + 1) * CW]

        def by_token(m):
            return psum[:, (4 + m % 2) * CW:(5 + m % 2) * CW]

        def other(m):
            return psum[:, (6 + m % 2) * CW:(7 + m % 2) * CW]

        FIRST_IN = CHUNKS * UP
        FIRST_PAIR = FIRST_IN + CHUNKS * IN

        def wait_wide(pe, m):
            m -= 4
            if m < 0:
                return
            if m < FIRST_IN:
                pe.wait_ge(gelu_made, m + 1)
            elif m < FIRST_PAIR:
                pe.wait_ge(silu_made, m - FIRST_IN + 1)
            else:
                pe.wait_ge(up_taken, (m - FIRST_PAIR) // 2 + 1)

        def wait_by_token(pe, m):
            if m >= 2:
                pe.wait_ge(token_out, m - 1)

        OTHER = ([("rows", n) for n in range(8)]
                 + [(kind, 4 * h + n) for h in range(2) for n, kind in enumerate(("turned_q", "dots", "dots", "dots"))]
                 + [("rows", n) for n in range(8, 12)])

        def wait_other(pe, m):
            if m < 2:
                return
            kind, n = OTHER[m - 2]
            if kind == "rows":
                pe.wait_ge(rows_kept, n + 1)
            elif kind == "turned_q":
                pe.wait_ge(prod_made, 3 * (n // 4) + 3)
            else:
                pe.wait_ge(relu_made, 3 * (n // 4) + n % 4)

        block = own.enter_context(nc.Block())

        @block.sync
        def _(sp):
            sp.dma_start(turn_q[:, :], turn).then_inc(turn_in, 16)
            for b in range(BATCH):
                sp.wait_ge(chosen_made, b + 1)
                for k in range(TOP):
                    e = sp.value_load(chosen[0:1, b, k:k + 1], min_val=0, max_val=EXPERTS - 1)
                    sp.dma_start(w1s[:, b, k, :], a["L0_ffn_W1"][bass.ds(e, 1), :, :].rearrange("e d f -> d (e f)")).then_inc(experts_in[b], 16)
                    sp.dma_start(w2s[:, b, k, :, :], a["L0_ffn_W2"][bass.ds(e, 1), :, :].rearrange("e (t f) d -> f (e t) d", f=P)).then_inc(experts_in[b], 16)
                    sp.dma_start(b1s[:, b, k, :], a["L0_ffn_b1"][bass.ds(e, 1), :].rearrange("e (t f) -> f (e t)", f=P), allow_slow_non_contiguous=True).then_inc(experts_in[b], 16)
                    sp.dma_start(b2s[:, b, k, :], a["L0_ffn_b2"][bass.ds(e, 1), :]).then_inc(experts_in[b], 16)
            for n, ch in enumerate(PAIRED):
                b, h = batch_half(ch)
                sp.wait_ge(x_final, n + 1)
                sp.dma_start(out[b].rearrange("(p j) d -> p j d", j=TILES)[:, T * h:T * (h + 1), :], xc(ch)).then_inc(stored, 16)
            sp.wait_ge(stored, 16 * CHUNKS)

        @block.gpsimd
        def _(pool):
            pool.memset(half_power[:, :], -0.5).then_inc(pool_step, 1)
            pool.wait_ge(pool_step, 1)

            roots = [0]

            def root(k):
                roots[0] += 1
                pool.wait_ge(var_made, roots[0])
                flat = inv[:, k, :, :].rearrange("p s t -> p (s t)")
                pool.tensor_tensor(flat, flat, half_power[:, :], ALU.pow).then_inc(inv_made, 1)

            def shortcut(ch):
                b, h = batch_half(ch)
                k = 2 * CHUNKS + ch
                pool.wait_ge(rows_made, CHUNKS + ch + 1)
                for t in range(T):
                    last = pool.tensor_scalar(yb[:, t, :], xc(ch)[:, t, :], mv[:, k, t, 0:1], inv[:, k, 0, t:t + 1], ALU.subtract, ALU.mult)
                last.then_inc(pool_step, 1)
                pool.tensor_tensor(xb[:, ch, :, :], xc(ch), over_mid(bo[:, :], T), ALU.add).then_inc(pool_step, 1)
                pool.wait_ge(pool_step, 1 + 2 * (ch + 1))
                pool.tensor_tensor(xb[:, ch, :, :], xb[:, ch, :, :], yb[:, :, :], ALU.add).then_inc(short_made, 1)

            def products(h):
                pool.wait_ge(silu_made, (3 + h) * IN)
                if h:
                    pool.wait_ge(mix_made, 1)
                for n, (l, m) in enumerate(((0, 0), (1, 0), (1, 1))):
                    last = pool.tensor_tensor(vu[:, n, :, :], uvb[:, 2 * m + h, 2:4, :], uvb[:, 2 * l + h, 0:2, :], ALU.mult)
                last.then_inc(vu_made, 1)

            for k in range(CHUNKS):
                root(k)
            for ch in range(CHUNKS):
                pool.tensor_tensor(xb[:, ch, :, :], xc(ch), over_mid(beta[:, :], T), ALU.add).then_inc(beta_added, 1)
            for ch in range(CHUNKS):
                root(CHUNKS + ch)
                root(2 * CHUNKS + ch)
                shortcut(ch)
            products(0)
            root(3 * CHUNKS)
            root(3 * CHUNKS + 1)
            products(1)
            root(3 * CHUNKS + 2)
            root(3 * CHUNKS + 3)

        @block.tensor
        def _(pe):
            others = [0]

            def next_other():
                wait_other(pe, others[0])
                others[0] += 1
                return other(others[0] - 1)

            def turn(n, ch):
                pe.wait_ge(rows_made, n + 1)
                at = next_other()
                for t in range(T):
                    last = pe.transpose(at[:, t * P:(t + 1) * P], y0[:, ch, t, :], ident[:, :])
                last.then_inc(rows_turned, 1)

            def ffn_up(ch):
                b = ch // 2
                if ch % 2 == 0:
                    pe.wait_ge(experts_in[b], 16 * EXPERT_DMAS)
                for n in range(UP):
                    m = ch * UP + n
                    wait_wide(pe, m)
                    pe.matmul(wide(m), w1s[:, b, n // FT, (n % FT) * P:(n % FT + 1) * P], turned[:, ch, :],
                              start=True, stop=True).then_inc(hid_made, 1)

            def ffn_down(ch):
                b = ch // 2
                pe.wait_ge(gelu_made, (ch + 1) * UP)
                pe.wait_ge(w2_scaled, b + 1)
                wait_by_token(pe, ch)
                for t in range(T):
                    o = by_token(ch)[:, t * P:(t + 1) * P]
                    pe.matmul(o, ones[0:1, :], b2w[:, b, 1, :], start=True, stop=False)
                    for n in range(UP):
                        last = pe.matmul(o, hid[ch % 2][:, n, t * P:(t + 1) * P], w2s[:, b, n // FT, n % FT, :],
                                         start=False, stop=(n == UP - 1))
                last.then_inc(ffn_made, 1)

            def gau_in(n, ch):
                pe.wait_ge(rows_kept, CHUNKS + n + 1)
                for e in range(IN):
                    m = FIRST_IN + n * IN + e
                    wait_wide(pe, m)
                    pe.matmul(wide(m), wt[:, e * P:(e + 1) * P], turned[:, ch, :], start=True, stop=True).then_inc(uvb_made, 1)

            def gau_dots(h):
                pe.wait_ge(heads_made, h + 1)
                pe.wait_ge(turn_in, 16)
                pe.matmul(next_other(), turn_q[:, :], heads[:, 1, 0, :], start=True, stop=True).then_inc(turned_q, 1)
                for n in (0, 2, 1):
                    pe.wait_ge(prod_made, 3 * h + {0: 1, 2: 2, 1: 3}[n])
                    pe.matmul(next_other(), c["ones_square"][:, :], prod[:, n, :], start=True, stop=True).then_inc(dots_made, 1)

            def gau_out(h):
                for l in range(BATCH):
                    wait_by_token(pe, CHUNKS + 2 * h + l)
                    pe.wait_ge(mix_made, h + 1)
                    for t in range(T):
                        for e in range(2):
                            last = pe.matmul(by_token(CHUNKS + 2 * h + l)[:, t * P:(t + 1) * P], mix[:, l, e, t * P:(t + 1) * P],
                                             wt[:, (W_O + e) * P:(W_O + e + 1) * P], start=(e == 0), stop=(e == 1))
                    last.then_inc(gau_made, 1)

            def gate_up(n):
                pe.wait_ge(rows_kept, 2 * CHUNKS + n + 1)
                for k in range(HT):
                    for s, w in enumerate((W_GATE, W_UP)):
                        m = FIRST_PAIR + 2 * (n * HT + k) + s
                        wait_wide(pe, m)
                        last = pe.matmul(wide(m), wt[:, (w + k) * P:(w + k + 1) * P], turned[:, PAIRED[n], :], start=True, stop=True)
                    last.then_inc(pair_made, 1)

            def down(n):
                pe.wait_ge(up_taken, (n + 1) * HT)
                if n < 2:
                    wait_by_token(pe, 2 * CHUNKS + n)
                else:
                    pe.wait_ge(x_final, n - 1)
                for t in range(T):
                    for k in range(HT):
                        last = pe.matmul(by_token(n)[:, t * P:(t + 1) * P], hid1[n % 2][:, k, t * P:(t + 1) * P],
                                         wt[:, (W_DOWN + k) * P:(W_DOWN + k + 1) * P], start=(k == 0), stop=(k == HT - 1))
                last.then_inc(down_made, 1)

            for ch in range(CHUNKS):
                turn(ch, ch)
            for b in range(BATCH):
                pe.wait_ge(rows_kept, 2 * b + 2)
                at = by_token(b)
                for h in range(2):
                    last = pe.matmul(at[0:1, 0:EXPERTS], ysum[:, 2 * b + h:2 * b + h + 1], wr[:, :], start=(h == 0), stop=(h == 1))
                last.then_inc(logits_made, 1)
            for b in range(BATCH):
                pe.wait_ge(wv_made, b + 1)
                pe.matmul(by_token(b)[:, P:P + TOP], ones[0:1, :], wv[:, b, 0:TOP], start=True, stop=True).then_inc(wb_spread, 1)
            ffn_up(0)
            ffn_up(1)
            pe.wait_ge(w2_scaled, BATCH)
            ffn_down(0)
            ffn_up(2)
            ffn_down(1)
            ffn_up(3)
            ffn_down(2)
            turn(CHUNKS, 0)
            turn(CHUNKS + 1, 1)
            ffn_down(3)
            gau_in(0, 0)
            turn(CHUNKS + 2, 2)
            gau_in(1, 1)
            gau_in(2, 2)
            turn(CHUNKS + 3, 3)
            gau_dots(0)
            gau_in(3, 3)
            gau_out(0)
            gau_dots(1)
            turn(2 * CHUNKS, PAIRED[0])
            turn(2 * CHUNKS + 1, PAIRED[1])
            gate_up(0)
            gau_out(1)
            gate_up(1)
            turn(2 * CHUNKS + 2, PAIRED[2])
            turn(2 * CHUNKS + 3, PAIRED[3])
            down(0)
            gate_up(2)
            down(1)
            gate_up(3)
            down(2)
            down(3)

        @block.scalar
        def _(act):
            def keep(n, ch, scale=None, bias=None, total=None):
                act.wait_ge(rows_turned, n + 1)
                at = other(OTHER.index(("rows", n)))
                if scale is None:
                    act.activation(turned[:, ch, :], at, ACT.Copy, **({} if total is None else dict(accum_out=total))).then_inc(rows_kept, 1)
                else:
                    act.activation(turned[:, ch, :], at, ACT.Identity, bias=bias, scale=scale).then_inc(rows_kept, 1)

            def gelu(ch):
                b = ch // 2
                for n in range(UP):
                    m = ch * UP + n
                    act.wait_ge(hid_made, m + 1)
                    if n == 0:
                        act.wait_ge(experts_in[b], 16 * EXPERT_DMAS)
                        if ch >= 2:
                            act.wait_ge(ffn_made, ch - 1)
                    act.activation(hid[ch % 2][:, n, :], wide(m), ACT.Gelu, bias=b1s[:, b, n // FT, n % FT:n % FT + 1]).then_inc(gelu_made, 1)

            def silu(n, ch):
                for e in range(IN):
                    act.wait_ge(uvb_made, n * IN + e + 1)
                    act.activation(uvb[:, ch, e, :], wide(FIRST_IN + n * IN + e), ACT.Silu, bias=c["uvb_bias"][:, e:e + 1])\
                       .then_inc(silu_made, 1)

            def relus(h):
                for i, n in enumerate((0, 2, 1)):
                    act.wait_ge(dots_made, 3 * h + i + 1)
                    if h and i == 0:
                        act.wait_ge(mix_made, 1)
                    act.activation(kern[:, n, :], other(OTHER.index(("dots", 4 * h + i + 1))), ACT.Relu, bias=c["rel"][:, n:n + 1],
                                   scale=1.0 / CHUNK).then_inc(relu_made, 1)

            def gates(n):
                for k in range(HT):
                    act.wait_ge(pair_made, n * HT + k + 1)
                    if n >= 2:
                        act.wait_ge(up_taken, (n - 2) * HT + k + 1)
                    act.activation(gate[n % 2][:, k, :], wide(FIRST_PAIR + 2 * (n * HT + k)), ACT.Silu).then_inc(gate_made, 1)

            for ch in range(CHUNKS):
                keep(ch, ch, total=ysum[:, ch:ch + 1])
            for b in range(BATCH):
                act.wait_ge(shifted, 2 * b + 1)
                act.activation(router[:, b, 2, :], router[:, b, 1, :], ACT.Exp, accum_out=wv[:, b, 2:3]).then_inc(exp_made, 1)
                act.wait_ge(shifted, 2 * b + 2)
                act.activation(router[:, b, 6, 0:1], router[:, b, 5, 0:1], ACT.Exp).then_inc(exp_w, 1)
            for ch in range(CHUNKS):
                gelu(ch)
            keep(CHUNKS, 0, c["lng"][:, 0:1], c["lnb"][:, 0:1])
            keep(CHUNKS + 1, 1, c["lng"][:, 0:1], c["lnb"][:, 0:1])
            silu(0, 0)
            keep(CHUNKS + 2, 2, c["lng"][:, 0:1], c["lnb"][:, 0:1])
            silu(1, 1)
            silu(2, 2)
            keep(CHUNKS + 3, 3, c["lng"][:, 0:1], c["lnb"][:, 0:1])
            relus(0)
            silu(3, 3)
            relus(1)
            keep(2 * CHUNKS, PAIRED[0])
            keep(2 * CHUNKS + 1, PAIRED[1])
            gates(0)
            gates(1)
            keep(2 * CHUNKS + 2, PAIRED[2])
            keep(2 * CHUNKS + 3, PAIRED[3])
            gates(2)
            gates(3)

        @block.vector
        def _(dve):
            steps = [0]

            def link(ins):
                steps[0] += 1
                ins.then_inc(step, 1)
                dve.wait_ge(step, steps[0])

            def moments(k, rows, eps, outer=0.0):
                for t in range(T):
                    last = dve.bn_stats(stats[:, k, t, :], rows[:, t, :])
                link(last)
                for t in range(T):
                    last = dve.bn_aggr(mv[:, k, t, :], stats[:, k, t, :])
                link(last)
                dve.tensor_scalar(inv[:, k, 0, :], mv[:, k, :, 1], eps, None, ALU.add)
                dve.tensor_scalar(inv[:, k, 1, :], mv[:, k, :, 1], 1.0 + outer, outer * eps if outer else eps, ALU.mult, ALU.add)\
                   .then_inc(var_made, 1)

            def normalise(k, rows, ch, which=0):
                dve.wait_ge(inv_made, k + 1)
                for t in range(T):
                    last = dve.tensor_scalar(y0[:, ch, t, :], rows[:, t, :], mv[:, k, t, 0:1], inv[:, k, which, t:t + 1], ALU.subtract, ALU.mult)
                last.then_inc(rows_made, 1)

            def route(b):
                r = router[:, b, :, :]
                dve.wait_ge(logits_made, b + 1)
                link(dve.scalar_tensor_tensor(out=r[:, 0, :], in0=by_token(b)[0:1, 0:EXPERTS], scalar=1.0 / SEQ, in1=br[:, :],
                                              op0=ALU.mult, op1=ALU.add))
                link(dve.tensor_reduce(wv[:, b, 3:4], r[:, 0, :], AX_X, ALU.max))
                dve.tensor_scalar(r[:, 1, :], r[:, 0, :], wv[:, b, 3:4], None, ALU.subtract).then_inc(shifted, 1)
                dve.wait_ge(exp_made, b + 1)
                link(dve.reciprocal(wv[:, b, 2:3], wv[:, b, 2:3]))
                link(dve.tensor_scalar(r[:, 3, :], r[:, 2, :], wv[:, b, 2:3], None, ALU.mult))
                link(dve.max(r[:, 4, :], r[:, 3, :]))
                dve.max_index(chosen[:, b, :], r[:, 4, :], r[:, 3, :]).then_inc(chosen_made, 1)
                dve.tensor_tensor(r[:, 5, 0:1], r[:, 4, 1:2], r[:, 4, 0:1], ALU.subtract).then_inc(shifted, 1)
                dve.wait_ge(exp_w, b + 1)
                link(dve.tensor_scalar(r[:, 6, 1:2], r[:, 6, 0:1], 1.0, None, ALU.add))
                link(dve.reciprocal(wv[:, b, 0:1], r[:, 6, 1:2]))
                dve.tensor_tensor(wv[:, b, 1:2], wv[:, b, 0:1], r[:, 6, 0:1], ALU.mult).then_inc(wv_made, 1)

            def weigh(b):
                dve.wait_ge(wb_spread, b + 1)
                link(dve.tensor_copy(wb[:, b, :], by_token(b)[:, P:P + TOP]))
                dve.wait_ge(experts_in[b], 16 * EXPERT_DMAS)
                dve.wait_ge(wv_made, b + 1)
                for k in range(TOP):
                    dve.tensor_scalar(w2s[:, b, k, :, :], w2s[:, b, k, :, :], wb[:, b, k:k + 1], None, ALU.mult)
                link(dve.tensor_scalar(b2w[:, b, 0, :], b2s[:, b, 0, :], wv[:, b, 0:1], None, ALU.mult))
                dve.scalar_tensor_tensor(out=b2w[:, b, 1, :], in0=b2s[:, b, 1, :], scalar=wv[:, b, 1:2], in1=b2w[:, b, 0, :],
                                         op0=ALU.mult, op1=ALU.add).then_inc(w2_scaled, 1)

            def after_ffn(ch):
                k = CHUNKS + ch
                y = y0[:, ch, :, :]
                dve.wait_ge(ffn_made, ch + 1)
                dve.tensor_tensor(y, by_token(ch).rearrange("p (t d) -> p t d", d=DIM), y, ALU.add).then_inc(token_out, 1)
                dve.wait_ge(token_out, ch + 1)
                moments(k, y, LN_EPS)
                for t in range(T):
                    last = dve.scalar_tensor_tensor(out=y[:, t, :], in0=y[:, t, :], scalar=mv[:, k, t, 0:1], in1=gamma[:, :],
                                                    op0=ALU.subtract, op1=ALU.mult)
                link(last)
                dve.wait_ge(inv_made, 2 * ch + CHUNKS + 1)
                dve.wait_ge(beta_added, ch + 1)
                for t in range(T):
                    last = dve.scalar_tensor_tensor(out=xc(ch)[:, t, :], in0=y[:, t, :], scalar=inv[:, k, 0, t:t + 1], in1=xb[:, ch, t, :],
                                                    op0=ALU.mult, op1=ALU.add)
                last.then_inc(new_x, 1)
                dve.wait_ge(new_x, ch + 1)
                k = 2 * CHUNKS + ch
                moments(k, xc(ch), LN_EPS, LN_EPS)
                dve.wait_ge(inv_made, 2 * ch + CHUNKS + 2)
                for t in range(T):
                    last = dve.tensor_scalar(y[:, t, :], xc(ch)[:, t, :], mv[:, k, t, 0:1], inv[:, k, 1, t:t + 1], ALU.subtract, ALU.mult)
                last.then_inc(rows_made, 1)

            def gau_heads(h):
                dve.wait_ge(silu_made, (3 + h) * IN)
                if h:
                    dve.wait_ge(dots_made, 3)
                for l, n in ((1, 0), (0, 1), (0, 0), (1, 1)):
                    last = dve.tensor_scalar(heads[:, l, n, :], uvb[:, 2 * l + h, IN - 1, :], c["qk_cols"][:, n:n + 1], c["qk_cols"][:, 2 + n:3 + n],
                                             ALU.mult, ALU.add)
                last.then_inc(heads_made, 1)
                dve.wait_ge(heads_made, h + 1)
                dve.tensor_tensor(prod[:, 0, :], heads[:, 0, 0, :], heads[:, 0, 1, :], ALU.mult).then_inc(prod_made, 1)
                dve.tensor_tensor(prod[:, 2, :], heads[:, 1, 0, :], heads[:, 1, 1, :], ALU.mult).then_inc(prod_made, 1)
                dve.wait_ge(turned_q, h + 1)
                dve.tensor_tensor(prod[:, 1, :], other(OTHER.index(("turned_q", 4 * h))), heads[:, 0, 1, :], ALU.mult).then_inc(prod_made, 1)

            def gau_mix(h):
                dve.wait_ge(relu_made, 3 * h + 3)
                link(dve.tensor_tensor(kern[:, :, :], kern[:, :, :], kern[:, :, :], ALU.mult))
                dve.wait_ge(vu_made, h + 1)
                if h:
                    dve.wait_ge(gau_made, 2)
                dve.tensor_tensor(mix[:, 0, :, :], vu[:, 0, :, :], over_mid(kern[:, 0, :], 2), ALU.mult)
                dve.tensor_tensor(vu[:, 1, :, :], vu[:, 1, :, :], over_mid(kern[:, 1, :], 2), ALU.mult)
                link(dve.tensor_tensor(vu[:, 2, :, :], vu[:, 2, :, :], over_mid(kern[:, 2, :], 2), ALU.mult))
                dve.tensor_tensor(mix[:, 1, :, :], vu[:, 1, :, :], vu[:, 2, :, :], ALU.add).then_inc(mix_made, 1)

            def after_gau(n):
                ch = PAIRED[n]
                k = 3 * CHUNKS + n
                dve.wait_ge(gau_made, n + 1)
                dve.wait_ge(short_made, ch + 1)
                dve.tensor_tensor(xc(ch), by_token(n).rearrange("p (t d) -> p t d", d=DIM), xb[:, ch, :, :], ALU.add).then_inc(token_out, 1)
                dve.wait_ge(token_out, CHUNKS + n + 1)
                moments(k, xc(ch), LN_EPS)
                normalise(k, xc(ch), ch)

            def after_gates(n):
                for k in range(HT):
                    dve.wait_ge(gate_made, n * HT + k + 1)
                    if k == 0 and n >= 2:
                        dve.wait_ge(down_made, n - 1)
                    dve.tensor_tensor(hid1[n % 2][:, k, :], wide(FIRST_PAIR + 2 * (n * HT + k) + 1), gate[n % 2][:, k, :], ALU.mult)\
                       .then_inc(up_taken, 1)

            def final(n):
                dve.wait_ge(down_made, n + 1)
                dve.tensor_tensor(xc(PAIRED[n]), by_token(n).rearrange("p (t d) -> p t d", d=DIM), xc(PAIRED[n]), ALU.add)\
                   .then_inc(x_final, 1)

            for ch in range(CHUNKS):
                moments(ch, xc(ch), LN_EPS)
                if ch:
                    normalise(ch - 1, xc(ch - 1), ch - 1)
            normalise(CHUNKS - 1, xc(CHUNKS - 1), CHUNKS - 1)
            for b in range(BATCH):
                route(b)
            for b in range(BATCH):
                weigh(b)
            for ch in range(CHUNKS):
                after_ffn(ch)
            gau_heads(0)
            gau_mix(0)
            gau_heads(1)
            after_gau(0)
            after_gau(1)
            gau_mix(1)
            after_gates(0)
            after_gau(2)
            after_gau(3)
            after_gates(1)
            after_gates(2)
            final(0)
            final(1)
            after_gates(3)
            final(2)
            final(3)


_OUTS = [((BATCH, SEQ, DIM), "float32")]


def turn_of_position_1():
    half = S // 2
    angle = np.float32(10000.0) ** (-np.arange(half, dtype=np.float32) / np.float32(half))
    cos, sin = np.cos(angle), np.sin(angle)
    turn = np.zeros((S, S), np.float32)
    at = np.arange(half)
    turn[at, at] = turn[at + half, at + half] = cos
    turn[at, at + half] = -sin
    turn[at + half, at] = sin
    return np.ascontiguousarray(turn.T)


def kernel(**inputs):
    import concourse.bacc as _bacc
    from concourse.bass_utils import run_bass_kernel_spmd as _run

    nc = _bacc.Bacc("TRN2", target_bir_lowering=False, num_devices=1)
    arrays, args = {}, {}
    for name, value in inputs.items():
        v = np.ascontiguousarray(value)
        arrays[f"in_{name}"] = v
        args[name] = nc.dram_tensor(f"in_{name}", v.shape, mybir.dt.from_np(v.dtype), kind="ExternalInput").ap()
    arrays["turn"] = turn_of_position_1()
    turn = nc.dram_tensor("turn", (S, S), F32, kind="ExternalInput").ap()
    shape, dtype = _OUTS[0]
    out = nc.dram_tensor("out_0", shape, mybir.dt.from_np(np.dtype(dtype)), kind="ExternalOutput").ap()
    build(nc, args, turn, out)
    r = _run(nc, [arrays], core_ids=[0])
    return r.results[0]["out_0"]
```

```python
from contextlib import ExitStack

import numpy as np

import concourse.bass as bass
from concourse import mybir

F32 = mybir.dt.float32
F32R = mybir.dt.float32r
I32 = mybir.dt.int32
U32 = mybir.dt.uint32
ALU = mybir.AluOpType
ACT = mybir.ActivationFunctionType
AX_X = mybir.AxisListType.X

P = 128
BATCH, SEQ, DIM = 2, 1024, 128
TILES = SEQ // P
HEADS, GROUPS, DH = 16, 4, 64
INNER, KV = HEADS * DH, GROUPS * DH
NORMED = HEADS + GROUPS
QKV = INNER + 2 * KV
EXPERTS, HID, TOP = 8, 512, 2
FT = HID // P
EH, S = 256, 128
UVB = 2 * EH + S
CHUNK = 64
HID1 = 384
HT = HID1 // P
SCALE1 = 1.0 / 127.0
LN_EPS, ATT_EPS = 1e-5, 1e-6

TURNED = HEADS // 2 + GROUPS
UNITS = 4
BLOCKS = HEADS // 2 * TILES // 2
BODY = 4
BODIES = BLOCKS // BODY
QB = 2 * P
KR = DH + UNITS
LATE = 5
FIRST = 1
T = 4
CW = T * P
CHUNKS = BATCH * TILES // T
PAIRED = [0, 2, 1, 3]
LNS = 4 * CHUNKS
W_UVB, W_O, W_GATE, W_UP, W_DOWN, W_TILES = 0, 5, 7, 10, 13, 16


def column(v):
    return v.rearrange("(p a) -> p a", a=1)


def row(v):
    return v.rearrange("(a n) -> a n", a=1)


def everywhere(v, parts=P):
    return v.partition_broadcast(parts)


def over_last(t, n):
    return t.unsqueeze(2).broadcast_to([t.shape[0], t.shape[1], n])


def over_mid(t, m):
    return t.unsqueeze(1).broadcast_to([t.shape[0], m, t.shape[1]])


def build(nc, a, turn, out):
    with ExitStack() as ctx:
        def sb(name, shape, dt=F32, where=ctx):
            return where.enter_context(nc.sbuf_tensor(name, shape, dt))

        def sem(name):
            return ctx.enter_context(nc.semaphore(name))

        psum = ctx.enter_context(nc.psum_tensor("psum", [P, 4096], F32))
        x = sb("x", [P, BATCH, TILES, DIM])
        xv = [a["L0_attn_x"][b].rearrange("(p j) d -> p j d", j=TILES) for b in range(BATCH)]
        ident = sb("ident", [P, P])
        wt = sb("wt", [P, W_TILES * P])
        gamma = sb("gamma", [P, DIM])
        beta = sb("beta", [P, DIM])
        wr = sb("wr", [P, EXPERTS])
        br = sb("br", [1, EXPERTS])
        lng = sb("lng", [P, 1])
        lnb = sb("lnb", [P, 1])
        uvb_bias = sb("uvb_bias", [P, UVB // P])
        qk_cols = sb("qk_cols", [P, 4])
        ones_square = sb("ones_square", [P, P])
        bo = sb("bo", [P, DIM])
        rel = sb("rel", [P, 3])

        shared = dict(gamma=gamma, beta=beta, wr=wr, br=br, lng=lng, lnb=lnb, uvb_bias=uvb_bias, qk_cols=qk_cols,
                      ones_square=ones_square, bo=bo, rel=rel)
        first_layer(nc, a, xv, x, ident, wt, psum, sb, sem, shared)
        rest(nc, a, x, ident, wt, psum, sb, sem, out, shared, turn)


def first_layer(nc, a, xv, x, ident, wt, psum, sb, sem, c):
    with ExitStack() as own:
        def mine(name, shape, dt=F32):
            return sb(name, shape, dt, own)

        wqkv = mine("wqkv", [P, QKV])
        wmean = mine("wmean", [P, NORMED])
        wout = mine("wout", [P, HEADS // 2, DIM])
        aln_s = mine("aln_s", [P, 1])
        aln_b = mine("aln_b", [P, 1])
        qk_s = mine("qk_s", [P, 2])
        qk_o = mine("qk_o", [P, 2])
        st = mine("st", [P, BATCH, 4, TILES])
        hst = mine("hst", [P, 3, NORMED])
        eps = mine("eps", [P, 1])
        qh = mine("qh", [P, HEADS // 2, SEQ], F32R)
        ql = mine("ql", [P, HEADS // 2, SEQ], F32R)
        kh = mine("kh", [P, GROUPS, SEQ], F32R)
        kl = mine("kl", [P, GROUPS, SEQ], F32R)
        vb = mine("vb", [P, GROUPS, TILES, DH])
        qs = [mine(f"qs{i}", [P, UNITS, P], F32R) for i in range(BODY)]
        qm = [mine(f"qm{i}", [P, UNITS, P], F32R) for i in range(BODY)]
        kg = mine("kg", [P, SEQ], F32R)
        kgl = mine("kgl", [P, SEQ], F32R)
        vg = mine("vg", [P, TILES, DH])
        PT = TILES * 2 * QB
        space = mine("space", [P, 12 * SEQ])
        pt = [space[:, i * PT:(i + 1) * PT].rearrange("p (k q) -> p k q", k=TILES) for i in range(2)]
        work = space[:, 2 * PT:]
        acc = [work[:, i * 2 * QB:(i + 1) * 2 * QB] for i in range(2)]
        ot = [work[:, (4 + i) * QB:(5 + i) * QB] for i in range(2)]
        rinv = work[:, 6 * QB:7 * QB]
        late = work[:, 7 * QB:9 * QB]
        xkeep = space[:, 11 * SEQ:]
        nmx = mine("nmx", [P, UNITS])
        raw = space[:, 7 * SEQ:9 * SEQ]
        rawi = space[:, 9 * SEQ:9 * SEQ + (W_TILES - W_GATE) * P].bitcast(I32)
        at = 0
        spaces = []
        for size in (NORMED * DH, SEQ, TURNED * P, TURNED * P, TURNED * P, NORMED * DH, NORMED * DH):
            spaces.append(space[:, at:at + size])
            at += size
        hsq = spaces[0]
        xnt = spaces[1]
        qn = spaces[2][:, 0:INNER].rearrange("p (h d) -> p h d", d=DH)
        kn = spaces[2][:, INNER:].rearrange("p (g t d) -> p g t d", t=2, d=DH)
        t1 = [t.rearrange("p (h q) -> p h q", q=P) for t in spaces[3:5]]
        qk_raw = spaces[5:7]
        cen = [space[:, (3 + i) * SEQ:(4 + i) * SEQ].rearrange("p (j d) -> p j d", d=DIM) for i in range(BATCH)]
        sq = [space[:, (5 + i) * SEQ:(6 + i) * SEQ] for i in range(BATCH)]

        x_in = [sem(f"x_in{b}") for b in range(BATCH)]
        w_in = sem("w_in")
        c_in = sem("c_in")
        shared_in = sem("shared_in")
        r_in = sem("r_in")
        ident_made = sem("ident_made")
        w_float = sem("w_float")
        w_turned = sem("w_turned")
        w_kept = sem("w_kept")
        dve_step = sem("dve_step")
        pool_step = sem("pool_step")
        cen_made = sem("cen_made")
        sq_made = sem("sq_made")
        var_made = sem("var_made")
        root_made = sem("root_made")
        xn_made = sem("xn_made")
        xn_turned = sem("xn_turned")
        xnt_made = sem("xnt_made")
        w_centred = sem("w_centred")
        qkv_made = sem("qkv_made")
        hsq_made = sem("hsq_made")
        hroot_made = sem("hroot_made")
        hsum = sem("hsum")
        hinv_made = sem("hinv_made")
        raw_made = sem("raw_made")
        keep_made = sem("keep_made")
        kn_made = sem("kn_made")
        qn_made = sem("qn_made")
        v_made = sem("v_made")
        twin_made = sem("twin_made")
        qn_turned = sem("qn_turned")
        t1_keys_made = sem("t1_keys_made")
        t1_made = sem("t1_made")
        keys_high_made = sem("keys_high_made")
        high_made = sem("high_made")
        low_made = sem("low_made")
        keys_low_made = sem("keys_low_made")
        q_in = [sem(f"q_in{i}") for i in range(BODY)]
        k_in = [sem(f"k_in{i}") for i in range(4)]
        v_in = [sem(f"v_in{i}") for i in range(4)]
        scored = sem("scored")
        max_made = sem("max_made")
        max_turned = sem("max_turned")
        max_placed = sem("max_placed")
        key_scored = sem("key_scored")
        exp_made = sem("exp_made")
        pool_added = sem("pool_added")
        late_added = sem("late_added")
        pv_made = sem("pv_made")
        sums_made = sem("sums_made")
        rinv_made = sem("rinv_made")
        ot_made = sem("ot_made")
        y_made = sem("y_made")
        x_added = sem("x_added")

        small = [(c["gamma"][:, :], everywhere(a["L0_ffn_gamma"])), (c["beta"][:, :], everywhere(a["L0_ffn_beta"])),
                 (c["wr"][:, :], a["L0_ffn_Wr"]), (c["br"][:, :], row(a["L0_ffn_br"])),
                 (c["lng"][:, :], column(a["L1_attn_ln_g"])), (c["lnb"][:, :], column(a["L1_attn_ln_b"])),
                 (c["bo"][:, :], everywhere(a["L1_attn_bo"])),
                 (c["rel"][:, 0:1], everywhere(a["L1_attn_w_rel"][CHUNK - 1:CHUNK])),
                 (c["rel"][:, 1:2], everywhere(a["L1_attn_w_rel"][CHUNK - 2:CHUNK - 1])),
                 (c["rel"][:, 2:3], everywhere(a["L1_attn_w_rel"][CHUNK - 1:CHUNK]))]
        biases = [a["L1_attn_bu"][0:P], a["L1_attn_bu"][P:EH], a["L1_attn_bv"][0:P], a["L1_attn_bv"][P:EH], a["L1_attn_bb"]]
        small += [(c["uvb_bias"][:, e:e + 1], column(v)) for e, v in enumerate(biases)]
        small += [(c["qk_cols"][:, n:n + 1], column(a[f"L1_attn_{v}"])) for n, v in enumerate(("qqw", "qkw", "qqb", "qkb"))]
        mine_small = [(aln_s[:, :], column(a["L0_attn_ln_scale"])), (aln_b[:, :], column(a["L0_attn_ln_bias"])),
                      (wout[:, :, :], a["L0_attn_Wout"].rearrange("(h p) d -> p h d", p=P))]
        for half in range(2):
            rows = slice(half * DH, (half + 1) * DH)
            mine_small += [(qk_s[rows, 0:1], column(a["L0_attn_qn_scale"])), (qk_s[rows, 1:2], column(a["L0_attn_kn_scale"])),
                           (qk_o[rows, 0:1], column(a["L0_attn_qn_bias"])), (qk_o[rows, 1:2], column(a["L0_attn_kn_bias"]))]
        N_RAW, N_SMALL = 7, len(mine_small)

        scores = [psum[:, SEQ * i:SEQ * (i + 1)] for i in range(2)]
        key_scores = [psum[:, 2 * SEQ + 512 * i:2 * SEQ + 512 * (i + 1)] for i in range(2)]
        outp = [psum[:, 3 * SEQ + 512 * i:3 * SEQ + 512 * (i + 1)] for i in range(2)]
        qkv = psum[:, 0:QKV]
        qnt = psum[:, QKV:QKV + TURNED * P]

        def exists(beta, part, back):
            return {"first": beta >= back, "mid": True, "last": beta < back}[part]

        block = own.enter_context(nc.Block())

        @block.sync
        def _(sp):
            sp.dma_start(x[:, 0], xv[0]).then_inc(x_in[0], 16)
            sp.dma_start(x[:, 1], xv[1]).then_inc(x_in[1], 16)
            for dst, src in mine_small:
                sp.dma_start(dst, src).then_inc(c_in, 16)
            sp.dma_start(wqkv[:, 0:INNER], a["L0_attn_Wq"]).then_inc(w_in, 16)
            sp.dma_start(wqkv[:, INNER:QKV], a["L0_attn_Wkv"]).then_inc(w_in, 16)
            for dst, src in small:
                sp.dma_start(dst, src).then_inc(shared_in, 16)
            with sp.Fori(0, BATCH) as b:
                def load_q(i, beta, wait=True):
                    n = BODY * i + beta
                    to = beta % BODY
                    if wait:
                        sp.wait_ge(key_scored, (b * BLOCKS + n - BODY + 1) * TILES)
                    at = bass.ds(n * QB, QB)
                    for h in range(2):
                        rows, cols = slice(h * DH, (h + 1) * DH), slice(2 * h, 2 * h + 2)
                        high = qh[rows, :, :].bitcast(F32).rearrange("p h q -> p (h q)")[:, at]
                        low = ql[rows, :, :].bitcast(F32).rearrange("p h q -> p (h q)")[:, at]
                        for dst, src in ((qs[to][0:DH, cols, :], high), (qs[to][DH:P, cols, :], low), (qm[to][0:DH, cols, :], high)):
                            sp.dma_start(dst.rearrange("p u q -> p (u q)").bitcast(F32), src).then_inc(q_in[to], 16)

                def load_k(i, quarter, wait=True):
                    if wait:
                        sp.wait_ge(key_scored, (b * BLOCKS + BODY * i - 1) * TILES + 2 * quarter + 2)
                    at = slice(quarter * QB, (quarter + 1) * QB)
                    sp.dma_start(kg[:, at].bitcast(F32), kh[:, :, at].bitcast(F32)[:, bass.ds(i // 2, 1), :].rearrange("p g k -> p (g k)")).then_inc(k_in[quarter], 16)
                    sp.dma_start(kgl[0:KR, at].bitcast(F32), kl[0:KR, :, at].bitcast(F32)[:, bass.ds(i // 2, 1), :].rearrange("p g k -> p (g k)")).then_inc(k_in[quarter], 16)

                def load_v(i, quarter, wait=True):
                    if wait:
                        sp.wait_ge(pv_made, (b * BLOCKS + BODY * i - 1) * TILES + 2 * quarter + 2)
                    at = slice(2 * quarter, 2 * quarter + 2)
                    sp.dma_start(vg[:, at, :], vb[:, i // 2, at, :]).then_inc(v_in[quarter], 16)

                def body(i, last):
                    load_q(i, 2)
                    for quarter in range(4):
                        load_k(i, quarter)
                        if quarter:
                            load_v(i, quarter - 1)
                    load_q(i, 3)
                    load_v(i, 3)
                    if not last:
                        load_q(i, 4)
                        load_q(i, 5)

                for t in range(4):
                    for made in (keys_low_made, v_made):
                        sp.wait_ge(made, TILES * b + 2 * t + 2)
                    load_k(0, t, wait=False)
                    load_v(0, t, wait=False)
                    for made in (high_made, low_made):
                        sp.wait_ge(made, TILES * b + 2 * t + 2)
                    load_q(0, t, wait=False)
                load_q(0, 4)
                load_q(0, 5)
                with sp.Fori(1, BODIES - 1) as i:
                    body(i, last=False)
                body(BODIES - 1, last=True)

        @block.gpsimd
        def _(pool):
            pool.memset(ident[:, :], 0.0).then_inc(pool_step, 1)
            pool.memset(c["ones_square"][:, :], 1.0).then_inc(pool_step, 1)
            pool.wait_ge(pool_step, 1)
            pool.affine_select(out=ident[:, :], in_=ident[:, :], compare_op=ALU.not_equal, fill=1.0, base=0,
                               pattern=[[-1, P]], channel_multiplier=1).then_inc(ident_made, 1)
            pool.wait_ge(ident_made, 1)
            pool.memset(kl[DH:KR, :, :].bitcast(F32), 1.0).then_inc(pool_step, 1)
            pool.wait_ge(pool_step, 3)
            with pool.Fori(0, BATCH) as b:
                def high(j):
                    at = slice(j * P, (j + 1) * P)
                    pool.wait_ge(t1_keys_made, TILES * b + j + 1)
                    pool.sem_inc(pool_step, 1)
                    pool.tensor_scalar(kh[:, :, at], t1[j % 2][:, HEADS // 2:, :], 1.0, 0.0, ALU.mult, ALU.add)\
                        .then_inc(keys_high_made, 1)
                    pool.wait_ge(keys_high_made, TILES * b + j + 1)
                    pool.tensor_tensor(kl[0:DH, :, at], t1[j % 2][0:DH, HEADS // 2:, :], kh[0:DH, :, at].bitcast(F32),
                                       ALU.subtract).then_inc(keys_low_made, 1)
                    pool.wait_ge(t1_made, TILES * b + j + 1)
                    pool.sem_inc(pool_step, 1)
                    pool.tensor_scalar(qh[:, :, at], t1[j % 2][:, 0:HEADS // 2, :], 1.0, 0.0, ALU.mult, ALU.add)\
                        .then_inc(high_made, 1)

                for j in range(TILES):
                    pool.wait_ge(kn_made, TILES * b + j + 1)
                    pool.sem_inc(pool_step, 1)
                    pool.tensor_scalar(kn[:, :, 1, :], kn[:, :, 0, :], 1.0, 0.0, ALU.mult, ALU.add).then_inc(twin_made, 1)
                    if j:
                        high(j - 1)
                high(TILES - 1)

                def slot(i, beta, part):
                    if not exists(beta, part, 1):
                        return
                    m = b * BLOCKS + BODY * i + beta - 1
                    par = (beta - 1) % 2
                    for kt in range(1, TILES if part != "last" else LATE):
                        pool.wait_ge(exp_made, m * TILES + kt + 1)
                        if kt == 1:
                            if exists(beta, part, 3):
                                pool.wait_ge(sums_made, m - 1)
                        else:
                            pool.wait_ge(pool_added, m * (TILES - 1) + kt - 1)
                        pool.tensor_tensor(acc[par], pt[par][:, 0, :] if kt == 1 else acc[par], pt[par][:, kt, :], ALU.add)\
                            .then_inc(pool_added, 1)

                for beta in range(BODY):
                    slot(0, beta, "first")
                with pool.Fori(1, BODIES) as i:
                    for beta in range(BODY):
                        slot(i, beta, "mid")
                slot(BODIES, 0, "last")

        @block.tensor
        def _(pe):
            pe.wait_ge(ident_made, 1)
            for b in range(BATCH):
                pe.wait_ge(xn_made, b + 1)
                for j in range(TILES):
                    last = pe.transpose(psum[:, b * SEQ + j * P:b * SEQ + (j + 1) * P], cen[b][:, j, :], ident[:, :])
                last.then_inc(xn_turned, 1)
            pe.wait_ge(r_in, 16 * N_RAW)
            pe.wait_ge(w_float, 1)
            for t in range(W_TILES):
                last = pe.transpose(psum[:, 2 * SEQ + t * P:2 * SEQ + (t + 1) * P], raw[:, t * P:(t + 1) * P], ident[:, :])
            last.then_inc(w_turned, 1)
            pe.wait_ge(w_centred, 1)
            pe.wait_ge(keep_made, 1)
            with pe.Fori(0, BATCH) as b:
                def project(j):
                    if j:
                        pe.wait_ge(raw_made, TILES * b + j)
                        pe.wait_ge(v_made, TILES * b + j)
                    for n in range(QKV // 512):
                        last = pe.matmul(qkv[:, n * 512:(n + 1) * 512], xnt[:, j * P:(j + 1) * P],
                                         wqkv[:, n * 512:(n + 1) * 512], start=True, stop=True)
                    last.then_inc(qkv_made, 1)

                pe.wait_ge(xnt_made, b + 1)
                project(0)
                project(1)
                pe.wait_ge(w_kept, 1)
                pe.wait_ge(x_added, FIRST + b * BLOCKS)
                for j in range(TILES):
                    if j + 2 < TILES:
                        project(j + 2)
                    pe.wait_ge(qn_made, TILES * b + j + 1)
                    if j:
                        pe.wait_ge(t1_made, TILES * b + j)
                    pe.wait_ge(twin_made, TILES * b + j + 1)
                    for h in range(TURNED):
                        last = pe.transpose(qnt[:, h * P:(h + 1) * P], spaces[2][:, h * P:(h + 1) * P], ident[:, :])
                    last.then_inc(qn_turned, 1)

                pe.wait_ge(t1_made, TILES * b + TILES)
                pe.wait_ge(keys_high_made, TILES * b + TILES)

                def unit_scores(i, beta, part, u):
                    n = b * BLOCKS + BODY * i + beta
                    if u == 0:
                        pe.wait_ge(q_in[beta], 96 * (b * BODIES + i + 1))
                        if not (part == "first" and beta == 0):
                            pe.wait_ge(max_placed, n)
                    if not (part == "first" and beta == 0 and u < 2):
                        pe.wait_ge(max_made, n * UNITS + u - 1)
                    for half in range(2):
                        cols = slice(half * 512, half * 512 + 512)
                        last = pe.matmul(scores[u % 2][:, cols], qs[beta][:, u, :], kh[:, i // 2, cols], start=True, stop=True)
                    last.then_inc(scored, 1)

                def tile_scores(i, beta, part, kt):
                    m, to = b * BLOCKS + BODY * i + beta - 1, (beta - 1) % BODY
                    if kt == 0:
                        pe.wait_ge(max_placed, m + 1)
                    if kt % 2 == 0:
                        pe.wait_ge(k_in[kt // 2], 32 * (b * BODIES + (i if beta else i - 1) + 1))
                    if not (part == "first" and beta == 1 and kt < 2):
                        pe.wait_ge(exp_made, m * TILES + kt - 1)
                    keys = slice(kt * P, (kt + 1) * P)
                    pe.matmul(key_scores[kt % 2], kg[:, keys], qs[to][:, :, :].rearrange("p u q -> p (u q)"), start=True, stop=False)
                    pe.matmul(key_scores[kt % 2], kgl[0:KR, keys], qm[to][0:KR, :, :].rearrange("p u q -> p (u q)"),
                              start=False, stop=True).then_inc(key_scored, 1)

                def tile_values(i, beta, part, back, kt):
                    m, par = b * BLOCKS + BODY * i + beta - back, (beta - back) % 2
                    if not exists(beta, part, 1) or (part == "first" and beta == 1):
                        pe.wait_ge(exp_made, m * TILES + kt + 1)
                    if kt % 2 == 0:
                        pe.wait_ge(v_in[kt // 2], 16 * (b * BODIES + (i if beta >= back else i - 1) + 1))
                    if kt == 0 and exists(beta, part, 3):
                        pe.wait_ge(x_added, FIRST + m - 1)
                    for h in range(2):
                        last = pe.matmul(outp[par][h * DH:(h + 1) * DH, 0:QB], vg[:, kt, :], pt[par][:, kt, h * QB:(h + 1) * QB],
                                         start=(kt == 0), stop=(kt == TILES - 1))
                    last.then_inc(pv_made, 1)

                def sums(i, beta, part):
                    m, par = b * BLOCKS + BODY * i + beta - 2, (beta - 2) % 2
                    pe.wait_ge(pool_added, (m + 1) * (TILES - 1))
                    terms = [acc[par]] + ([late] if part == "last" and beta == 1 else [])
                    for k, term in enumerate(terms):
                        for h in range(2):
                            last = pe.matmul(outp[par][h * DH:(h + 1) * DH, QB:2 * QB], c["ones_square"][:, 0:DH],
                                             term[:, h * QB:(h + 1) * QB], start=(k == 0), stop=(k == len(terms) - 1))
                    last.then_inc(sums_made, 1)

                def turn_maxima(i, beta):
                    pe.wait_ge(max_made, (b * BLOCKS + BODY * i + beta + 1) * UNITS)
                    pe.matmul(scores[0][DH:KR, 0:P], nmx[:, :], ident[:, :], start=True, stop=True).then_inc(max_turned, 1)

                def project_out(i, beta):
                    m, par = b * BLOCKS + BODY * i + beta - 2, (beta - 2) % 2
                    pe.wait_ge(ot_made, m + 1)
                    for t in range(2):
                        last = pe.matmul(outp[par][:, QB + t * P:QB + (t + 1) * P], ot[par][:, t * P:(t + 1) * P],
                                         wout[:, (i if beta >= 2 else i - 1), :], start=True, stop=True)
                    last.then_inc(y_made, 1)

                def slot(i, beta, part):
                    for pair in range(TILES // 2):
                        both = (2 * pair, 2 * pair + 1)
                        if part != "last" and pair < UNITS // 2:
                            for u in both:
                                unit_scores(i, beta, part, u)
                        if exists(beta, part, 1):
                            for kt in both:
                                tile_scores(i, beta, part, kt)
                        back = 1 if pair else 2
                        if exists(beta, part, back):
                            for kt in both:
                                tile_values(i, beta, part, back, (kt - 2) % TILES)
                        if pair == 1 and exists(beta, part, 2):
                            sums(i, beta, part)
                        if pair == 2 and part != "last":
                            turn_maxima(i, beta)
                        if pair == 3 and exists(beta, part, 2):
                            project_out(i, beta)

                for beta in range(BODY):
                    slot(0, beta, "first")
                with pe.Fori(1, BODIES) as i:
                    for beta in range(BODY):
                        slot(i, beta, "mid")
                for beta in range(2):
                    slot(BODIES, beta, "last")

        @block.scalar
        def _(act):
            act.dma_start(raw[:, 0:2 * P].rearrange("p (t d) -> p t d", t=2), a["L1_attn_Wu"].rearrange("(t p) d -> p t d", p=P)).then_inc(r_in, 16)
            act.dma_start(raw[:, 2 * P:4 * P].rearrange("p (t d) -> p t d", t=2), a["L1_attn_Wv"].rearrange("(t p) d -> p t d", p=P)).then_inc(r_in, 16)
            act.dma_start(raw[:, 4 * P:5 * P], a["L1_attn_Wb"]).then_inc(r_in, 16)
            act.dma_start(raw[:, W_O * P:W_GATE * P], a["L1_attn_Wo"]).then_inc(r_in, 16)
            act.dma_start(rawi[:, 0:HID1].rearrange("p (t d) -> p t d", t=HT), a["L1_ffn_w_gate"].rearrange("(t p) d -> p t d", p=P)).then_inc(r_in, 16)
            act.dma_start(rawi[:, HID1:2 * HID1].rearrange("p (t d) -> p t d", t=HT), a["L1_ffn_w_up"].rearrange("(t p) d -> p t d", p=P)).then_inc(r_in, 16)
            act.dma_start(rawi[:, 2 * HID1:3 * HID1], a["L1_ffn_w_down"]).then_inc(r_in, 16)
            for b in range(BATCH):
                act.wait_ge(cen_made, b + 1)
                act.activation(sq[b], cen[b].rearrange("p j d -> p (j d)"), ACT.Square).then_inc(sq_made, 1)
            for b in range(BATCH):
                act.wait_ge(var_made, b + 1)
                act.activation(st[:, b, 2, :], st[:, b, 1, :], ACT.Sqrt).then_inc(root_made, 1)
            act.wait_ge(c_in, 16 * N_SMALL)
            for b in range(BATCH):
                act.wait_ge(xn_turned, b + 1)
                act.activation((xnt, xkeep)[b], psum[:, b * SEQ:(b + 1) * SEQ], ACT.Identity, bias=aln_b[:, 0:1], scale=aln_s[:, 0:1])\
                   .then_inc((xnt_made, keep_made)[b], 1)
            act.wait_ge(w_turned, 1)
            act.activation(wt[:, 0:SEQ], psum[:, 2 * SEQ:3 * SEQ], ACT.Copy)
            act.activation(wt[:, SEQ:2 * SEQ], psum[:, 3 * SEQ:4 * SEQ], ACT.Copy).then_inc(w_kept, 1)
            with act.Fori(0, BATCH) as b:
                def scale(j):
                    act.wait_ge(qn_turned, TILES * b + j + 1)
                    if j >= 2:
                        act.wait_ge(high_made, TILES * b + j - 1)
                        act.wait_ge(low_made, TILES * b + j - 1)
                        act.wait_ge(keys_low_made, TILES * b + j - 1)
                    act.activation(t1[j % 2][:, HEADS // 2:, :].rearrange("p h q -> p (h q)"), qnt[:, HEADS // 2 * P:], ACT.Identity,
                                   bias=qk_o[:, 1:2], scale=qk_s[:, 1:2]).then_inc(t1_keys_made, 1)
                    act.activation(t1[j % 2][:, 0:HEADS // 2, :].rearrange("p h q -> p (h q)"), qnt[:, 0:HEADS // 2 * P], ACT.Identity,
                                   bias=qk_o[:, 0:1], scale=qk_s[:, 0:1]).then_inc(t1_made, 1)

                def out_of_psum(j):
                    act.wait_ge(qkv_made, TILES * b + j + 1)
                    if j >= 2:
                        act.wait_ge(qn_made, TILES * b + j - 1)
                    act.activation(qk_raw[j % 2], qkv[:, 0:NORMED * DH], ACT.Copy).then_inc(raw_made, 1)
                    act.activation(vb[:, :, j, :], qkv[:, NORMED * DH:QKV].rearrange("p (g d) -> p g d", d=DH), ACT.Copy).then_inc(v_made, 1)

                out_of_psum(0)
                for j in range(TILES):
                    act.wait_ge(raw_made, TILES * b + j + 1)
                    act.activation(hsq, qk_raw[j % 2], ACT.Square).then_inc(hsq_made, 1)
                    if j + 1 < TILES:
                        out_of_psum(j + 1)
                    act.wait_ge(hsum, TILES * b + j + 1)
                    act.activation(hst[:, 1, :], hst[:, 0, :], ACT.Sqrt, bias=eps[:, 0:1], scale=1.0 / DH).then_inc(hroot_made, 1)
                    if j:
                        scale(j - 1)
                scale(TILES - 1)

                def slot(i, beta, part):
                    if not exists(beta, part, 1):
                        return
                    m = b * BLOCKS + BODY * i + beta - 1
                    par = (beta - 1) % 2
                    for kt in range(TILES):
                        act.wait_ge(key_scored, m * TILES + kt + 1)
                        if exists(beta, part, 3):
                            if kt == 0:
                                act.wait_ge(pool_added, (m - 1) * (TILES - 1))
                            act.wait_ge(pv_made, (m - 2) * TILES + kt + 1)
                        act.activation(pt[par][:, kt, :], key_scores[kt % 2], ACT.Exp).then_inc(exp_made, 1)

                for beta in range(BODY):
                    slot(0, beta, "first")
                with act.Fori(1, BODIES) as i:
                    for beta in range(BODY):
                        slot(i, beta, "mid")
                slot(BODIES, 0, "last")

        @block.vector
        def _(dve):
            dve.memset(eps[:, :], ATT_EPS)
            dve.sem_inc(x_added, FIRST)
            steps = 0
            for b in range(BATCH):
                xb = x[:, b, :, :]
                dve.wait_ge(x_in[b], 16)
                dve.tensor_reduce(st[:, b, 0, :], xb, AX_X, ALU.add).then_inc(dve_step, 1)
                dve.wait_ge(dve_step, steps + 1)
                dve.tensor_scalar(st[:, b, 0, :], st[:, b, 0, :], 1.0 / DIM, None, ALU.mult).then_inc(dve_step, 1)
                dve.wait_ge(dve_step, steps + 2)
                dve.tensor_tensor(cen[b], xb, over_last(st[:, b, 0, :], DIM), ALU.subtract).then_inc(cen_made, 1)
                steps += 2
            for b in range(BATCH):
                dve.wait_ge(sq_made, b + 1)
                dve.tensor_reduce(st[:, b, 1, :], sq[b].rearrange("p (j d) -> p j d", d=DIM), AX_X, ALU.add).then_inc(dve_step, 1)
                steps += 1
                dve.wait_ge(dve_step, steps)
                dve.tensor_scalar(st[:, b, 1, :], st[:, b, 1, :], (1.0 + ATT_EPS) / DIM, ATT_EPS * LN_EPS, ALU.mult, ALU.add).then_inc(var_made, 1)
            for b in range(BATCH):
                dve.wait_ge(root_made, b + 1)
                dve.reciprocal(st[:, b, 3, :], st[:, b, 2, :]).then_inc(dve_step, 1)
                steps += 1
                dve.wait_ge(dve_step, steps)
                dve.tensor_tensor(cen[b], cen[b], over_last(st[:, b, 3, :], DIM), ALU.mult).then_inc(xn_made, 1)
            dve.wait_ge(r_in, 16 * N_RAW)
            dve.tensor_scalar(raw[:, W_GATE * P:], rawi[:, :], SCALE1, None, ALU.mult).then_inc(w_float, 1)
            dve.wait_ge(w_in, 32)
            heads = wqkv[:, 0:NORMED * DH].rearrange("p (h d) -> p h d", d=DH)
            dve.tensor_reduce(wmean[:, :], heads, AX_X, ALU.add).then_inc(dve_step, 1)
            dve.wait_ge(dve_step, steps + 1)
            dve.tensor_scalar(wmean[:, :], wmean[:, :], 1.0 / DH, None, ALU.mult).then_inc(dve_step, 1)
            dve.wait_ge(dve_step, steps + 2)
            dve.tensor_tensor(heads, heads, over_last(wmean[:, :], DH), ALU.subtract).then_inc(w_centred, 1)
            dve.wait_ge(c_in, 16 * N_SMALL)
            dve.tensor_scalar(qk_s[:, 0:1], qk_s[:, 0:1], DH ** -0.5, None, ALU.mult).then_inc(dve_step, 1)
            dve.tensor_scalar(qk_o[:, 0:1], qk_o[:, 0:1], DH ** -0.5, None, ALU.mult).then_inc(dve_step, 1)
            dve.wait_ge(shared_in, 16 * len(small))
            dve.wait_ge(keep_made, 1)
            with dve.Fori(0, BATCH) as b:
                def low(j):
                    dve.wait_ge(high_made, TILES * b + j + 1)
                    dve.tensor_tensor(ql[:, :, j * P:(j + 1) * P], t1[j % 2][:, 0:HEADS // 2, :],
                                      qh[:, :, j * P:(j + 1) * P].bitcast(F32), ALU.subtract).then_inc(low_made, 1)

                for j in range(TILES):
                    n = TILES * b + j
                    dve.wait_ge(hsq_made, n + 1)
                    dve.tensor_reduce(hst[:, 0, :], hsq.rearrange("p (h d) -> p h d", d=DH), AX_X, ALU.add)\
                       .then_inc(hsum, 1)
                    dve.wait_ge(hroot_made, n + 1)
                    dve.reciprocal(hst[:, 2, :], hst[:, 1, :]).then_inc(hinv_made, 1)
                    dve.wait_ge(hinv_made, n + 1)
                    if j:
                        dve.wait_ge(qn_turned, n)
                    dve.wait_ge(raw_made, n + 1)
                    heads_raw = qk_raw[j % 2].rearrange("p (h d) -> p h d", d=DH)
                    dve.tensor_tensor(kn[:, :, 0, :], heads_raw[:, HEADS:, :], over_last(hst[:, 2, HEADS:], DH), ALU.mult).then_inc(kn_made, 1)
                    dve.tensor_tensor(qn, heads_raw[:, 0:HEADS, :], over_last(hst[:, 2, 0:HEADS], DH), ALU.mult).then_inc(qn_made, 1)
                    if j >= 2:
                        low(j - 2)
                low(TILES - 2)

                def slot(i, beta, part):
                    n = b * BLOCKS + BODY * i + beta

                    def add(m, par):
                        dve.wait_ge(y_made, m + 1)
                        dve.wait_ge(x_added, FIRST + m)
                        c_at = (beta - 3) % BODY
                        at = x[:, b, 2 * c_at:2 * c_at + 2, :]
                        dve.tensor_tensor(at, at, outp[par][:, QB:2 * QB].rearrange("p (t d) -> p t d", d=DIM), ALU.add)\
                           .then_inc(x_added, 1)

                    if part != "last":
                        for u in range(UNITS):
                            dve.wait_ge(scored, n * UNITS + u + 1)
                            if u == 0 and not (part == "first" and beta == 0):
                                dve.wait_ge(max_turned, n)
                            dve.tensor_reduce(nmx[:, u:u + 1], scores[u % 2], AX_X, ALU.max, negate=True).then_inc(max_made, 1)
                            if u == 1 and exists(beta, part, 3):
                                add(n - 3, (beta - 3) % 2)
                    elif exists(beta, part, 3):
                        add(n - 3, (beta - 3) % 2)
                    if exists(beta, part, 2):
                        m, par = n - 2, (beta - 2) % 2
                        dve.wait_ge(sums_made, m + 1)
                        dve.reciprocal(rinv, outp[par][:, QB:2 * QB]).then_inc(rinv_made, 1)
                    if exists(beta, part, 2):
                        m, par = n - 2, (beta - 2) % 2
                        dve.wait_ge(rinv_made, m + 1)
                        dve.wait_ge(pv_made, (m + 1) * TILES)
                        if exists(beta, part, 4):
                            dve.wait_ge(y_made, m - 1)
                        dve.tensor_tensor(ot[par], outp[par][:, 0:QB], rinv, ALU.mult).then_inc(ot_made, 1)
                    if part != "last":
                        dve.wait_ge(max_turned, n + 1)
                        dve.tensor_tensor(qm[beta][DH:KR, :, :], over_mid(scores[0][DH:KR, 0:P], UNITS),
                                          over_last(ident[DH:KR, DH:KR], P), ALU.mult).then_inc(max_placed, 1)

                slot(0, 0, "first")
                low(TILES - 1)
                for beta in range(1, BODY):
                    slot(0, beta, "first")
                with dve.Fori(1, BODIES) as i:
                    for beta in range(BODY):
                        slot(i, beta, "mid")
                slot(BODIES, 0, "last")
                dve.tensor_copy(xnt, xkeep).then_inc(xnt_made, 1)
                m = (b + 1) * BLOCKS - 1
                tiles = pt[(BLOCKS - 1) % 2]
                for kt in range(LATE + 1, TILES):
                    dve.wait_ge(exp_made, m * TILES + kt + 1)
                    if kt > LATE + 1:
                        dve.wait_ge(late_added, b * (TILES - LATE - 2) + kt - LATE - 1)
                    if kt == TILES - 1:
                        dve.wait_ge(pool_added, m * (TILES - 1) + LATE - 1)
                    dve.tensor_tensor(late, tiles[:, LATE, :] if kt == LATE + 1 else late, tiles[:, kt, :], ALU.add)\
                       .then_inc(*((late_added, 1) if kt < TILES - 1 else (pool_added, TILES - LATE)))
                for beta in (1, 2):
                    slot(BODIES, beta, "last")


def rest(nc, a, x, ident, wt, psum, sb, sem, out, c, turn):
    gamma, beta, bo, ones, br, wr = c["gamma"], c["beta"], c["bo"], c["ones_square"], c["br"], c["wr"]
    with ExitStack() as own:
        def mine(name, shape, dt=F32):
            return sb(name, shape, dt, own)

        stats = mine("stats", [P, LNS, T, 6])
        mv = mine("mv", [P, LNS, T, 2])
        inv = mine("inv", [P, LNS, 2, T])
        minus = mine("minus", [P, CHUNKS, T])
        half_power = mine("half_power", [P, 2 * T])
        y0 = mine("y0", [P, CHUNKS, T, DIM])
        yb = mine("yb", [P, T, DIM])
        xb = mine("xb", [P, CHUNKS, T, DIM])
        turned = mine("turned_rows", [P, CHUNKS, CW])
        ysum = mine("ysum", [P, CHUNKS])
        turn_q = mine("turn_q", [P, S])
        router = mine("router", [1, BATCH, 8, EXPERTS])
        chosen = mine("chosen", [1, BATCH, EXPERTS], U32)
        wv = mine("wv", [1, BATCH, 4])
        wb = mine("wb", [P, BATCH, TOP])
        w1s = mine("w1s", [P, BATCH, TOP, HID])
        w2s = mine("w2s", [P, BATCH, TOP, FT, DIM])
        b1s = mine("b1s", [P, BATCH, TOP, FT])
        b2s = mine("b2s", [1, BATCH, TOP, DIM])
        b2w = mine("b2w", [1, BATCH, 2, DIM])
        hid = [mine(f"hid{i}", [P, TOP * FT, CW]) for i in range(2)]
        uvb = mine("uvb", [P, CHUNKS, UVB // P, CW])
        heads = mine("heads", [P, BATCH, 2, CW])
        prod = mine("prod", [P, 3, CW])
        kern = mine("kern", [P, 3, CW])
        vu = mine("vu", [P, 3, 2, CW])
        mix = mine("mix", [P, BATCH, 2, CW])
        gate = [hid[i][:, 0:HT, :] for i in range(2)]
        hid1 = [hid[i][:, HT:2 * HT, :] for i in range(2)]

        step = sem("step")
        pool_step = sem("pool_step2")
        var_made = sem("var2_made")
        inv_made = sem("inv_made")
        rows_made = sem("rows_made")
        rows_turned = sem("rows_turned")
        rows_kept = sem("rows_kept")
        logits_made = sem("logits_made")
        shifted = sem("shifted")
        exp_made = sem("exp2_made")
        chosen_made = sem("chosen_made")
        wv_made = sem("wv_made")
        wb_spread = sem("wb_spread")
        exp_w = sem("exp_w")
        up_in = [sem(f"up_in{b}") for b in range(BATCH)]
        b1_in = [sem(f"b1_in{b}") for b in range(BATCH)]
        down_in = [sem(f"down_in{b}") for b in range(BATCH)]
        w2_scaled = sem("w2_scaled")
        b2_spread = sem("b2_spread")
        b2_added = sem("b2_added")
        hid_made = sem("hid_made")
        gelu_made = sem("gelu_made")
        beta_added = sem("beta_added")
        ffn_made = sem("ffn_made")
        new_x = sem("new_x")
        short_made = sem("short_made")
        token_out = sem("token_out")
        uvb_made = sem("uvb_made")
        silu_made = sem("silu_made")
        heads_made = sem("heads_made")
        turned_q = sem("turned_q")
        prod_made = sem("prod_made")
        dots_made = sem("dots_made")
        relu_made = sem("relu_made")
        kern_made = sem("kern_made")
        vu_made = sem("vu_made")
        mix_made = sem("mix_made")
        gau_made = sem("gau_made")
        pair_made = sem("pair_made")
        gate_made = sem("gate_made")
        up_taken = sem("up_taken")
        down_made = sem("down_made")
        x_final = sem("x_final")
        turn_in = sem("turn_in")
        stored = sem("stored")

        UP = TOP * FT
        IN = UVB // P

        def batch_half(ch):
            return ch // 2, ch % 2

        def xc(ch):
            b, h = batch_half(ch)
            return x[:, b, T * h:T * (h + 1), :]

        def wide(m):
            return psum[:, (m % 4) * CW:(m % 4 + 1) * CW]

        def by_token(m):
            return psum[:, (4 + m % 2) * CW:(5 + m % 2) * CW]

        def other(m):
            return psum[:, (6 + m % 2) * CW:(7 + m % 2) * CW]

        FIRST_IN = CHUNKS * UP
        FIRST_PAIR = FIRST_IN + CHUNKS * IN

        def wait_wide(pe, m):
            m -= 4
            if m < 0:
                return
            if m < FIRST_IN:
                pe.wait_ge(gelu_made, m + 1)
            elif m < FIRST_PAIR:
                pe.wait_ge(silu_made, m - FIRST_IN + 1)
            else:
                pe.wait_ge(up_taken, (m - FIRST_PAIR) // 2 + 1)

        def wait_by_token(pe, m):
            if m >= 2:
                pe.wait_ge(token_out, m - 1)

        OTHER = ([("rows", n) for n in range(8)]
                 + [("turned_q", 0), ("dots", 1), ("dots", 2), ("dots", 3)]
                 + [("turned_q", 4), ("rows", 8), ("dots", 5), ("dots", 6), ("dots", 7)]
                 + [("rows", n) for n in range(9, 12)])

        def wait_other(pe, m):
            if m < 2:
                return
            kind, n = OTHER[m - 2]
            if kind == "rows":
                pe.wait_ge(rows_kept, n + 1)
            elif kind == "turned_q":
                pe.wait_ge(prod_made, 3 * (n // 4) + 3)
            else:
                pe.wait_ge(relu_made, 3 * (n // 4) + n % 4)

        block = own.enter_context(nc.Block())

        @block.sync
        def _(sp):
            sp.dma_start(turn_q[:, :], turn).then_inc(turn_in, 16)
            for b in range(BATCH):
                sp.wait_ge(chosen_made, b + 1)
                es = [sp.value_load(chosen[0:1, b, k:k + 1], min_val=0, max_val=EXPERTS - 1) for k in range(TOP)]
                for k, e in enumerate(es):
                    sp.dma_start(w1s[:, b, k, :], a["L0_ffn_W1"][bass.ds(e, 1), :, :].rearrange("e d f -> d (e f)")).then_inc(up_in[b], 16)
                for k, e in enumerate(es):
                    sp.dma_start(b1s[:, b, k, :], a["L0_ffn_b1"][bass.ds(e, 1), :].rearrange("e (t f) -> f (e t)", f=P), allow_slow_non_contiguous=True).then_inc(b1_in[b], 16)
                for k, e in enumerate(es):
                    sp.dma_start(w2s[:, b, k, :, :], a["L0_ffn_W2"][bass.ds(e, 1), :, :].rearrange("e (t f) d -> f (e t) d", f=P)).then_inc(down_in[b], 16)
                    sp.dma_start(b2s[:, b, k, :], a["L0_ffn_b2"][bass.ds(e, 1), :]).then_inc(down_in[b], 16)
            for n, ch in enumerate(PAIRED):
                b, h = batch_half(ch)
                sp.wait_ge(x_final, n + 1)
                sp.dma_start(out[b].rearrange("(p j) d -> p j d", j=TILES)[:, T * h:T * (h + 1), :], xc(ch)).then_inc(stored, 16)
            sp.wait_ge(stored, 16 * CHUNKS)

        @block.gpsimd
        def _(pool):
            pool.memset(half_power[:, :], -0.5).then_inc(pool_step, 1)
            pool.wait_ge(pool_step, 1)

            roots = [0]

            def root(k, both=False):
                roots[0] += 1
                pool.wait_ge(var_made, roots[0])
                flat = inv[:, k, 0:2 if both else 1, :].rearrange("p s t -> p (s t)")
                pool.tensor_tensor(flat, flat, half_power[:, 0:2 * T if both else T], ALU.pow).then_inc(inv_made, 1)

            def shortcut(ch):
                b, h = batch_half(ch)
                k = 2 * CHUNKS + ch
                pool.wait_ge(rows_made, CHUNKS + ch + 1)
                pool.tensor_tensor(minus[:, ch, :], mv[:, k, :, 0], inv[:, k, 0, :], ALU.mult).then_inc(pool_step, 1)
                pool.tensor_tensor(xb[:, ch, :, :], xc(ch), over_mid(bo[:, :], T), ALU.add).then_inc(pool_step, 1)
                pool.wait_ge(pool_step, 1 + 4 * ch + 2)
                pool.tensor_scalar(minus[:, ch, :], minus[:, ch, :], -1.0, 0.0, ALU.mult, ALU.add).then_inc(pool_step, 1)
                pool.wait_ge(pool_step, 1 + 4 * ch + 3)
                for t in range(T):
                    last = pool.tensor_scalar(yb[:, t, :], xc(ch)[:, t, :], inv[:, k, 0, t:t + 1], minus[:, ch, t:t + 1], ALU.mult, ALU.add)
                last.then_inc(pool_step, 1)
                pool.wait_ge(pool_step, 1 + 4 * ch + 4)
                pool.tensor_tensor(xb[:, ch, :, :], xb[:, ch, :, :], yb[:, :, :], ALU.add).then_inc(short_made, 1)

            def products(h):
                pool.wait_ge(silu_made, (3 + h) * IN)
                if h:
                    pool.wait_ge(mix_made, 1)
                for n, (l, m) in ((1, (1, 0)), (2, (1, 1))):
                    last = pool.tensor_tensor(vu[:, n, :, :], uvb[:, 2 * m + h, 2:4, :], uvb[:, 2 * l + h, 0:2, :], ALU.mult)
                last.then_inc(vu_made, 1)

            for k in range(CHUNKS):
                root(k)
            for ch in range(CHUNKS):
                pool.tensor_tensor(xb[:, ch, :, :], xc(ch), over_mid(beta[:, :], T), ALU.add).then_inc(beta_added, 1)
            for ch in range(CHUNKS):
                root(CHUNKS + ch)
                root(2 * CHUNKS + ch, both=True)
                shortcut(ch)
            products(0)
            products(1)
            root(3 * CHUNKS)
            root(3 * CHUNKS + 1)
            root(3 * CHUNKS + 2)
            root(3 * CHUNKS + 3)

        @block.tensor
        def _(pe):
            others = [0]

            def next_other():
                wait_other(pe, others[0])
                others[0] += 1
                return other(others[0] - 1)

            def turn(n, ch):
                pe.wait_ge(rows_made, n + 1)
                at = next_other()
                for t in range(T):
                    last = pe.transpose(at[:, t * P:(t + 1) * P], y0[:, ch, t, :], ident[:, :])
                last.then_inc(rows_turned, 1)

            def ffn_up(ch):
                b = ch // 2
                if ch % 2 == 0:
                    pe.wait_ge(up_in[b], 16 * TOP)
                for n in range(UP):
                    m = ch * UP + n
                    wait_wide(pe, m)
                    pe.matmul(wide(m), w1s[:, b, n // FT, (n % FT) * P:(n % FT + 1) * P], turned[:, ch, :],
                              start=True, stop=True).then_inc(hid_made, 1)

            def ffn_down(ch):
                b = ch // 2
                pe.wait_ge(gelu_made, (ch + 1) * UP)
                pe.wait_ge(w2_scaled, b + 1)
                wait_by_token(pe, ch)
                for t in range(T):
                    o = by_token(ch)[:, t * P:(t + 1) * P]
                    for n in range(UP):
                        last = pe.matmul(o, hid[ch % 2][:, n, t * P:(t + 1) * P], w2s[:, b, n // FT, n % FT, :],
                                         start=(n == 0), stop=(n == UP - 1))
                last.then_inc(ffn_made, 1)

            def gau_in(n, ch):
                pe.wait_ge(rows_kept, CHUNKS + n + 1)
                for e in range(IN):
                    m = FIRST_IN + n * IN + e
                    wait_wide(pe, m)
                    pe.matmul(wide(m), wt[:, e * P:(e + 1) * P], turned[:, ch, :], start=True, stop=True).then_inc(uvb_made, 1)

            def turn_position(h):
                pe.wait_ge(heads_made, h + 1)
                pe.wait_ge(turn_in, 16)
                pe.matmul(next_other(), turn_q[:, :], heads[:, 1, 0, :], start=True, stop=True).then_inc(turned_q, 1)

            def gau_dots(h):
                for n in (0, 2, 1):
                    pe.wait_ge(prod_made, 3 * h + {0: 1, 2: 2, 1: 3}[n])
                    pe.matmul(next_other(), c["ones_square"][:, :], prod[:, n, :], start=True, stop=True).then_inc(dots_made, 1)

            def gau_out(h):
                for l in range(BATCH):
                    wait_by_token(pe, CHUNKS + 2 * h + l)
                    pe.wait_ge(mix_made, h + 1)
                    for t in range(T):
                        for e in range(2):
                            last = pe.matmul(by_token(CHUNKS + 2 * h + l)[:, t * P:(t + 1) * P], mix[:, l, e, t * P:(t + 1) * P],
                                             wt[:, (W_O + e) * P:(W_O + e + 1) * P], start=(e == 0), stop=(e == 1))
                    last.then_inc(gau_made, 1)

            def gate_up(n):
                pe.wait_ge(rows_kept, 2 * CHUNKS + n + 1)
                for k in range(HT):
                    for s, w in enumerate((W_GATE, W_UP)):
                        m = FIRST_PAIR + 2 * (n * HT + k) + s
                        wait_wide(pe, m)
                        last = pe.matmul(wide(m), wt[:, (w + k) * P:(w + k + 1) * P], turned[:, PAIRED[n], :], start=True, stop=True)
                    last.then_inc(pair_made, 1)

            def down(n):
                pe.wait_ge(up_taken, (n + 1) * HT)
                if n < 2:
                    wait_by_token(pe, 2 * CHUNKS + n)
                else:
                    pe.wait_ge(x_final, n - 1)
                for t in range(T):
                    for k in range(HT):
                        last = pe.matmul(by_token(n)[:, t * P:(t + 1) * P], hid1[n % 2][:, k, t * P:(t + 1) * P],
                                         wt[:, (W_DOWN + k) * P:(W_DOWN + k + 1) * P], start=(k == 0), stop=(k == HT - 1))
                last.then_inc(down_made, 1)

            def logits(b):
                pe.wait_ge(rows_kept, 2 * b + 2)
                for h in range(2):
                    last = pe.matmul(by_token(b)[0:1, 0:EXPERTS], ysum[:, 2 * b + h:2 * b + h + 1], wr[:, :], start=(h == 0), stop=(h == 1))
                last.then_inc(logits_made, 1)

            def spread(b):
                pe.wait_ge(wv_made, b + 1)
                pe.matmul(by_token(b)[:, P:P + TOP], ones[0:1, :], wv[:, b, 0:TOP], start=True, stop=True).then_inc(wb_spread, 1)

            turn(0, 0)
            turn(1, 1)
            logits(0)
            spread(0)
            turn(2, 2)
            turn(3, 3)
            logits(1)
            ffn_up(0)
            spread(1)
            for b in range(BATCH):
                pe.wait_ge(w2_scaled, b + 1)
                pe.matmul(by_token(b)[:, 2 * P:3 * P], ones[0:1, :], b2w[:, b, 1, :], start=True, stop=True).then_inc(b2_spread, 1)
            ffn_up(1)
            pe.wait_ge(b2_added, CHUNKS)
            ffn_down(0)
            ffn_up(2)
            ffn_down(1)
            ffn_up(3)
            ffn_down(2)
            turn(CHUNKS, 0)
            turn(CHUNKS + 1, 1)
            ffn_down(3)
            gau_in(0, 0)
            turn(CHUNKS + 2, 2)
            gau_in(1, 1)
            gau_in(2, 2)
            turn(CHUNKS + 3, 3)
            turn_position(0)
            gau_dots(0)
            gau_in(3, 3)
            gau_out(0)
            turn_position(1)
            turn(2 * CHUNKS, PAIRED[0])
            gau_dots(1)
            turn(2 * CHUNKS + 1, PAIRED[1])
            gate_up(0)
            gau_out(1)
            gate_up(1)
            down(0)
            turn(2 * CHUNKS + 2, PAIRED[2])
            turn(2 * CHUNKS + 3, PAIRED[3])
            gate_up(2)
            down(1)
            gate_up(3)
            down(2)
            down(3)

        @block.scalar
        def _(act):
            def keep(n, ch, scale=None, bias=None, total=None):
                act.wait_ge(rows_turned, n + 1)
                at = other(OTHER.index(("rows", n)))
                if scale is None:
                    act.activation(turned[:, ch, :], at, ACT.Copy, **({} if total is None else dict(accum_out=total))).then_inc(rows_kept, 1)
                else:
                    act.activation(turned[:, ch, :], at, ACT.Identity, bias=bias, scale=scale).then_inc(rows_kept, 1)

            def gelu(ch):
                b = ch // 2
                for n in range(UP):
                    m = ch * UP + n
                    act.wait_ge(hid_made, m + 1)
                    if n == 0:
                        act.wait_ge(b1_in[b], 16 * TOP)
                        if ch >= 2:
                            act.wait_ge(ffn_made, ch - 1)
                    act.activation(hid[ch % 2][:, n, :], wide(m), ACT.Gelu, bias=b1s[:, b, n // FT, n % FT:n % FT + 1]).then_inc(gelu_made, 1)

            def silu(n, ch):
                for e in range(IN):
                    act.wait_ge(uvb_made, n * IN + e + 1)
                    act.activation(uvb[:, ch, e, :], wide(FIRST_IN + n * IN + e), ACT.Silu, bias=c["uvb_bias"][:, e:e + 1])\
                       .then_inc(silu_made, 1)

            def relus(h):
                for i, n in enumerate((0, 2, 1)):
                    act.wait_ge(dots_made, 3 * h + i + 1)
                    if h and i == 0:
                        act.wait_ge(mix_made, 1)
                    act.activation(kern[:, n, :], other(OTHER.index(("dots", 4 * h + i + 1))), ACT.Relu, bias=c["rel"][:, n:n + 1],
                                   scale=1.0 / CHUNK).then_inc(relu_made, 1)
                act.wait_ge(relu_made, 3 * (h + 1))
                act.activation(kern[:, :, :], kern[:, :, :], ACT.Square).then_inc(kern_made, 1)

            def gates(n):
                for k in range(HT):
                    act.wait_ge(pair_made, n * HT + k + 1)
                    if n >= 2:
                        act.wait_ge(up_taken, (n - 2) * HT + k + 1)
                    act.activation(gate[n % 2][:, k, :], wide(FIRST_PAIR + 2 * (n * HT + k)), ACT.Silu).then_inc(gate_made, 1)

            for b in range(BATCH):
                for ch in (2 * b, 2 * b + 1):
                    keep(ch, ch, total=ysum[:, ch:ch + 1])
                act.wait_ge(shifted, 2 * b + 1)
                act.activation(router[:, b, 2, :], router[:, b, 1, :], ACT.Exp, accum_out=wv[:, b, 2:3]).then_inc(exp_made, 1)
                act.wait_ge(shifted, 2 * b + 2)
                act.activation(router[:, b, 6, 0:1], router[:, b, 5, 0:1], ACT.Exp).then_inc(exp_w, 1)
            for ch in range(CHUNKS):
                gelu(ch)
            keep(CHUNKS, 0, c["lng"][:, 0:1], c["lnb"][:, 0:1])
            keep(CHUNKS + 1, 1, c["lng"][:, 0:1], c["lnb"][:, 0:1])
            silu(0, 0)
            keep(CHUNKS + 2, 2, c["lng"][:, 0:1], c["lnb"][:, 0:1])
            silu(1, 1)
            silu(2, 2)
            keep(CHUNKS + 3, 3, c["lng"][:, 0:1], c["lnb"][:, 0:1])
            relus(0)
            silu(3, 3)
            keep(2 * CHUNKS, PAIRED[0])
            relus(1)
            keep(2 * CHUNKS + 1, PAIRED[1])
            gates(0)
            gates(1)
            keep(2 * CHUNKS + 2, PAIRED[2])
            keep(2 * CHUNKS + 3, PAIRED[3])
            gates(2)
            gates(3)

        @block.vector
        def _(dve):
            steps = [0]

            def link(ins):
                steps[0] += 1
                ins.then_inc(step, 1)
                dve.wait_ge(step, steps[0])

            def moments(k, rows, eps, outer=0.0):
                for t in range(T):
                    last = dve.bn_stats(stats[:, k, t, :], rows[:, t, :])
                link(last)
                for t in range(T):
                    last = dve.bn_aggr(mv[:, k, t, :], stats[:, k, t, :])
                link(last)
                last = dve.tensor_scalar(inv[:, k, 0, :], mv[:, k, :, 1], eps, None, ALU.add)
                if outer:
                    last = dve.tensor_scalar(inv[:, k, 1, :], mv[:, k, :, 1], 1.0 + outer, outer * eps, ALU.mult, ALU.add)
                last.then_inc(var_made, 1)

            def normalise(k, rows, ch, which=0):
                dve.wait_ge(inv_made, k + 1)
                for t in range(T):
                    last = dve.tensor_scalar(y0[:, ch, t, :], rows[:, t, :], mv[:, k, t, 0:1], inv[:, k, which, t:t + 1], ALU.subtract, ALU.mult)
                last.then_inc(rows_made, 1)

            def route(b):
                r = router[:, b, :, :]
                dve.wait_ge(logits_made, b + 1)
                link(dve.scalar_tensor_tensor(out=r[:, 0, :], in0=by_token(b)[0:1, 0:EXPERTS], scalar=1.0 / SEQ, in1=br[:, :],
                                              op0=ALU.mult, op1=ALU.add))
                link(dve.tensor_reduce(wv[:, b, 3:4], r[:, 0, :], AX_X, ALU.max))
                dve.tensor_scalar(r[:, 1, :], r[:, 0, :], wv[:, b, 3:4], None, ALU.subtract).then_inc(shifted, 1)
                dve.wait_ge(exp_made, b + 1)
                link(dve.reciprocal(wv[:, b, 2:3], wv[:, b, 2:3]))
                link(dve.tensor_scalar(r[:, 3, :], r[:, 2, :], wv[:, b, 2:3], None, ALU.mult))
                link(dve.max(r[:, 4, :], r[:, 3, :]))
                dve.max_index(chosen[:, b, :], r[:, 4, :], r[:, 3, :]).then_inc(chosen_made, 1)
                dve.tensor_tensor(r[:, 5, 0:1], r[:, 4, 1:2], r[:, 4, 0:1], ALU.subtract).then_inc(shifted, 1)
                dve.wait_ge(exp_w, b + 1)
                link(dve.tensor_scalar(r[:, 6, 1:2], r[:, 6, 0:1], 1.0, None, ALU.add))
                link(dve.reciprocal(wv[:, b, 0:1], r[:, 6, 1:2]))
                dve.tensor_tensor(wv[:, b, 1:2], wv[:, b, 0:1], r[:, 6, 0:1], ALU.mult).then_inc(wv_made, 1)

            def weigh(b):
                dve.wait_ge(wb_spread, b + 1)
                link(dve.tensor_copy(wb[:, b, :], by_token(b)[:, P:P + TOP]))
                dve.wait_ge(down_in[b], 16 * 2 * TOP)
                dve.wait_ge(wv_made, b + 1)
                for k in range(TOP):
                    dve.tensor_scalar(w2s[:, b, k, :, :], w2s[:, b, k, :, :], wb[:, b, k:k + 1], None, ALU.mult)
                link(dve.tensor_scalar(b2w[:, b, 0, :], b2s[:, b, 0, :], wv[:, b, 0:1], None, ALU.mult))
                dve.scalar_tensor_tensor(out=b2w[:, b, 1, :], in0=b2s[:, b, 1, :], scalar=wv[:, b, 1:2], in1=b2w[:, b, 0, :],
                                         op0=ALU.mult, op1=ALU.add).then_inc(w2_scaled, 1)

            def after_ffn(ch):
                k = CHUNKS + ch
                y = y0[:, ch, :, :]
                dve.wait_ge(ffn_made, ch + 1)
                dve.tensor_tensor(y, by_token(ch).rearrange("p (t d) -> p t d", d=DIM), y, ALU.add).then_inc(token_out, 1)
                dve.wait_ge(token_out, ch + 1)
                moments(k, y, LN_EPS)
                for t in range(T):
                    last = dve.scalar_tensor_tensor(out=y[:, t, :], in0=y[:, t, :], scalar=mv[:, k, t, 0:1], in1=gamma[:, :],
                                                    op0=ALU.subtract, op1=ALU.mult)
                link(last)
                dve.wait_ge(inv_made, 2 * ch + CHUNKS + 1)
                dve.wait_ge(beta_added, ch + 1)
                for t in range(T):
                    last = dve.scalar_tensor_tensor(out=xc(ch)[:, t, :], in0=y[:, t, :], scalar=inv[:, k, 0, t:t + 1], in1=xb[:, ch, t, :],
                                                    op0=ALU.mult, op1=ALU.add)
                last.then_inc(new_x, 1)
                dve.wait_ge(new_x, ch + 1)
                k = 2 * CHUNKS + ch
                moments(k, xc(ch), LN_EPS, LN_EPS)
                dve.wait_ge(inv_made, 2 * ch + CHUNKS + 2)
                for t in range(T):
                    last = dve.tensor_scalar(y[:, t, :], xc(ch)[:, t, :], mv[:, k, t, 0:1], inv[:, k, 1, t:t + 1], ALU.subtract, ALU.mult)
                last.then_inc(rows_made, 1)

            def gau_heads(h):
                dve.wait_ge(silu_made, (3 + h) * IN)
                if h:
                    dve.wait_ge(dots_made, 3)
                for l, n in ((1, 0), (0, 1), (0, 0), (1, 1)):
                    last = dve.tensor_scalar(heads[:, l, n, :], uvb[:, 2 * l + h, IN - 1, :], c["qk_cols"][:, n:n + 1],
                                             c["qk_cols"][:, 2 + n:3 + n], ALU.mult, ALU.add)
                last.then_inc(heads_made, 1)

            def gau_same(h):
                dve.wait_ge(heads_made, h + 1)
                dve.tensor_tensor(prod[:, 0, :], heads[:, 0, 0, :], heads[:, 0, 1, :], ALU.mult).then_inc(prod_made, 1)
                dve.tensor_tensor(prod[:, 2, :], heads[:, 1, 0, :], heads[:, 1, 1, :], ALU.mult).then_inc(prod_made, 1)

            def gau_cross(h):
                dve.wait_ge(turned_q, h + 1)
                dve.tensor_tensor(prod[:, 1, :], other(OTHER.index(("turned_q", 4 * h))), heads[:, 0, 1, :], ALU.mult).then_inc(prod_made, 1)
                link(dve.tensor_tensor(vu[:, 0, :, :], uvb[:, h, 2:4, :], uvb[:, h, 0:2, :], ALU.mult))

            def gau_mix(h, between=lambda k: None):
                dve.wait_ge(kern_made, h + 1)
                dve.wait_ge(vu_made, h + 1)
                if h:
                    dve.wait_ge(gau_made, 2)
                dve.tensor_tensor(mix[:, 0, :, :], vu[:, 0, :, :], over_mid(kern[:, 0, :], 2), ALU.mult)
                between(0)
                dve.tensor_tensor(vu[:, 1, :, :], vu[:, 1, :, :], over_mid(kern[:, 1, :], 2), ALU.mult)
                between(1)
                link(dve.tensor_tensor(vu[:, 2, :, :], vu[:, 2, :, :], over_mid(kern[:, 2, :], 2), ALU.mult))
                dve.tensor_tensor(mix[:, 1, :, :], vu[:, 1, :, :], vu[:, 2, :, :], ALU.add).then_inc(mix_made, 1)
                between(2)

            def add_gau(n):
                ch = PAIRED[n]
                dve.wait_ge(gau_made, n + 1)
                dve.wait_ge(short_made, ch + 1)
                dve.tensor_tensor(xc(ch), by_token(n).rearrange("p (t d) -> p t d", d=DIM), xb[:, ch, :, :], ALU.add).then_inc(token_out, 1)
                dve.wait_ge(token_out, CHUNKS + n + 1)
                moments(3 * CHUNKS + n, xc(ch), LN_EPS)

            def last_rows(n):
                normalise(3 * CHUNKS + n, xc(PAIRED[n]), PAIRED[n])

            def gate_times_up(n, k):
                dve.wait_ge(gate_made, n * HT + k + 1)
                if k == 0 and n >= 2:
                    dve.wait_ge(down_made, n - 1)
                dve.tensor_tensor(hid1[n % 2][:, k, :], wide(FIRST_PAIR + 2 * (n * HT + k) + 1), gate[n % 2][:, k, :], ALU.mult)\
                   .then_inc(up_taken, 1)

            def after_gates(n):
                for k in range(HT):
                    gate_times_up(n, k)

            def final(n):
                dve.wait_ge(down_made, n + 1)
                dve.tensor_tensor(xc(PAIRED[n]), by_token(n).rearrange("p (t d) -> p t d", d=DIM), xc(PAIRED[n]), ALU.add)\
                   .then_inc(x_final, 1)

            for ch in (0, 1):
                moments(ch, xc(ch), LN_EPS)
            for ch in (0, 1):
                normalise(ch, xc(ch), ch)
            route(0)
            for ch in (2, 3):
                moments(ch, xc(ch), LN_EPS)
            for ch in (2, 3):
                normalise(ch, xc(ch), ch)
            route(1)
            weigh(0)
            weigh(1)
            for ch in range(CHUNKS):
                dve.wait_ge(b2_spread, ch // 2 + 1)
                dve.wait_ge(rows_turned, ch + 1)
                y = y0[:, ch, :, :]
                dve.tensor_tensor(y, y, over_mid(by_token(ch // 2)[:, 2 * P:3 * P], T), ALU.add).then_inc(b2_added, 1)
            dve.wait_ge(b2_added, CHUNKS)
            for ch in range(CHUNKS):
                after_ffn(ch)
            gau_heads(0)
            gau_same(0)
            gau_cross(0)
            gau_mix(0)
            gau_heads(1)
            add_gau(0)
            gau_same(1)
            last_rows(0)
            add_gau(1)
            gau_cross(1)
            last_rows(1)
            gau_mix(1, between=lambda k: gate_times_up(0, k))
            add_gau(2)
            gate_times_up(1, 0)
            last_rows(2)
            add_gau(3)
            gate_times_up(1, 1)
            last_rows(3)
            gate_times_up(1, 2)
            after_gates(2)
            final(0)
            final(1)
            after_gates(3)
            final(2)
            final(3)


_OUTS = [((BATCH, SEQ, DIM), "float32")]


def turn_of_position_1():
    half = S // 2
    angle = np.float32(10000.0) ** (-np.arange(half, dtype=np.float32) / np.float32(half))
    cos, sin = np.cos(angle), np.sin(angle)
    turn = np.zeros((S, S), np.float32)
    at = np.arange(half)
    turn[at, at] = turn[at + half, at + half] = cos
    turn[at, at + half] = -sin
    turn[at + half, at] = sin
    return np.ascontiguousarray(turn.T)


def kernel(**inputs):
    import concourse.bacc as _bacc
    from concourse.bass_utils import run_bass_kernel_spmd as _run

    nc = _bacc.Bacc("TRN2", target_bir_lowering=False, num_devices=1)
    arrays, args = {}, {}
    for name, value in inputs.items():
        v = np.ascontiguousarray(value)
        arrays[f"in_{name}"] = v
        args[name] = nc.dram_tensor(f"in_{name}", v.shape, mybir.dt.from_np(v.dtype), kind="ExternalInput").ap()
    arrays["turn"] = turn_of_position_1()
    turn = nc.dram_tensor("turn", (S, S), F32, kind="ExternalInput").ap()
    shape, dtype = _OUTS[0]
    out = nc.dram_tensor("out_0", shape, mybir.dt.from_np(np.dtype(dtype)), kind="ExternalOutput").ap()
    build(nc, args, turn, out)
    r = _run(nc, [arrays], core_ids=[0])
    return r.results[0]["out_0"]
```
